# Optimizing a Trainium2 kernel written in Bass

```python
import numpy as np
import jax
import jax.numpy as jnp

def _softmax(x, axis=-1):
    return jax.nn.softmax(x, axis=axis)

def _gelu(x):
    return jax.nn.gelu(x, approximate=True)

def _silu(x):
    return jax.nn.silu(x)

def _sigmoid(x):
    return jax.nn.sigmoid(x)

def _layernorm(x, axis=-1, eps=1e-05):
    m = jnp.mean(x, axis=axis, keepdims=True)
    v = jnp.var(x, axis=axis, keepdims=True)
    return (x - m) / jnp.sqrt(v + eps)

def _scatter_add(tgt, idx, src, axis=0):
    return tgt.at[idx].add(src)

def _segment_sum(src, seg, n):
    return jax.ops.segment_sum(src, seg, n)
kernel_name = 'mk_gnn_preln_d4_gnn_r8_f0e1db'

def setup_inputs(seed: int=0):
    np.random.seed(seed)
    _w = jnp.asarray

    def _rec_inputs():
        import jax
        import jax.numpy as jnp
        _gk = jax.random.key(seed)
        x = -0.0003713 + 1 * jax.random.normal(jax.random.fold_in(_gk, 1), (6250, 256), jnp.float32)
        src = jax.random.randint(jax.random.fold_in(_gk, 2), (100000,), 0, 6250, jnp.int32)
        dst = jnp.minimum((6250 * jax.random.uniform(jax.random.fold_in(_gk, 3), (100000,)) ** 2.0).astype(jnp.int32), 49999)
        _o = jnp.argsort(dst, stable=True)
        src = src[_o]
        dst = dst[_o]
        edge_attr_64 = 0.000189758 + 1.00013 * jax.random.normal(jax.random.fold_in(_gk, 12), (100000, 64), jnp.float32)
        edge_type_8 = jax.random.randint(jax.random.fold_in(_gk, 14), (100000,), 0, 8, jnp.int32)
        edge_weight = jax.random.uniform(jax.random.fold_in(_gk, 15), (100000,), jnp.float32, 0.0, 0.999998)
        return (x, src, dst, edge_attr_64, edge_type_8, edge_weight)
    x, src, dst, edge_attr_64, edge_type_8, edge_weight = _rec_inputs()

    def _L0_gnn_setup():
        import jax, jax.numpy as jnp
        import numpy as np
        N_NODES = 6250
        N_EDGES = 37500
        N_REL = 8
        D = 256
        N_LAYERS = 3

        def _rgcn_layer(x, W, root, bias, src, dst, seg):
            agg = jax.ops.segment_sum(x[src], seg, num_segments=N_REL * N_NODES)
            agg = agg.reshape(N_REL, N_NODES, -1)
            return jnp.einsum('rnd,rde->ne', agg, W) + x @ root + bias
        key = jax.random.key(seed)
        k1, k2, k3, k4, k5 = jax.random.split(key, 5)
        x = jax.random.normal(k1, (N_NODES, D), dtype=jnp.float32)
        scale = 1.0 / np.sqrt(D)
        weights = jax.random.normal(k2, (N_LAYERS, N_REL, D, D), dtype=jnp.float32) * scale
        roots = jax.random.normal(k3, (N_LAYERS, D, D), dtype=jnp.float32) * scale
        biases = jnp.zeros((N_LAYERS, D), dtype=jnp.float32)
        edge_index = jax.random.randint(k4, (2, N_EDGES), 0, N_NODES, dtype=jnp.int64)
        edge_type = jax.random.randint(k5, (N_EDGES,), 0, N_REL, dtype=jnp.int64)
        return {'x': x, 'weights': weights, 'roots': roots, 'biases': biases, 'edge_index': edge_index, 'edge_type': edge_type}
    _L0_gnn_all = _L0_gnn_setup()
    _L0_gnn_in = {k: v for k, v in _L0_gnn_all.items() if k in ('weights', 'roots', 'biases')}
    del _L0_gnn_all

    def _L1_gnn_setup():
        import jax, jax.numpy as jnp
        import numpy as np
        EPS = 1e-05

        def _ln(x, g, b):
            m = jnp.mean(x, axis=-1, keepdims=True)
            v = jnp.var(x, axis=-1, keepdims=True)
            return (x - m) * jax.lax.rsqrt(v + EPS) * g + b
        N, E, D, L = (6250, 100000, 256, 4)
        key = jax.random.key(seed)
        ks = jax.random.split(key, 10)
        node = jax.random.normal(ks[0], (N, D), jnp.float32)
        edge_index = jax.random.randint(ks[1], (2, E), 0, N, dtype=jnp.int32)
        edge_attr = jax.random.uniform(ks[2], (E,), jnp.float32)
        batch_ptr = jnp.array([0, N], dtype=jnp.int32)
        s = 1.0 / np.sqrt(D)
        W_rel = jax.random.uniform(ks[3], (L, D, D), jnp.float32, -s, s)
        b_rel = jnp.zeros((L, D), jnp.float32)
        W_root = jax.random.uniform(ks[4], (L, D, D), jnp.float32, -s, s)
        ln_g = jnp.ones((L, D), jnp.float32)
        ln_b = jnp.zeros((L, D), jnp.float32)
        W1 = jax.random.uniform(ks[5], (D, D), jnp.float32, -s, s)
        b1 = jnp.zeros((D,), jnp.float32)
        mg1 = jnp.ones((D,), jnp.float32)
        mb1 = jnp.zeros((D,), jnp.float32)
        W2 = jax.random.uniform(ks[6], (D, D), jnp.float32, -s, s)
        b2 = jnp.zeros((D,), jnp.float32)
        mg2 = jnp.ones((D,), jnp.float32)
        mb2 = jnp.zeros((D,), jnp.float32)
        return dict(node=node, edge_index=edge_index, edge_attr=edge_attr, batch_ptr=batch_ptr, W_rel=W_rel, b_rel=b_rel, W_root=W_root, ln_g=ln_g, ln_b=ln_b, W1=W1, b1=b1, mg1=mg1, mb1=mb1, W2=W2, b2=b2, mg2=mg2, mb2=mb2)
    _L1_gnn_all = _L1_gnn_setup()
    _L1_gnn_in = {k: v for k, v in _L1_gnn_all.items() if k in ('batch_ptr', 'W_rel', 'b_rel', 'W_root', 'ln_g', 'ln_b', 'W1', 'b1', 'mg1', 'mb1', 'W2', 'b2', 'mg2', 'mb2')}
    del _L1_gnn_all

    def _L2_gnn_setup():
        import jax, jax.numpy as jnp
        import numpy as np
        N_NODES = 6250
        N_EDGES = 100000
        NODE_IN = 256
        EDGE_OUT = 64
        GLOBAL_IN = 128
        NODE_OUT = 256
        HIDDEN = 512
        N_GRAPHS = 64
        key = jax.random.key(seed)
        ks = jax.random.split(key, 8)
        x = jax.random.normal(ks[0], (N_NODES, NODE_IN), dtype=jnp.float32)
        edge_index = jax.random.randint(ks[1], (2, N_EDGES), 0, N_NODES, dtype=jnp.int64)
        edge_attr = jax.random.normal(ks[2], (N_EDGES, EDGE_OUT), dtype=jnp.float32)
        u = jax.random.normal(ks[3], (N_GRAPHS, GLOBAL_IN), dtype=jnp.float32)
        batch = jnp.sort(jax.random.randint(ks[4], (N_NODES,), 0, N_GRAPHS, dtype=jnp.int64))
        in_dim = NODE_IN + EDGE_OUT + GLOBAL_IN
        b1s = 1.0 / np.sqrt(in_dim)
        b2s = 1.0 / np.sqrt(HIDDEN)
        W1 = jax.random.uniform(ks[5], (in_dim, HIDDEN), dtype=jnp.float32, minval=-b1s, maxval=b1s)
        b1 = jnp.zeros((HIDDEN,), dtype=jnp.float32)
        W2 = jax.random.uniform(ks[6], (HIDDEN, NODE_OUT), dtype=jnp.float32, minval=-b2s, maxval=b2s)
        b2 = jnp.zeros((NODE_OUT,), dtype=jnp.float32)
        return {'x': x, 'edge_index': edge_index, 'edge_attr': edge_attr, 'u': u, 'batch': batch, 'W1': W1, 'b1': b1, 'W2': W2, 'b2': b2}
    _L2_gnn_all = _L2_gnn_setup()
    _L2_gnn_in = {k: v for k, v in _L2_gnn_all.items() if k in ('u', 'W1', 'b1', 'W2', 'b2')}
    del _L2_gnn_all

    def _L3_gnn_setup():
        import jax, jax.numpy as jnp
        import numpy as np
        N = 6250
        E = 100000
        F_DIM = 256
        H = 4
        C = 64
        SLOPE = 0.2

        def gat_layer(x, src, dst, W, a_src, a_dst, bias, heads, out_ch):
            n = x.shape[0]
            xW = (x @ W).reshape(n, heads, out_ch)
            alpha_s = jnp.sum(xW * a_src, axis=-1)
            alpha_d = jnp.sum(xW * a_dst, axis=-1)
            e = jax.nn.leaky_relu(alpha_s[src] + alpha_d[dst], SLOPE)
            m = jax.ops.segment_max(e, dst, num_segments=n)
            w = jnp.exp(e - m[dst])
            z = jax.ops.segment_sum(w, dst, num_segments=n)
            alpha = w / z[dst]
            out = jax.ops.segment_sum(xW[src] * alpha[:, :, None], dst, num_segments=n)
            return out.reshape(n, heads * out_ch) + bias
        key = jax.random.key(seed)
        ks = jax.random.split(key, 11)
        s = 0.05
        return {'x': jax.random.normal(ks[0], (N, F_DIM), jnp.float32), 'edge_index': jax.random.randint(ks[1], (2, E), 0, N), 'W1': jax.random.normal(ks[2], (F_DIM, H * C), jnp.float32) * s, 'a_src1': jax.random.normal(ks[3], (H, C), jnp.float32) * s, 'a_dst1': jax.random.normal(ks[4], (H, C), jnp.float32) * s, 'b1': jnp.zeros((H * C,), jnp.float32), 'W2': jax.random.normal(ks[5], (H * C, F_DIM), jnp.float32) * s, 'a_src2': jax.random.normal(ks[6], (1, F_DIM), jnp.float32) * s, 'a_dst2': jax.random.normal(ks[7], (1, F_DIM), jnp.float32) * s, 'b2': jnp.zeros((F_DIM,), jnp.float32)}
    _L3_gnn_all = _L3_gnn_setup()
    _L3_gnn_in = {k: v for k, v in _L3_gnn_all.items() if k in ('W1', 'a_src1', 'a_dst1', 'b1', 'W2', 'a_src2', 'a_dst2', 'b2')}
    del _L3_gnn_all
    return {'x': x, 'src': src, 'dst': dst, 'edge_attr_64': edge_attr_64, 'edge_type_8': edge_type_8, 'edge_weight': edge_weight, 'L0_gnn_weights': _L0_gnn_in['weights'], 'L0_gnn_roots': _L0_gnn_in['roots'], 'L0_gnn_biases': _L0_gnn_in['biases'], 'L1_gnn_batch_ptr': _L1_gnn_in['batch_ptr'], 'L1_gnn_W_rel': _L1_gnn_in['W_rel'], 'L1_gnn_b_rel': _L1_gnn_in['b_rel'], 'L1_gnn_W_root': _L1_gnn_in['W_root'], 'L1_gnn_ln_g': _L1_gnn_in['ln_g'], 'L1_gnn_ln_b': _L1_gnn_in['ln_b'], 'L1_gnn_W1': _L1_gnn_in['W1'], 'L1_gnn_b1': _L1_gnn_in['b1'], 'L1_gnn_mg1': _L1_gnn_in['mg1'], 'L1_gnn_mb1': _L1_gnn_in['mb1'], 'L1_gnn_W2': _L1_gnn_in['W2'], 'L1_gnn_b2': _L1_gnn_in['b2'], 'L1_gnn_mg2': _L1_gnn_in['mg2'], 'L1_gnn_mb2': _L1_gnn_in['mb2'], 'L2_gnn_u': _L2_gnn_in['u'], 'L2_gnn_W1': _L2_gnn_in['W1'], 'L2_gnn_b1': _L2_gnn_in['b1'], 'L2_gnn_W2': _L2_gnn_in['W2'], 'L2_gnn_b2': _L2_gnn_in['b2'], 'L3_gnn_W1': _L3_gnn_in['W1'], 'L3_gnn_a_src1': _L3_gnn_in['a_src1'], 'L3_gnn_a_dst1': _L3_gnn_in['a_dst1'], 'L3_gnn_b1': _L3_gnn_in['b1'], 'L3_gnn_W2': _L3_gnn_in['W2'], 'L3_gnn_a_src2': _L3_gnn_in['a_src2'], 'L3_gnn_a_dst2': _L3_gnn_in['a_dst2'], 'L3_gnn_b2': _L3_gnn_in['b2']}

def reference(x, src, dst, edge_attr_64, edge_type_8, edge_weight, L0_gnn_weights, L0_gnn_roots, L0_gnn_biases, L1_gnn_batch_ptr, L1_gnn_W_rel, L1_gnn_b_rel, L1_gnn_W_root, L1_gnn_ln_g, L1_gnn_ln_b, L1_gnn_W1, L1_gnn_b1, L1_gnn_mg1, L1_gnn_mb1, L1_gnn_W2, L1_gnn_b2, L1_gnn_mg2, L1_gnn_mb2, L2_gnn_u, L2_gnn_W1, L2_gnn_b1, L2_gnn_W2, L2_gnn_b2, L3_gnn_W1, L3_gnn_a_src1, L3_gnn_a_dst1, L3_gnn_b1, L3_gnn_W2, L3_gnn_a_src2, L3_gnn_a_dst2, L3_gnn_b2):
    import jax
    import jax.numpy as jnp

    def _L0_gnn_ref(x, weights, roots, biases, edge_index, edge_type):
        import jax, jax.numpy as jnp
        import numpy as np
        N_NODES = 6250
        N_EDGES = 37500
        N_REL = 8
        D = 256
        N_LAYERS = 3

        def _rgcn_layer(x, W, root, bias, src, dst, seg):
            agg = jax.ops.segment_sum(x[src], seg, num_segments=N_REL * N_NODES)
            agg = agg.reshape(N_REL, N_NODES, -1)
            return jnp.einsum('rnd,rde->ne', agg, W) + x @ root + bias
        src, dst = (edge_index[0], edge_index[1])
        seg = edge_type * N_NODES + dst
        h = x
        for l in range(N_LAYERS - 1):
            h = jax.nn.relu(_rgcn_layer(h, weights[l], roots[l], biases[l], src, dst, seg))
        h = jax.nn.sigmoid(_rgcn_layer(h, weights[-1], roots[-1], biases[-1], src, dst, seg))
        return h

    def _L1_gnn_ref(node, edge_index, edge_attr, batch_ptr, W_rel, b_rel, W_root, ln_g, ln_b, W1, b1, mg1, mb1, W2, b2, mg2, mb2):
        import jax, jax.numpy as jnp
        import numpy as np
        EPS = 1e-05

        def _ln(x, g, b):
            m = jnp.mean(x, axis=-1, keepdims=True)
            v = jnp.var(x, axis=-1, keepdims=True)
            return (x - m) * jax.lax.rsqrt(v + EPS) * g + b
        N = node.shape[0]
        L = W_rel.shape[0]
        src, dst = (edge_index[0], edge_index[1])
        msg = node[src] * edge_attr[:, None]
        deg = jnp.clip(jax.ops.segment_sum(jnp.ones_like(edge_attr), dst, num_segments=N), 1.0)
        agg = jax.ops.segment_sum(msg, dst, num_segments=N) / deg[:, None]

        def conv_layer(i):
            h = agg @ W_rel[i].T + b_rel[i] + node @ W_root[i].T
            return jax.nn.relu(_ln(node + h, ln_g[i], ln_b[i]))
        out = conv_layer(0)
        for i in range(1, L):
            out = out + conv_layer(i)
        h = jax.nn.relu(_ln(out @ W1.T + b1, mg1, mb1))
        h = jax.nn.relu(_ln(h @ W2.T + b2, mg2, mb2))
        return h

    def _L2_gnn_ref(x, edge_index, edge_attr, u, batch, W1, b1, W2, b2):
        import jax, jax.numpy as jnp
        import numpy as np
        N_NODES = 6250
        N_EDGES = 100000
        NODE_IN = 256
        EDGE_OUT = 64
        GLOBAL_IN = 128
        NODE_OUT = 256
        HIDDEN = 512
        N_GRAPHS = 64
        n = x.shape[0]
        src = edge_index[0]
        sums = jax.ops.segment_sum(edge_attr, src, num_segments=n)
        counts = jax.ops.segment_sum(jnp.ones((edge_attr.shape[0],), edge_attr.dtype), src, num_segments=n)
        edge_attr_agg = sums / jnp.maximum(counts, 1.0)[:, None]
        u_expanded = u[batch]
        combined = jnp.concatenate([x, edge_attr_agg, u_expanded], axis=1)
        h = jax.nn.relu(combined @ W1 + b1)
        return h @ W2 + b2

    def _L3_gnn_ref(x, edge_index, W1, a_src1, a_dst1, b1, W2, a_src2, a_dst2, b2):
        import jax, jax.numpy as jnp
        import numpy as np
        N = 6250
        E = 100000
        F_DIM = 256
        H = 4
        C = 64
        SLOPE = 0.2

        def gat_layer(x, src, dst, W, a_src, a_dst, bias, heads, out_ch):
            n = x.shape[0]
            xW = (x @ W).reshape(n, heads, out_ch)
            alpha_s = jnp.sum(xW * a_src, axis=-1)
            alpha_d = jnp.sum(xW * a_dst, axis=-1)
            e = jax.nn.leaky_relu(alpha_s[src] + alpha_d[dst], SLOPE)
            m = jax.ops.segment_max(e, dst, num_segments=n)
            w = jnp.exp(e - m[dst])
            z = jax.ops.segment_sum(w, dst, num_segments=n)
            alpha = w / z[dst]
            out = jax.ops.segment_sum(xW[src] * alpha[:, :, None], dst, num_segments=n)
            return out.reshape(n, heads * out_ch) + bias
        loop = jnp.arange(N)
        src = jnp.concatenate([edge_index[0], loop])
        dst = jnp.concatenate([edge_index[1], loop])
        h = jax.nn.elu(gat_layer(x, src, dst, W1, a_src1, a_dst1, b1, H, C))
        return gat_layer(h, src, dst, W2, a_src2, a_dst2, b2, 1, F_DIM)
    edge_index = jnp.stack([src, dst])
    batch0 = jnp.zeros((6250,), jnp.int32)
    h = jnp.maximum(_layernorm(x, axis=-1), 0.0)
    x = x + _L0_gnn_ref(h, L0_gnn_weights, L0_gnn_roots, L0_gnn_biases, edge_index, edge_type_8)
    h = jnp.maximum(_layernorm(x, axis=-1), 0.0)
    x = x + _L1_gnn_ref(h, edge_index, edge_weight, L1_gnn_batch_ptr, L1_gnn_W_rel, L1_gnn_b_rel, L1_gnn_W_root, L1_gnn_ln_g, L1_gnn_ln_b, L1_gnn_W1, L1_gnn_b1, L1_gnn_mg1, L1_gnn_mb1, L1_gnn_W2, L1_gnn_b2, L1_gnn_mg2, L1_gnn_mb2)
    h = jnp.maximum(_layernorm(x, axis=-1), 0.0)
    x = x + _L2_gnn_ref(h, edge_index, edge_attr_64, L2_gnn_u, batch0, L2_gnn_W1, L2_gnn_b1, L2_gnn_W2, L2_gnn_b2)
    h = jnp.maximum(_layernorm(x, axis=-1), 0.0)
    x = x + _L3_gnn_ref(h, edge_index, L3_gnn_W1, L3_gnn_a_src1, L3_gnn_a_dst1, L3_gnn_b1, L3_gnn_W2, L3_gnn_a_src2, L3_gnn_a_dst2, L3_gnn_b2)
    return x

_drawn_inputs = setup_inputs


def setup_inputs(seed=0):
    import zlib

    import numpy as np

    out = dict(_drawn_inputs(seed))
    spreads = {'L0_gnn_biases': (0.0, 0.1),
     'L1_gnn_b_rel': (0.0, 0.278),
     'L1_gnn_ln_g': (1.0, 0.2),
     'L1_gnn_ln_b': (0.0, 0.426),
     'L1_gnn_b1': (0.0, 0.31),
     'L1_gnn_mg1': (1.0, 0.2),
     'L1_gnn_mb1': (0.0, 0.1),
     'L1_gnn_b2': (0.0, 0.1),
     'L1_gnn_mg2': (1.0, 0.2),
     'L1_gnn_mb2': (0.0, 0.1),
     'L2_gnn_b1': (0.0, 0.326),
     'L2_gnn_b2': (0.0, 0.1),
     'L3_gnn_b1': (0.0, 0.1),
     'L3_gnn_b2': (0.0, 0.1)}
    factors = {'edge_attr_64': 3.896,
     'edge_weight': 5.214,
     'L3_gnn_a_src1': 8.0,
     'L3_gnn_a_dst1': 152.994,
     'L3_gnn_a_src2': 24.762,
     'L3_gnn_a_dst2': 200.0}
    for name, (base, spread) in spreads.items():
        noise = np.random.default_rng([zlib.crc32(name.encode()), seed]).standard_normal(out[name].shape)
        drawn = base * np.exp(spread * noise) if base else spread * noise
        out[name] = jnp.asarray(drawn.astype(out[name].dtype))
    for name, factor in factors.items():
        out[name] = (out[name] * factor).astype(out[name].dtype)
    return out
```

```python
from contextlib import ExitStack

import numpy as np
import concourse.bass as bass
from concourse import mybir

ALU = mybir.AluOpType
ACT = mybir.ActivationFunctionType
AX = mybir.AxisListType
F32 = mybir.dt.float32
I32 = mybir.dt.int32

P = 128
N_NODES = 6250
N_EDGES = 100000
D = 256
REL = 8
EDGE_D = 64
HEADS = 4
EPS = 1e-5
SLOPE = 0.2

BUCKETS = 50
NPAD = BUCKETS * P
GROUP = 4
GROUPS = 4
RING = GROUP * GROUPS
COLS = -(-(-(-N_EDGES // P)) // RING) * RING
EPAD = COLS * P
REAL = -(-N_NODES // P)
NT = -(-((N_EDGES - REAL) // P + REAL + (EPAD - N_EDGES) // P) // RING) * RING
SLOTS = NT * P
ACCW = 260
ECOLS = EDGE_D + 1
NO_NODE = 255.0


def cols(t, width, lo=0, n=None):
    return bass.ds(t * width + lo, width if n is None else n)


def rounds(engine, n, body):
    body(0)
    with engine.Fori(1, n) as i:
        body(i)


def is_first(i):
    return isinstance(i, int) and i == 0


class Phase:

    def __init__(self, nc, name):
        self.nc, self.name, self.ctx, self.sems = nc, name, ExitStack(), []

    def __enter__(self):
        self.turn = self.sem("turn")
        return self

    def __exit__(self, kind, *rest):
        self.ctx.close()
        if kind is None and self.sems:
            self.nc.clear_and_free_semaphores(self.sems)
            self.nc.all_engine_barrier()

    def sb(self, name, shape, dt=F32):
        return self.ctx.enter_context(self.nc.sbuf_tensor(f"{self.name}_{name}", shape, dt))

    def psum(self, name, shape):
        return self.ctx.enter_context(self.nc.psum_tensor(f"{self.name}_{name}", shape, F32))

    def sem(self, name):
        self.sems.append(self.nc.alloc_semaphore(f"{self.name}_{name}"))
        return self.sems[-1]

    def block(self):
        return self.ctx.enter_context(self.nc.Block())


class Mem:

    def __init__(self, nc, ctx):
        def sb(name, shape, dt=F32):
            return ctx.enter_context(nc.sbuf_tensor(name, shape, dt))

        self.x = sb("x_nodes", [P, BUCKETS * D])
        self.acc = sb("acc", [P, BUCKETS * ACCW])
        self.edge_acc = sb("edge_acc", [P, BUCKETS * ECOLS])
        self.slot_rel = sb("slot_rel", [P, NT], I32)
        self.slot_src = sb("slot_src", [P, NT], I32)
        self.slot_weight = sb("slot_weight", [P, NT])
        self.slot_node = sb("slot_node", [P, NT + 2 * GROUP])
        self.tile_of_dst = sb("tile_of_dst", [1, NT], I32)
        self.tile_of_src = sb("tile_of_src", [1, NT], I32)
        self.iota = sb("iota_row", [P, P])
        self.ident = sb("ident", [P, P])
        self.ones = sb("ones", [P, P])
        self.mean_var = sb("mean_var", [P, BUCKETS * 2])
        self.rstd = sb("rstd", [P, BUCKETS])
        self.shift = sb("shift", [P, BUCKETS])
        self.inv_deg = sb("inv_deg", [P, BUCKETS])
        self.eps = sb("eps", [P, 1])


def sort_by_tile(nc, mem, name, key_dram, addr, loc, tile_of):
    with Phase(nc, name) as ph:
        sb, sem = ph.sb, ph.sem
        key, bucket_i = sb("key", [P, COLS], I32), sb("bucket_i", [P, COLS], I32)
        bucket, running, place = sb("bucket", [P, COLS]), sb("running", [P, COLS]), sb("place", [P, COLS])
        mask = sb("mask", [P, COLS], I32)
        count, tiles, ends, seed, zero = (sb(n, [P, BUCKETS]) for n in ("count", "tiles", "ends", "seed", "zero"))
        total_i, number, before = sb("total_i", [P, BUCKETS], I32), sb("number", [P, BUCKETS]), sb("before", [P, P])
        end_col, junk = sb("end_col", [P, 1]), sb("junk", [P, BUCKETS])
        tile_no, past = sb("tile_no", [REAL, NT]), sb("past", [REAL, NT])
        offset_ps = ph.psum("offset_ps", [P, BUCKETS])
        total_ps = ph.psum("total_ps", [P, BUCKETS])
        tile_ps = [ph.psum(f"tile_ps{h}", [1, NT // 2]) for h in range(2)]
        loaded, consts, chain, counted, offsets, past_ready, tiles_ready = (
            sem(n) for n in ("loaded", "consts", "chain", "counted", "offsets", "past_ready", "tiles_ready"))
        block = ph.block()

        @block.sync
        def _(sp):
            sp.dma_start(key[:, :], key_dram).then_inc(loaded, 16)

        @block.gpsimd
        def _(pool):
            pool.iota(number[:, :], [[1, BUCKETS]], base=0, channel_multiplier=0,
                      allow_small_or_imprecise_dtypes=True).then_inc(consts, 1)
            pool.iota(tile_no[:, :], [[1, NT]], base=0, channel_multiplier=0,
                      allow_small_or_imprecise_dtypes=True).then_inc(consts, 1)
            pool.memset(zero[:, :], 0.0).then_inc(consts, 1)
            pool.memset(before[:, :], 1.0).then_inc(consts, 1)
            pool.wait_ge(consts, 4)
            pool.affine_select(out=before[:, :], in_=before[:, :], compare_op=ALU.is_gt, fill=0.0,
                               base=0, pattern=[[1, P]], channel_multiplier=-1).then_inc(consts, 1)

        @block.tensor
        def _(pe):
            pe.wait_ge(consts, 5)
            pe.wait_ge(counted, BUCKETS)
            pe.matmul(offset_ps[:, :], before[:, :], count[:, :], start=True, stop=True).then_inc(offsets, 1)
            pe.matmul(total_ps[:, :], mem.ones[:, :], count[:, :], start=True, stop=True).then_inc(offsets, 1)
            pe.wait_ge(past_ready, 1)
            for h in range(2):
                pe.matmul(tile_ps[h][:, :], mem.ones[0:REAL, 0:1], past[:, cols(h, NT // 2)],
                          start=True, stop=True).then_inc(tiles_ready, 1)

        @block.vector
        def _(dve):
            steps = [0]

            def link(ins):
                steps[0] += 1
                ins.then_inc(chain, 1)
                dve.wait_ge(chain, steps[0])

            dve.wait_ge(loaded, 16)
            dve.wait_ge(consts, 5)
            link(dve.tensor_scalar(bucket_i[:, :], key[:, :], 7, None, ALU.logical_shift_right))
            link(dve.tensor_copy(bucket[:, :], bucket_i[:, :]))
            link(dve.tensor_scalar(mask[:, :], key[:, :], P - 1, None, ALU.bitwise_and))
            link(dve.tensor_copy(loc, mask[:, :]))
            with dve.Fori(0, BUCKETS) as b:
                dve.tensor_scalar(running[:, :], bucket[:, :], number[:, bass.ds(b, 1)], None, ALU.is_equal, ALU.add,
                                  accum_out=count[:, bass.ds(b, 1)]).then_inc(counted, 1)
                dve.wait_ge(counted, b + 1)
            dve.wait_ge(offsets, 2)
            link(dve.tensor_scalar(total_i[:, :], total_ps[:, :], float(P - 1), None, ALU.add))
            link(dve.tensor_scalar(total_i[:, :], total_i[:, :], 7, None, ALU.logical_shift_right))
            link(dve.tensor_copy(tiles[:, :], total_i[:, :]))
            link(dve.tensor_tensor_scan(ends[:, :], tiles[:, :], zero[:, :], 0.0, ALU.add, ALU.add))
            link(dve.tensor_tensor(seed[:, :], ends[:, :], tiles[:, :], ALU.subtract))
            link(dve.tensor_scalar(seed[:, :], seed[:, :], float(P), -1.0, ALU.mult, ALU.add))
            link(dve.tensor_tensor(seed[:, :], seed[:, :], offset_ps[:, :], ALU.add))
            link(dve.tensor_tensor_reduce(junk[:, :], ends[:, :], mem.ident[:, 0:BUCKETS], 1.0, 0.0,
                                          ALU.mult, ALU.add, end_col[:, :]))
            dve.tensor_scalar(past[:, :], tile_no[:, :], end_col[0:REAL, :], None, ALU.is_ge).then_inc(past_ready, 1)
            for h in range(2):
                dve.wait_ge(tiles_ready, h + 1)
                link(dve.tensor_copy(tile_of[:, cols(h, NT // 2)], tile_ps[h][:, :]))
            link(dve.memset(place[:, :], 0.0))
            at = steps[0]
            with dve.Fori(0, BUCKETS) as b:
                dve.tensor_scalar(mask[:, :], bucket[:, :], number[:, bass.ds(b, 1)], None,
                                  ALU.is_equal).then_inc(chain, 1)
                dve.wait_ge(chain, b * 4 + at + 1)
                dve.tensor_tensor_scan(running[:, :], mask[:, :], bucket[:, :], seed[:, bass.ds(b, 1)],
                                       ALU.add, ALU.bypass).then_inc(chain, 1)
                dve.wait_ge(chain, b * 4 + at + 2)
                dve.tensor_tensor(running[:, :], running[:, :], mask[:, :], ALU.mult).then_inc(chain, 1)
                dve.wait_ge(chain, b * 4 + at + 3)
                dve.tensor_tensor(place[:, :], place[:, :], running[:, :], ALU.add).then_inc(chain, 1)
                dve.wait_ge(chain, b * 4 + at + 4)
            steps[0] += 4 * BUCKETS
            link(dve.tensor_copy(bucket_i[:, :], place[:, :]))
            link(dve.tensor_scalar(mask[:, :], bucket_i[:, :], P - 1, None, ALU.bitwise_and))
            link(dve.tensor_scalar(bucket_i[:, :], bucket_i[:, :], 7, None, ALU.logical_shift_right))
            link(dve.scalar_tensor_tensor(addr, mask[:, :], float(NT), bucket_i[:, :], ALU.mult, ALU.add))


def constants(nc, mem):
    with Phase(nc, "consts") as ph:
        made = ph.sem("made")
        block = ph.block()

        @block.gpsimd
        def _(pool):
            pool.iota(mem.iota[:, :], [[1, P]], base=0, channel_multiplier=0,
                      allow_small_or_imprecise_dtypes=True).then_inc(made, 1)
            pool.memset(mem.ident[:, :], 0.0).then_inc(made, 1)
            pool.memset(mem.eps[:, :], EPS).then_inc(made, 1)
            pool.wait_ge(made, 3)
            pool.affine_select(out=mem.ident[:, :], in_=mem.ident[:, :], compare_op=ALU.not_equal, fill=1.0,
                               base=0, pattern=[[-1, P]], channel_multiplier=1).then_inc(made, 1)

        @block.vector
        def _(dve):
            dve.memset(mem.ones[:, :], 1.0)
            dve.memset(mem.acc[:, :], 0.0)
            dve.memset(mem.edge_acc[:, :], 0.0)
            dve.memset(mem.slot_node[:, NT:NT + 2 * GROUP], NO_NODE)


def scatter(nc, name, addr, table, pieces, labels=None):
    width = table.shape[1]
    with Phase(nc, name) as ph:
        sem = ph.sem
        rows = ph.sb("rows", [P, RING, width], table.dtype)
        where = ph.sb("where", [P, RING], I32)
        staged = [sem(f"staged{g}") for g in range(GROUPS)]
        written = [sem(f"written{g}") for g in range(GROUPS)]
        labelled = sem("labelled")
        n_staged = 1 + len(pieces(None, 0, GROUP, rows, 0))
        block = ph.block()

        @block.sync
        def _(sp):
            def stage(i):
                for g in range(GROUPS):
                    if not is_first(i):
                        sp.wait_ge(written[g], i * (16 * GROUP))
                        sp.sem_inc(ph.turn, 1)
                    sp.dma_start(where[:, cols(g, GROUP)], addr[:, cols(i, RING, g * GROUP, GROUP)]
                                 ).then_inc(staged[g], 16)
                    for load in pieces(sp, i * RING + g * GROUP, GROUP, rows, g * GROUP):
                        load().then_inc(staged[g], 16)
            rounds(sp, COLS // RING, stage)

        @block.scalar
        def _(act):
            def label(i):
                for g in range(GROUPS):
                    if not is_first(i):
                        act.wait_ge(written[g], i * (16 * GROUP))
                        act.sem_inc(ph.turn, 1)
                    act.copy(rows[:, cols(g, GROUP), 0], labels[:, cols(i, RING, g * GROUP, GROUP)]
                             ).then_inc(labelled, 1)
            if labels is not None:
                rounds(act, COLS // RING, label)

        @block.gpsimd
        def _(pool):
            with pool.Fori(0, COLS // RING) as i:
                for g in range(GROUPS):
                    pool.wait_ge(staged[g], (i + 1) * (16 * n_staged))
                    if labels is not None:
                        pool.wait_ge(labelled, i * GROUPS + g + 1)
                    pool.sem_inc(ph.turn, 1)
                    for k in range(g * GROUP, (g + 1) * GROUP):
                        pool.indirect_dma_start(table, bass.IndirectOffsetOnAxis(where[:, k:k + 1], 0),
                                                rows[:, k, :], None).then_inc(written[g], 16)
            for g in range(GROUPS):
                pool.wait_ge(written[g], COLS // RING * GROUP * 16)


def build_slots(nc, mem, e, scratch):
    with ExitStack() as ctx:
        addr = ctx.enter_context(nc.sbuf_tensor("dst_addr", [P, COLS], I32))
        info = ctx.enter_context(nc.sbuf_tensor("info", [P, COLS, 4], I32))
        sort_by_tile(nc, mem, "dst", e["dst"], addr[:, :], info[:, :, 3].bitcast(F32), mem.tile_of_dst)
        with Phase(nc, "pack") as ph:
            src, rel = ph.sb("src", [P, COLS], I32), ph.sb("rel", [P, COLS], I32)
            weight = ph.sb("weight", [P, COLS])
            empty = ph.sb("empty", [P, NT, 4], I32)
            loaded, cleared, filled = (ph.sem(n) for n in ("loaded", "cleared", "filled"))
            block = ph.block()

            @block.sync
            def _(sp):
                sp.dma_start(src[:, :], e["src"]).then_inc(loaded, 16)
                sp.dma_start(rel[:, :], e["rel"]).then_inc(loaded, 16)
                sp.dma_start(weight[:, :], e["weight"]).then_inc(loaded, 16)
                sp.wait_ge(cleared, 2)
                sp.dma_start(scratch["slots"].rearrange("(p t) c -> p t c", p=P), empty[:, :, :]).then_inc(filled, 16)
                sp.wait_ge(filled, 16)

            @block.vector
            def _(dve):
                dve.memset(empty[:, :, 0:3], 0).then_inc(cleared, 1)
                dve.memset(empty[:, :, 3].bitcast(F32), NO_NODE).then_inc(cleared, 1)
                dve.wait_ge(loaded, 48)
                dve.scalar_tensor_tensor(info[:, :, 0], src[:, :], float(REL), rel[:, :], ALU.mult, ALU.add)
                dve.tensor_copy(info[:, :, 1], src[:, :])
                dve.tensor_copy(info[:, :, 2].bitcast(F32), weight[:, :])

        info_flat = info[:, :, :].rearrange("p t c -> p (t c)")

        def pieces(sp, t, n, rows, first):
            return [lambda: sp.dma_start(rows[:, first:first + n, :].rearrange("p t c -> p (t c)"),
                                         info_flat[:, bass.ds(t * 4, n * 4)])]

        scatter(nc, "info", addr, scratch["slots"], pieces)
    with Phase(nc, "unpack") as ph:
        back = ph.sb("back", [P, NT, 4], I32)
        loaded = ph.sem("loaded")
        block = ph.block()

        @block.sync
        def _(sp):
            sp.dma_start(back[:, :, :], scratch["slots"].rearrange("(p t) c -> p t c", p=P)).then_inc(loaded, 16)

        @block.vector
        def _(dve):
            dve.wait_ge(loaded, 16)
            dve.tensor_copy(mem.slot_rel[:, :], back[:, :, 0])
            dve.tensor_copy(mem.slot_src[:, :], back[:, :, 1])
            dve.tensor_copy(mem.slot_weight[:, :], back[:, :, 2].bitcast(F32))
            dve.tensor_copy(mem.slot_node[:, 0:NT], back[:, :, 3].bitcast(F32))


def sort_edge_rows(nc, mem, e, scratch):
    with ExitStack() as ctx:
        addr = ctx.enter_context(nc.sbuf_tensor("src_addr", [P, COLS], I32))
        node = ctx.enter_context(nc.sbuf_tensor("src_node", [P, COLS], F32))
        sort_by_tile(nc, mem, "src", e["src"], addr[:, :], node[:, :], mem.tile_of_src)
        with Phase(nc, "empty_rows") as ph:
            piece = NT // 16
            empty = ph.sb("empty", [P, piece, ECOLS])
            cleared, filled = ph.sem("cleared"), ph.sem("filled")
            block = ph.block()

            @block.vector
            def _(dve):
                dve.memset(empty[:, :, 1:ECOLS], 0.0).then_inc(cleared, 1)
                dve.memset(empty[:, :, 0], NO_NODE).then_inc(cleared, 1)

            @block.sync
            def _(sp):
                sp.wait_ge(cleared, 2)
                for n in range(16):
                    sp.dma_start(scratch["edge_rows"].rearrange("(p t) c -> p t c", p=P)[:, n * piece:(n + 1) * piece, :],
                                 empty[:, :, :]).then_inc(filled, 16)
                sp.wait_ge(filled, 16 * 16)

        def pieces(sp, t, n, rows, first):
            return [lambda: sp.dma_start(rows[:, first:first + n, 1:ECOLS], e["attr"][:, bass.ds(t, n), :])]

        scatter(nc, "rows", addr, scratch["edge_rows"], pieces, node)


def load_nodes(nc, mem, e):
    with Phase(nc, "nodes") as ph:
        loaded = ph.sem("loaded")
        block = ph.block()

        @block.sync
        def _(sp):
            sp.dma_start(mem.x[:, :].rearrange("p (t d) -> p t d", d=D),
                         e["x"].rearrange("(t p) d -> p t d", p=P)).then_inc(loaded, 16)
            sp.wait_ge(loaded, 16)


def finish_stats(nc, mem, name, halves):
    with Phase(nc, name) as ph:
        mean, diff, var, std = (ph.sb(n, [P, BUCKETS]) for n in ("mean", "diff", "var", "std"))
        chain, var_ready, std_ready = ph.sem("chain"), ph.sem("var_ready"), ph.sem("std_ready")
        h = halves[:, :].rearrange("p (t s) -> p t s", s=6)
        block = ph.block()

        @block.scalar
        def _(act):
            act.wait_ge(var_ready, 1)
            act.activation(std[:, :], var[:, :], ACT.Sqrt, bias=mem.eps[:, :]).then_inc(std_ready, 1)

        @block.vector
        def _(dve):
            dve.tensor_tensor(mean[:, :], h[:, :, 1], h[:, :, 4], ALU.add).then_inc(chain, 1)
            dve.tensor_tensor(diff[:, :], h[:, :, 1], h[:, :, 4], ALU.subtract).then_inc(chain, 1)
            dve.tensor_tensor(var[:, :], h[:, :, 2], h[:, :, 5], ALU.add).then_inc(chain, 1)
            dve.wait_ge(chain, 2)
            dve.scalar_tensor_tensor(diff[:, :], diff[:, :], 0.25, diff[:, :], ALU.mult, ALU.mult).then_inc(chain, 1)
            dve.wait_ge(chain, 4)
            dve.scalar_tensor_tensor(var[:, :], var[:, :], 1.0 / D, diff[:, :], ALU.mult, ALU.add
                                     ).then_inc(var_ready, 1)
            dve.wait_ge(std_ready, 1)
            dve.reciprocal(mem.rstd[:, :], std[:, :]).then_inc(chain, 1)
            dve.wait_ge(chain, 5)
            dve.scalar_tensor_tensor(mem.shift[:, :], mean[:, :], -0.5, mem.rstd[:, :], ALU.mult, ALU.mult)


def first_stats(nc, mem, halves):
    with Phase(nc, "stats") as ph:
        block = ph.block()

        @block.vector
        def _(dve):
            with dve.Fori(0, BUCKETS) as t:
                dve.bn_stats(halves[:, cols(t, 6)], mem.x[:, cols(t, D)])


PAIRS = BUCKETS // 2


def relational_tables(nc, mem, e, layer, table):
    chunks = REL * D // 512
    with Phase(nc, f"rel{layer}") as ph:
        w = ph.sb("w", [P, 2, REL * D + D])
        bias = ph.sb("bias", [P, D])
        h = [ph.sb(f"h{u}", [P, D]) for u in range(2)]
        turned = [ph.sb(f"turned{u}", [P, D]) for u in range(2)]
        out = [ph.sb(f"out{u}", [P, REL * D]) for u in range(2)]
        turned_ps = [ph.psum(f"turned_ps{u}", [P, 512]) for u in range(2)]
        product_ps = [ph.psum(f"product_ps{c}", [P, 512]) for c in range(chunks + 1)]
        loaded, h_ready, transposed, turned_ready, products, act_out, dve_out = (
            ph.sem(n) for n in ("loaded", "h_ready", "transposed", "turned_ready", "products",
                                "act_out", "dve_out"))
        stored = [ph.sem(f"stored{u}") for u in range(2)]
        block = ph.block()

        @block.sync
        def _(sp):
            for k in range(2):
                sp.dma_start(w[:, k, :], e["rel_w"][:, layer, k, :]).then_inc(loaded, 16)
            sp.dma_start(bias[:, :], e["rel_b"][layer].partition_broadcast(P)).then_inc(loaded, 16)

            def store(i):
                for u in range(2):
                    t = i * 2 + u
                    sp.wait_ge(act_out, (t + 1) * 3)
                    sp.sem_inc(ph.turn, 1)
                    sp.wait_ge(dve_out, (t + 1) * 2)
                    sp.sem_inc(ph.turn, 1)
                    sp.dma_start(table.rearrange("(n r) d -> n (r d)", r=REL)[bass.ds(t * P, P), :],
                                 out[u][:, :]).then_inc(stored[u], 16)
            rounds(sp, PAIRS, store)
            for u in range(2):
                sp.wait_ge(stored[u], 16 * PAIRS)

        @block.scalar
        def _(act):
            def tiles(i):
                for u in range(2):
                    t = i * 2 + u
                    if not is_first(i):
                        act.wait_ge(transposed, t - 1)
                        act.sem_inc(ph.turn, 1)
                    if layer == 0:
                        ins = act.activation(h[u][:, :], mem.x[:, cols(t, D)], ACT.Relu,
                                             bias=mem.shift[:, bass.ds(t, 1)], scale=mem.rstd[:, bass.ds(t, 1)])
                    else:
                        ins = act.activation(h[u][:, :], mem.acc[:, cols(t, ACCW, 0, D)], ACT.Relu)
                    ins.then_inc(h_ready, 1)
                for u in range(2):
                    t = i * 2 + u
                    act.wait_ge(transposed, t + 1)
                    if not is_first(i):
                        act.wait_ge(products, (t - 1) * (chunks + 1))
                    act.copy(turned[u][:, :], turned_ps[u][:, 0:D]).then_inc(turned_ready, 1)
                for u in range(2):
                    t = i * 2 + u
                    if not is_first(i):
                        act.wait_ge(stored[u], i * 16)
                    for c in range(3):
                        act.wait_ge(products, t * (chunks + 1) + c + 1)
                        act.copy(out[u][:, cols(c, 512)], product_ps[c][:, :]).then_inc(act_out, 1)
            rounds(act, PAIRS, tiles)

        @block.tensor
        def _(pe):
            pe.wait_ge(loaded, 48)

            def tiles(i):
                for u in range(2):
                    t = i * 2 + u
                    pe.wait_ge(h_ready, t + 1)
                    if not is_first(i):
                        pe.wait_ge(turned_ready, t - 1)
                    for k in range(2):
                        ins = pe.transpose(turned_ps[u][:, cols(k, P)], h[u][:, cols(k, P)], mem.ident[:, :])
                    ins.then_inc(transposed, 1)
                for u in range(2):
                    t = i * 2 + u
                    pe.wait_ge(turned_ready, t + 1)
                    if not (is_first(i) and u == 0):
                        pe.wait_ge(act_out, t * 3)
                        pe.wait_ge(dve_out, t * 2)
                    for c in range(chunks + 1):
                        n = 512 if c < chunks else D
                        for k in range(2):
                            ins = pe.matmul(product_ps[c][:, 0:n], turned[u][:, cols(k, P)],
                                            w[:, k, c * 512:c * 512 + n], start=(k == 0), stop=(k == 1))
                        ins.then_inc(products, 1)
            rounds(pe, PAIRS, tiles)

        @block.vector
        def _(dve):
            dve.wait_ge(loaded, 48)

            def tiles(i):
                for u in range(2):
                    t = i * 2 + u
                    if not is_first(i):
                        dve.wait_ge(stored[u], i * 16)
                    dve.wait_ge(products, t * (chunks + 1) + chunks)
                    dve.tensor_copy(out[u][:, cols(3, 512)], product_ps[3][:, :]).then_inc(dve_out, 1)
                    dve.wait_ge(products, (t + 1) * (chunks + 1))
                    dve.tensor_tensor(mem.acc[:, cols(t, ACCW, 0, D)], product_ps[chunks][:, 0:D], bias[:, :],
                                      ALU.add).then_inc(dve_out, 1)
            rounds(dve, PAIRS, tiles)


def aggregate(nc, mem, name, table, slot_row, weighted=False, degree=False, edge_rows=None):
    width = D + (1 if degree else 0)
    n_rounds = NT // RING
    with Phase(nc, name) as ph:
        rows = ph.sb("rows", [P, RING, width])
        which = ph.sb("which", [P, RING], I32)
        onehot = ph.sb("onehot", [P, 2 * GROUP, P])
        sums_ps = [ph.psum(f"sums_ps{k}", [P, 512]) for k in range(GROUP)]
        staged = [ph.sem(f"staged{g}") for g in range(GROUPS)]
        landed = [ph.sem(f"landed{g}") for g in range(GROUPS)]
        onehots, products, added, filled = (
            ph.sem(n) for n in ("onehots", "products", "added", "filled"))
        if edge_rows is not None:
            erow = ph.sb("erow", [P, RING, ECOLS])
            ehot = ph.sb("ehot", [P, GROUP, P])
            eones = ph.sb("eones", [P, 1])
            esums_ps = [ph.psum(f"esums_ps{k}", [P, 512]) for k in range(GROUP)]
            eloaded = [ph.sem(f"eloaded{g}") for g in range(GROUPS)]
            ehots, eproducts, eadded = ph.sem("ehots"), ph.sem("eproducts"), ph.sem("eadded")
        block = ph.block()

        @block.sync
        def _(sp):
            def stage(i):
                for g in range(GROUPS):
                    if not is_first(i):
                        sp.wait_ge(landed[g], i * (16 * GROUP))
                        sp.sem_inc(ph.turn, 1)
                    sp.dma_start(which[:, cols(g, GROUP)], slot_row[:, cols(i, RING, g * GROUP, GROUP)]
                                 ).then_inc(staged[g], 16)
                    if edge_rows is not None:
                        if not is_first(i):
                            sp.wait_ge(eproducts, (i - 1) * RING + (g + 1) * GROUP)
                            sp.sem_inc(ph.turn, 1)
                        sp.dma_start(erow[:, cols(g, GROUP), :],
                                     edge_rows.rearrange("(p t) c -> p t c", p=P)[:, cols(i, RING, g * GROUP, GROUP), :]
                                     ).then_inc(eloaded[g], 16)
            rounds(sp, n_rounds, stage)

        @block.gpsimd
        def _(pool):
            def gather(i):
                for g in range(GROUPS):
                    pool.wait_ge(staged[g], (i + 1) * 16)
                    if not is_first(i):
                        pool.wait_ge(products, (i - 1) * RING + (g + 1) * GROUP)
                        pool.sem_inc(ph.turn, 1)
                    for k in range(g * GROUP, (g + 1) * GROUP):
                        pool.indirect_dma_start(rows[:, k, 0:D], None, table,
                                                bass.IndirectOffsetOnAxis(which[:, k:k + 1], 0)
                                                ).then_inc(landed[g], 16)
            rounds(pool, n_rounds, gather)

        @block.tensor
        def _(pe):
            def products_of(i):
                for g in range(GROUPS):
                    pe.wait_ge(landed[g], (i + 1) * (16 * GROUP))
                    for k in range(GROUP):
                        t = i * RING + g * GROUP + k
                        pe.wait_ge(onehots, t + 1)
                        if degree and is_first(i) and g == 0 and k == 0:
                            pe.wait_ge(filled, 1)
                        if not (is_first(i) and g == 0):
                            pe.wait_ge(added, t - GROUP + 1)
                        pe.matmul(sums_ps[k][:, 0:width], onehot[:, g % 2 * GROUP + k, :],
                                  rows[:, g * GROUP + k, :], start=True, stop=True).then_inc(products, 1)
                    if edge_rows is not None:
                        pe.wait_ge(eloaded[g], (i + 1) * 16)
                        for k in range(GROUP):
                            t = i * RING + g * GROUP + k
                            pe.wait_ge(ehots, t + 1)
                            if not (is_first(i) and g == 0):
                                pe.wait_ge(eadded, t - GROUP + 1)
                            pe.matmul(esums_ps[k][:, 0:EDGE_D], ehot[:, k, :], erow[:, g * GROUP + k, 1:ECOLS],
                                      start=True, stop=True)
                            pe.matmul(esums_ps[k][:, EDGE_D:ECOLS], ehot[:, k, :], eones[:, :],
                                      start=True, stop=True).then_inc(eproducts, 1)
            rounds(pe, n_rounds, products_of)

        @block.vector
        def _(dve):
            def onehots_of(t, k):
                node = mem.slot_node[:, bass.ds(t, 1)]
                out = onehot[:, k, :]
                if weighted:
                    ins = dve.tensor_scalar(out, mem.iota[:, :], node, mem.slot_weight[:, bass.ds(t, 1)],
                                            ALU.is_equal, ALU.mult)
                else:
                    ins = dve.tensor_scalar(out, mem.iota[:, :], node, None, ALU.is_equal)
                ins.then_inc(onehots, 1)

            if degree:
                dve.memset(rows[:, :, D], 1.0).then_inc(filled, 1)
            if edge_rows is not None:
                dve.memset(eones[:, :], 1.0)
            for k in range(GROUP):
                onehots_of(k, k)

            def sums(i):
                for g in range(GROUPS):
                    for k in range(GROUP):
                        if not (isinstance(i, int) and i == n_rounds - 1 and g == GROUPS - 1):
                            onehots_of(i * RING + (g + 1) * GROUP + k, (g + 1) % 2 * GROUP + k)
                    if edge_rows is not None:
                        dve.wait_ge(eloaded[g], (i + 1) * 16)
                        for k in range(GROUP):
                            dve.tensor_scalar(ehot[:, k, :], mem.iota[:, :], erow[:, g * GROUP + k, 0:1], None,
                                              ALU.is_equal).then_inc(ehots, 1)
                    for k in range(GROUP):
                        t = i * RING + g * GROUP + k
                        tile = dve.value_load(mem.tile_of_dst[0:1, bass.ds(t, 1)], min_val=0, max_val=BUCKETS - 1)
                        into = mem.acc[:, cols(tile, ACCW, 0, width)]
                        dve.wait_ge(products, t + 1)
                        if not (is_first(i) and g == 0 and k == 0):
                            dve.wait_ge(added, t)
                        dve.tensor_tensor(into, into, sums_ps[k][:, 0:width], ALU.add).then_inc(added, 1)
                    if edge_rows is not None:
                        for k in range(GROUP):
                            t = i * RING + g * GROUP + k
                            tile = dve.value_load(mem.tile_of_src[0:1, bass.ds(t, 1)], min_val=0, max_val=BUCKETS - 1)
                            into = mem.edge_acc[:, cols(tile, ECOLS)]
                            dve.wait_ge(eproducts, t + 1)
                            if not (is_first(i) and g == 0 and k == 0):
                                dve.wait_ge(eadded, t)
                            dve.tensor_tensor(into, into, esums_ps[k][:, 0:ECOLS], ALU.add).then_inc(eadded, 1)
            sums(0)
            with dve.Fori(1, n_rounds - 1) as i:
                sums(i)
            sums(n_rounds - 1)


def relational_end(nc, mem, halves):
    with Phase(nc, "relend") as ph:
        s = [ph.sb(f"s{u}", [P, D]) for u in range(2)]
        sigmoids, x_ready = ph.sem("sigmoids"), ph.sem("x_ready")
        block = ph.block()

        @block.scalar
        def _(act):
            def tiles(i):
                for u in range(2):
                    t = i * 2 + u
                    if not is_first(i):
                        act.wait_ge(x_ready, t - 1)
                        act.sem_inc(ph.turn, 1)
                    act.activation(s[u][:, :], mem.acc[:, cols(t, ACCW, 0, D)], ACT.Sigmoid).then_inc(sigmoids, 1)
            rounds(act, PAIRS, tiles)

        @block.vector
        def _(dve):
            with dve.Fori(0, PAIRS) as i:
                for u in range(2):
                    t = i * 2 + u
                    x = mem.x[:, cols(t, D)]
                    dve.wait_ge(sigmoids, t + 1)
                    dve.tensor_tensor(x, x, s[u][:, :], ALU.add).then_inc(x_ready, 1)
                for u in range(2):
                    t = i * 2 + u
                    dve.wait_ge(x_ready, t + 1)
                    dve.sem_inc(ph.turn, 1)
                    dve.bn_stats(halves[:, cols(t, 6)], mem.x[:, cols(t, D)])


def node_table(nc, mem, table):
    with Phase(nc, "node_table") as ph:
        h = [ph.sb(f"h{u}", [P, D]) for u in range(2)]
        deg = ph.sb("deg", [P, BUCKETS])
        h_ready, chain = ph.sem("h_ready"), ph.sem("chain")
        stored = [ph.sem(f"stored{u}") for u in range(2)]
        block = ph.block()

        @block.scalar
        def _(act):
            def tiles(i):
                for u in range(2):
                    t = i * 2 + u
                    if not is_first(i):
                        act.wait_ge(stored[u], i * 16)
                        act.sem_inc(ph.turn, 1)
                    act.activation(h[u][:, :], mem.x[:, cols(t, D)], ACT.Relu, bias=mem.shift[:, bass.ds(t, 1)],
                                   scale=mem.rstd[:, bass.ds(t, 1)]).then_inc(h_ready, 1)
            rounds(act, PAIRS, tiles)

        @block.sync
        def _(sp):
            with sp.Fori(0, PAIRS) as i:
                for u in range(2):
                    sp.wait_ge(h_ready, i * 2 + u + 1)
                    sp.sem_inc(ph.turn, 1)
                    sp.dma_start(table[bass.ds((i * 2 + u) * P, P), :], h[u][:, :]).then_inc(stored[u], 16)
            for u in range(2):
                sp.wait_ge(stored[u], 16 * PAIRS)

        @block.vector
        def _(dve):
            acc = mem.acc[:, :].rearrange("p (t c) -> p t c", c=ACCW)
            dve.tensor_scalar(deg[:, :], acc[:, :, D], 1.0, None, ALU.max).then_inc(chain, 1)
            dve.wait_ge(chain, 1)
            dve.reciprocal(mem.inv_deg[:, :], deg[:, :])
            dve.memset(acc[:, :, 0:D], 0.0)


def conv_layers(nc, mem, e, table):
    L = 4
    with Phase(nc, "conv") as ph:
        sb, sem = ph.sb, ph.sem
        w = sb("w", [P, 2, 2, L * D])
        bias, gain, norm_b = (sb(n, [P, L * D]) for n in ("bias", "gain", "norm_b"))
        two = range(2)
        node, agg = [sb(f"node{u}", [P, D]) for u in two], [sb(f"agg{u}", [P, D]) for u in two]
        turned = [sb(f"turned{u}", [P, 4 * P]) for u in two]
        node_b = [sb(f"node_b{u}", [P, L * D]) for u in two]
        z = [sb(f"z{u}", [P, L * D]) for u in two]
        stats = [sb(f"stats{u}", [P, L * 6]) for u in two]
        mv = [sb(f"mv{u}", [P, L * 2]) for u in two]
        std, rstd, shift = ([sb(f"{n}{u}", [P, L]) for u in two] for n in ("std", "rstd", "shift"))
        turned_ps = [ph.psum(f"turned_ps{u}", [P, 512]) for u in two]
        z_ps = [[ph.psum(f"z_ps{u}{c}", [P, 512]) for c in two] for u in two]
        loaded = sem("loaded")
        node_loaded = [sem(f"node_loaded{u}") for u in two]
        (agg_ready, transposed, turned_ready, products, node_b_ready, z_ready, stats_ready, mv_ready, std_ready,
         rstd_ready, shift_ready, normed, gained, biased, positive, summed) = (
            sem(n) for n in ("agg_ready", "transposed", "turned_ready", "products", "node_b_ready", "z_ready",
                             "stats_ready", "mv_ready", "std_ready", "rstd_ready", "shift_ready", "normed",
                             "gained", "biased", "positive", "summed"))
        block = ph.block()

        @block.sync
        def _(sp):
            sp.dma_start(w[:, :, :, :], e["conv_w"]).then_inc(loaded, 16)
            for into, name in ((bias, "conv_b"), (gain, "conv_g"), (norm_b, "conv_n")):
                sp.dma_start(into[:, :], e[name][0].partition_broadcast(P)).then_inc(loaded, 16)

            def load(i):
                for u in two:
                    t = i * 2 + u
                    if not is_first(i):
                        sp.wait_ge(transposed, t - 1)
                        sp.sem_inc(ph.turn, 1)
                        sp.wait_ge(node_b_ready, t - 1)
                        sp.sem_inc(ph.turn, 1)
                    sp.dma_start(node[u][:, :], table[bass.ds(t * P, P), :]).then_inc(node_loaded[u], 16)
            rounds(sp, PAIRS, load)

        @block.gpsimd
        def _(pool):
            pool.wait_ge(loaded, 64)

            def tiles(i):
                for u in two:
                    t = i * 2 + u
                    pool.wait_ge(node_loaded[u], (i + 1) * 16)
                    if not is_first(i):
                        pool.wait_ge(z_ready, (t - 1) * 2)
                    pool.tensor_tensor(node_b[u][:, :].rearrange("p (l d) -> p l d", l=L),
                                       node[u][:, :].unsqueeze(1).broadcast_to([P, L, D]),
                                       bias[:, :].rearrange("p (l d) -> p l d", l=L), ALU.add).then_inc(node_b_ready, 1)
                for u in two:
                    t = i * 2 + u
                    pool.wait_ge(normed, (t + 1) * L)
                    pool.tensor_tensor(z[u][:, :], z[u][:, :], gain[:, :], ALU.mult).then_inc(gained, 1)
                    pool.wait_ge(gained, t + 1)
                    pool.tensor_tensor(z[u][:, :], z[u][:, :], norm_b[:, :], ALU.add).then_inc(biased, 1)
            rounds(pool, PAIRS, tiles)

        @block.tensor
        def _(pe):
            pe.wait_ge(loaded, 64)

            def tiles(i):
                for u in two:
                    t = i * 2 + u
                    pe.wait_ge(node_loaded[u], (i + 1) * 16)
                    pe.wait_ge(agg_ready, t + 1)
                    if not is_first(i):
                        pe.wait_ge(turned_ready, t - 1)
                    for k in range(4):
                        src = (agg, node)[k // 2][u]
                        ins = pe.transpose(turned_ps[u][:, cols(k, P)], src[:, cols(k % 2, P)], mem.ident[:, :])
                    ins.then_inc(transposed, 1)
                for u in two:
                    t = i * 2 + u
                    pe.wait_ge(turned_ready, t + 1)
                    if not is_first(i):
                        pe.wait_ge(z_ready, (t - 1) * 2)
                    for c in two:
                        for k in range(4):
                            ins = pe.matmul(z_ps[u][c][:, :], turned[u][:, cols(k, P)],
                                            w[:, k // 2, k % 2, cols(c, 512)], start=(k == 0), stop=(k == 3))
                        ins.then_inc(products, 1)
            rounds(pe, PAIRS, tiles)

        @block.scalar
        def _(act):
            def tiles(i):
                for u in two:
                    t = i * 2 + u
                    act.wait_ge(transposed, t + 1)
                    if not is_first(i):
                        act.wait_ge(products, (t - 1) * 2)
                    act.copy(turned[u][:, :], turned_ps[u][:, :]).then_inc(turned_ready, 1)
                for u in two:
                    t = i * 2 + u
                    act.wait_ge(mv_ready, (t + 1) * L)
                    act.activation(std[u][:, :], mv[u][:, :].rearrange("p (l s) -> p l s", s=2)[:, :, 1], ACT.Sqrt,
                                   bias=mem.eps[:, :]).then_inc(std_ready, 1)
                for u in two:
                    t = i * 2 + u
                    act.wait_ge(shift_ready, t + 1)
                    for n in range(L):
                        act.activation(z[u][:, cols(n, D)], z[u][:, cols(n, D)], ACT.Identity,
                                       bias=shift[u][:, n:n + 1], scale=rstd[u][:, n:n + 1]).then_inc(normed, 1)
                for u in two:
                    t = i * 2 + u
                    act.wait_ge(biased, t + 1)
                    act.activation(z[u][:, :], z[u][:, :], ACT.Relu).then_inc(positive, 1)
            rounds(act, PAIRS, tiles)

        @block.vector
        def _(dve):
            def tiles(i):
                for u in two:
                    t = i * 2 + u
                    if not is_first(i):
                        dve.wait_ge(transposed, t - 1)
                    dve.tensor_scalar(agg[u][:, :], mem.acc[:, cols(t, ACCW, 0, D)], mem.inv_deg[:, bass.ds(t, 1)],
                                      None, ALU.mult).then_inc(agg_ready, 1)
                for u in two:
                    t = i * 2 + u
                    dve.wait_ge(node_b_ready, t + 1)
                    if not is_first(i):
                        dve.wait_ge(summed, t - 1)
                    for c in two:
                        dve.wait_ge(products, t * 2 + c + 1)
                        dve.tensor_tensor(z[u][:, cols(c, 512)], z_ps[u][c][:, :], node_b[u][:, cols(c, 512)],
                                          ALU.add).then_inc(z_ready, 1)
                for u in two:
                    t = i * 2 + u
                    dve.wait_ge(z_ready, (t + 1) * 2)
                    for n in range(L):
                        dve.bn_stats(stats[u][:, cols(n, 6)], z[u][:, cols(n, D)]).then_inc(stats_ready, 1)
                for u in two:
                    t = i * 2 + u
                    dve.wait_ge(stats_ready, (t + 1) * L)
                    dve.sem_inc(ph.turn, 1)
                    for n in range(L):
                        dve.bn_aggr(mv[u][:, cols(n, 2)], stats[u][:, cols(n, 6)]).then_inc(mv_ready, 1)
                for u in two:
                    t = i * 2 + u
                    dve.wait_ge(std_ready, t + 1)
                    dve.reciprocal(rstd[u][:, :], std[u][:, :]).then_inc(rstd_ready, 1)
                for u in two:
                    t = i * 2 + u
                    dve.wait_ge(rstd_ready, t + 1)
                    dve.scalar_tensor_tensor(shift[u][:, :], mv[u][:, :].rearrange("p (l s) -> p l s", s=2)[:, :, 0],
                                             -1.0, rstd[u][:, :], ALU.mult, ALU.mult).then_inc(shift_ready, 1)
                for u in two:
                    t = i * 2 + u
                    dve.wait_ge(positive, t + 1)
                    dve.sem_inc(ph.turn, 1)
                    dve.tensor_reduce(mem.acc[:, cols(t, ACCW, 0, D)], z[u][:, :].rearrange("p (l d) -> p d l", l=L),
                                      AX.X, ALU.add).then_inc(summed, 1)
            rounds(dve, PAIRS, tiles)


def mlp_layer(nc, mem, e, n, halves):
    with Phase(nc, f"mlp{n}") as ph:
        sb, sem = ph.sb, ph.sem
        w = sb("w", [P, 2, D])
        bias, gain, norm_b = (sb(x, [P, D]) for x in ("bias", "gain", "norm_b"))
        two = range(2)
        h, turned, z = ([sb(f"{x}{u}", [P, D]) for u in two] for x in ("h", "turned", "z"))
        stats, mv = [sb(f"stats{u}", [P, 6]) for u in two], [sb(f"mv{u}", [P, 2]) for u in two]
        std, rstd, shift = ([sb(f"{x}{u}", [P, 1]) for u in two] for x in ("std", "rstd", "shift"))
        turned_ps = [ph.psum(f"turned_ps{u}", [P, 512]) for u in two]
        z_ps = [ph.psum(f"z_ps{u}", [P, 512]) for u in two]
        (loaded, h_ready, transposed, turned_ready, products, z_ready, stats_ready, mv_ready, std_ready,
         rstd_ready, shift_ready, normed, gained, biased, done) = (
            sem(x) for x in ("loaded", "h_ready", "transposed", "turned_ready", "products", "z_ready",
                             "stats_ready", "mv_ready", "std_ready", "rstd_ready", "shift_ready", "normed",
                             "gained", "biased", "done"))
        block = ph.block()

        @block.sync
        def _(sp):
            sp.dma_start(w[:, :, :], e["mlp_w"][:, n, :, :]).then_inc(loaded, 16)
            for into, row in ((bias, 0), (gain, 1), (norm_b, 2)):
                sp.dma_start(into[:, :], e["mlp_v"][3 * n + row].partition_broadcast(P)).then_inc(loaded, 16)

        @block.gpsimd
        def _(pool):
            pool.wait_ge(loaded, 64)
            with pool.Fori(0, PAIRS) as i:
                for u in two:
                    t = i * 2 + u
                    pool.wait_ge(normed, t + 1)
                    pool.tensor_tensor(z[u][:, :], z[u][:, :], gain[:, :], ALU.mult).then_inc(gained, 1)
                    pool.wait_ge(gained, t + 1)
                    pool.tensor_tensor(z[u][:, :], z[u][:, :], norm_b[:, :], ALU.add).then_inc(biased, 1)

        @block.tensor
        def _(pe):
            pe.wait_ge(loaded, 64)

            def tiles(i):
                for u in two:
                    t = i * 2 + u
                    pe.wait_ge(h_ready, t + 1)
                    if not is_first(i):
                        pe.wait_ge(turned_ready, t - 1)
                    for k in two:
                        ins = pe.transpose(turned_ps[u][:, cols(k, P)], h[u][:, cols(k, P)], mem.ident[:, :])
                    ins.then_inc(transposed, 1)
                for u in two:
                    t = i * 2 + u
                    pe.wait_ge(turned_ready, t + 1)
                    if not is_first(i):
                        pe.wait_ge(z_ready, t - 1)
                    for k in two:
                        ins = pe.matmul(z_ps[u][:, 0:D], turned[u][:, cols(k, P)], w[:, k, :],
                                        start=(k == 0), stop=(k == 1))
                    ins.then_inc(products, 1)
            rounds(pe, PAIRS, tiles)

        @block.scalar
        def _(act):
            def tiles(i):
                for u in two:
                    t = i * 2 + u
                    if not is_first(i):
                        act.wait_ge(transposed, t - 1)
                        act.sem_inc(ph.turn, 1)
                    act.copy(h[u][:, :], mem.acc[:, cols(t, ACCW, 0, D)]).then_inc(h_ready, 1)
                for u in two:
                    t = i * 2 + u
                    act.wait_ge(transposed, t + 1)
                    if not is_first(i):
                        act.wait_ge(products, t - 1)
                    act.copy(turned[u][:, :], turned_ps[u][:, 0:D]).then_inc(turned_ready, 1)
                for u in two:
                    t = i * 2 + u
                    act.wait_ge(mv_ready, t + 1)
                    act.activation(std[u][:, :], mv[u][:, 1:2], ACT.Sqrt, bias=mem.eps[:, :]).then_inc(std_ready, 1)
                for u in two:
                    t = i * 2 + u
                    act.wait_ge(shift_ready, t + 1)
                    act.activation(z[u][:, :], z[u][:, :], ACT.Identity, bias=shift[u][:, :], scale=rstd[u][:, :]
                                   ).then_inc(normed, 1)
            rounds(act, PAIRS, tiles)

        @block.vector
        def _(dve):
            dve.wait_ge(loaded, 64)

            def tiles(i):
                for u in two:
                    t = i * 2 + u
                    dve.wait_ge(products, t + 1)
                    if not is_first(i):
                        dve.wait_ge(done, t - 1)
                    dve.tensor_tensor(z[u][:, :], z_ps[u][:, 0:D], bias[:, :], ALU.add).then_inc(z_ready, 1)
                for u in two:
                    t = i * 2 + u
                    dve.wait_ge(z_ready, t + 1)
                    dve.bn_stats(stats[u][:, :], z[u][:, :]).then_inc(stats_ready, 1)
                for u in two:
                    t = i * 2 + u
                    dve.wait_ge(stats_ready, t + 1)
                    dve.sem_inc(ph.turn, 1)
                    dve.bn_aggr(mv[u][:, :], stats[u][:, :]).then_inc(mv_ready, 1)
                for u in two:
                    t = i * 2 + u
                    dve.wait_ge(std_ready, t + 1)
                    dve.reciprocal(rstd[u][:, :], std[u][:, :]).then_inc(rstd_ready, 1)
                for u in two:
                    t = i * 2 + u
                    dve.wait_ge(rstd_ready, t + 1)
                    dve.scalar_tensor_tensor(shift[u][:, :], mv[u][:, 0:1], -1.0, rstd[u][:, :], ALU.mult, ALU.mult
                                             ).then_inc(shift_ready, 1)
                for u in two:
                    t = i * 2 + u
                    dve.wait_ge(biased, t + 1)
                    if n == 0:
                        dve.tensor_scalar(mem.acc[:, cols(t, ACCW, 0, D)], z[u][:, :], 0.0, None, ALU.max
                                          ).then_inc(done, 1)
                    else:
                        x = mem.x[:, cols(t, D)]
                        dve.scalar_tensor_tensor(x, z[u][:, :], 0.0, x, ALU.max, ALU.add).then_inc(done, 1)
                if n == 1:
                    for u in two:
                        t = i * 2 + u
                        dve.wait_ge(done, t + 1)
                        dve.sem_inc(ph.turn, 1)
                        dve.bn_stats(halves[:, cols(t, 6)], mem.x[:, cols(t, D)])
            rounds(dve, PAIRS, tiles)


def edge_layer(nc, mem, e, halves):
    F = e["edge_w"].shape[2]
    with Phase(nc, "edge") as ph:
        sb, sem = ph.sb, ph.sem
        two = range(2)
        w1, w1e, w1u = sb("w1", [P, 2, F]), sb("w1e", [EDGE_D, F]), sb("w1u", [P, F])
        w2, b1, b2 = sb("w2", [P, F // P, D]), sb("b1", [P, F]), sb("b2", [P, D])
        u_col, u_wide = sb("u_col", [P, 1]), sb("u_wide", [P, P])
        count, inv_count = sb("count", [P, BUCKETS]), sb("inv_count", [P, BUCKETS])
        h, turned, out = ([sb(f"{x}{u}", [P, D]) for u in two] for x in ("h", "turned", "out"))
        mean, mean_t = [sb(f"mean{u}", [P, EDGE_D]) for u in two], [sb(f"mean_t{u}", [EDGE_D, P]) for u in two]
        hidden, hidden_t = ([sb(f"{x}{u}", [P, F]) for u in two] for x in ("hidden", "hidden_t"))
        turned_ps, hidden_ps, hidden_t_ps, out_ps = (
            [ph.psum(f"{x}{u}", [P, 512]) for u in two] for x in ("turned_ps", "hidden_ps", "hidden_t_ps", "out_ps"))
        (loaded, chain, u_ready, u_product, u_taken, h_ready, mean_ready, transposed, turned_ready, products,
         hidden_ready, positive, hidden_transposed, hidden_t_ready, out_products, out_ready, x_ready) = (
            sem(x) for x in ("loaded", "chain", "u_ready", "u_product", "u_taken", "h_ready", "mean_ready",
                             "transposed", "turned_ready", "products", "hidden_ready", "positive",
                             "hidden_transposed", "hidden_t_ready", "out_products", "out_ready", "x_ready"))
        block = ph.block()

        @block.sync
        def _(sp):
            for into, src in ((w1[:, :, :], e["edge_w"]), (w1e[:, :], e["edge_we"]), (w1u[:, :], e["edge_wu"]),
                              (w2[:, :, :], e["edge_w2"]), (u_col[:, :], e["edge_u"]),
                              (b1[:, :], e["edge_b1"][0].partition_broadcast(P)),
                              (b2[:, :], e["edge_b2"][0].partition_broadcast(P))):
                sp.dma_start(into, src).then_inc(loaded, 16)

        @block.tensor
        def _(pe):
            pe.wait_ge(loaded, 7 * 16)
            pe.wait_ge(u_ready, 1)
            pe.matmul(hidden_ps[0][:, :], u_wide[:, :], w1u[:, :], start=True, stop=True).then_inc(u_product, 1)
            pe.wait_ge(u_taken, 1)

            def tiles(i):
                for u in two:
                    t = i * 2 + u
                    pe.wait_ge(h_ready, t + 1)
                    pe.wait_ge(mean_ready, t + 1)
                    if not is_first(i):
                        pe.wait_ge(turned_ready, (t - 1) * 2)
                    for k in two:
                        pe.transpose(turned_ps[u][:, cols(k, P)], h[u][:, cols(k, P)], mem.ident[:, :])
                    pe.transpose(turned_ps[u][0:EDGE_D, cols(2, P)], mean[u][:, :], mem.ident[:, :]
                                 ).then_inc(transposed, 1)
                for u in two:
                    t = i * 2 + u
                    pe.wait_ge(turned_ready, (t + 1) * 2)
                    if not is_first(i):
                        pe.wait_ge(hidden_ready, t - 1)
                    for k in two:
                        pe.matmul(hidden_ps[u][:, :], turned[u][:, cols(k, P)], w1[:, k, :], start=(k == 0), stop=False)
                    pe.matmul(hidden_ps[u][:, :], mean_t[u][:, :], w1e[:, :], start=False, stop=True
                              ).then_inc(products, 1)
                for u in two:
                    t = i * 2 + u
                    pe.wait_ge(positive, t + 1)
                    if not is_first(i):
                        pe.wait_ge(hidden_t_ready, t - 1)
                    for k in range(F // P):
                        ins = pe.transpose(hidden_t_ps[u][:, cols(k, P)], hidden[u][:, cols(k, P)], mem.ident[:, :])
                    ins.then_inc(hidden_transposed, 1)
                for u in two:
                    t = i * 2 + u
                    pe.wait_ge(hidden_t_ready, t + 1)
                    if not is_first(i):
                        pe.wait_ge(out_ready, t - 1)
                    for k in range(F // P):
                        ins = pe.matmul(out_ps[u][:, 0:D], hidden_t[u][:, cols(k, P)], w2[:, k, :],
                                        start=(k == 0), stop=(k == F // P - 1))
                    ins.then_inc(out_products, 1)
            rounds(pe, PAIRS, tiles)

        @block.scalar
        def _(act):
            def tiles(i):
                for u in two:
                    t = i * 2 + u
                    if not is_first(i):
                        act.wait_ge(transposed, t - 1)
                        act.sem_inc(ph.turn, 1)
                    act.activation(h[u][:, :], mem.x[:, cols(t, D)], ACT.Relu, bias=mem.shift[:, bass.ds(t, 1)],
                                   scale=mem.rstd[:, bass.ds(t, 1)]).then_inc(h_ready, 1)
                for u in two:
                    t = i * 2 + u
                    act.wait_ge(transposed, t + 1)
                    if not is_first(i):
                        act.wait_ge(products, t - 1)
                    act.copy(turned[u][:, :], turned_ps[u][:, 0:D]).then_inc(turned_ready, 1)
                    act.copy(mean_t[u][:, :], turned_ps[u][0:EDGE_D, cols(2, P)]).then_inc(turned_ready, 1)
                for u in two:
                    t = i * 2 + u
                    act.wait_ge(hidden_ready, t + 1)
                    act.activation(hidden[u][:, :], hidden[u][:, :], ACT.Relu).then_inc(positive, 1)
                for u in two:
                    t = i * 2 + u
                    act.wait_ge(hidden_transposed, t + 1)
                    if not is_first(i):
                        act.wait_ge(out_products, t - 1)
                    act.copy(hidden_t[u][:, :], hidden_t_ps[u][:, :]).then_inc(hidden_t_ready, 1)
            rounds(act, PAIRS, tiles)

        @block.vector
        def _(dve):
            edges = mem.edge_acc[:, :].rearrange("p (t c) -> p t c", c=ECOLS)
            dve.tensor_scalar(count[:, :], edges[:, :, EDGE_D], 1.0, None, ALU.max).then_inc(chain, 1)
            dve.wait_ge(loaded, 7 * 16)
            dve.tensor_scalar(u_wide[:, :], mem.ones[:, :], u_col[:, :], None, ALU.mult).then_inc(u_ready, 1)
            dve.wait_ge(chain, 1)
            dve.reciprocal(inv_count[:, :], count[:, :]).then_inc(chain, 1)
            dve.wait_ge(u_product, 1)
            dve.tensor_tensor(b1[:, :], b1[:, :], hidden_ps[0][:, :], ALU.add).then_inc(u_taken, 1)
            dve.wait_ge(chain, 2)
            dve.wait_ge(u_taken, 1)

            def tiles(i):
                for u in two:
                    t = i * 2 + u
                    if not is_first(i):
                        dve.wait_ge(transposed, t - 1)
                    dve.tensor_scalar(mean[u][:, :], mem.edge_acc[:, cols(t, ECOLS, 0, EDGE_D)],
                                      inv_count[:, bass.ds(t, 1)], None, ALU.mult).then_inc(mean_ready, 1)
                for u in two:
                    t = i * 2 + u
                    dve.wait_ge(products, t + 1)
                    if not is_first(i):
                        dve.wait_ge(hidden_transposed, t - 1)
                    dve.tensor_tensor(hidden[u][:, :], hidden_ps[u][:, :], b1[:, :], ALU.add).then_inc(hidden_ready, 1)
                for u in two:
                    t = i * 2 + u
                    dve.wait_ge(out_products, t + 1)
                    if not is_first(i):
                        dve.wait_ge(x_ready, t - 1)
                    dve.tensor_tensor(out[u][:, :], out_ps[u][:, 0:D], b2[:, :], ALU.add).then_inc(out_ready, 1)
                for u in two:
                    t = i * 2 + u
                    x = mem.x[:, cols(t, D)]
                    dve.wait_ge(out_ready, t + 1)
                    dve.tensor_tensor(x, x, out[u][:, :], ALU.add).then_inc(x_ready, 1)
                for u in two:
                    t = i * 2 + u
                    dve.wait_ge(x_ready, t + 1)
                    dve.sem_inc(ph.turn, 1)
                    dve.bn_stats(halves[:, cols(t, 6)], mem.x[:, cols(t, D)])
            rounds(dve, PAIRS, tiles)


class Attention:

    def __init__(self, nc, ctx, n, heads):
        def sb(name, shape):
            return ctx.enter_context(nc.sbuf_tensor(f"att{n}_{name}", shape, F32))

        self.n, self.heads, self.part = n, heads, D // heads + 1
        self.width = heads * self.part
        self.src = sb("src", [P, BUCKETS * heads])
        self.dst = sb("dst", [P, BUCKETS * heads])
        self.top = sb("top", [P, BUCKETS * heads])
        self.least = sb("least", [P, heads])

    def by_head(self, ap):
        return ap.rearrange("p (h c) -> p h c", c=self.part)


def attention_tables(nc, mem, e, att, table, before=None):
    H, C = att.heads, D // att.heads
    W = att.width
    with Phase(nc, f"att_table{att.n}") as ph:
        sb, sem = ph.sb, ph.sem
        two = range(2)
        w_in, a_src, a_dst = sb("w_in", [P, 2, D]), sb("a_src", [P, D]), sb("a_dst", [P, D])
        w = sb("w", [P, 2, W + H])
        by_a = sb("by_a", [P, 4, D])
        h, turned = ([sb(f"{x}{u}", [P, D]) for u in two] for x in ("h", "turned"))
        row = [sb(f"row{u}", [P, W]) for u in two]
        least_t, least_h, diag = sb("least_t", [H, P]), sb("least_h", [H, 1]), sb("diag", [H, H])
        turned_ps, product_ps = ([ph.psum(f"{x}{u}", [P, 512]) for u in two] for x in ("turned_ps", "product_ps"))
        least_ps, wide_ps = ph.psum("least_ps", [P, 512]), ph.psum("wide_ps", [P, 512])
        (loaded, chain, w_ready, h_ready, transposed, turned_ready, products, row_ready, kept, least_ready,
         least_turned, diag_ready, wide_ready, own) = (
            sem(x) for x in ("loaded", "chain", "w_ready", "h_ready", "transposed", "turned_ready", "products",
                             "row_ready", "kept", "least_ready", "least_turned", "diag_ready", "wide_ready", "own"))
        stored = [sem(f"stored{u}") for u in two]
        if before is not None:
            bias = sb("bias", [P, D])
            v, neg, ex = ([sb(f"{x}{u}", [P, D]) for u in two] for x in ("v", "neg", "ex"))
            inv = [sb(f"inv{u}", [P, before.heads]) for u in two]
            inv_ready, scaled, v_ready, neg_ready, ex_ready, positive = (
                sem(x) for x in ("inv_ready", "scaled", "v_ready", "neg_ready", "ex_ready", "positive"))
        n_loaded = 3 + (before is not None)
        block = ph.block()

        @block.sync
        def _(sp):
            sp.dma_start(w_in[:, :, :], e["att_w"][:, att.n, :, :]).then_inc(loaded, 16)
            sp.dma_start(a_src[:, :], e["att_src"][att.n].partition_broadcast(P)).then_inc(loaded, 16)
            sp.dma_start(a_dst[:, :], e["att_dst"][att.n].partition_broadcast(P)).then_inc(loaded, 16)
            if before is not None:
                sp.dma_start(bias[:, :], e["att_b"][before.n].partition_broadcast(P)).then_inc(loaded, 16)
            with sp.Fori(0, PAIRS) as i:
                for u in two:
                    sp.wait_ge(row_ready, i * 2 + u + 1)
                    sp.sem_inc(ph.turn, 1)
                    sp.dma_start(table[bass.ds((i * 2 + u) * P, P), :], row[u][:, :]).then_inc(stored[u], 16)
            for u in two:
                sp.wait_ge(stored[u], 16 * PAIRS)

        @block.tensor
        def _(pe):
            pe.wait_ge(w_ready, 2)

            def tiles(i):
                for u in two:
                    t = i * 2 + u
                    pe.wait_ge(h_ready, t + 1)
                    if not is_first(i):
                        pe.wait_ge(turned_ready, t - 1)
                    for k in two:
                        ins = pe.transpose(turned_ps[u][:, cols(k, P)], h[u][:, cols(k, P)], mem.ident[:, :])
                    ins.then_inc(transposed, 1)
                for u in two:
                    t = i * 2 + u
                    pe.wait_ge(turned_ready, t + 1)
                    if not is_first(i):
                        pe.wait_ge(row_ready, t - 1)
                        pe.wait_ge(kept, (t - 1) * 3)
                    for k in two:
                        ins = pe.matmul(product_ps[u][:, 0:W + H], turned[u][:, cols(k, P)], w[:, k, :],
                                        start=(k == 0), stop=(k == 1))
                    ins.then_inc(products, 1)
            rounds(pe, PAIRS, tiles)
            pe.wait_ge(least_ready, 1)
            pe.transpose(least_ps[0:H, 0:P], att.least[:, :], mem.ident[:, :]).then_inc(least_turned, 1)
            pe.wait_ge(diag_ready, 1)
            pe.matmul(wide_ps[:, 0:H], mem.ones[0:H, :], diag[:, :], start=True, stop=True).then_inc(wide_ready, 1)

        @block.scalar
        def _(act):
            def tiles(i):
                for u in two:
                    t = i * 2 + u
                    if before is None:
                        if not is_first(i):
                            act.wait_ge(transposed, t - 1)
                            act.sem_inc(ph.turn, 1)
                        act.activation(h[u][:, :], mem.x[:, cols(t, D)], ACT.Relu, bias=mem.shift[:, bass.ds(t, 1)],
                                       scale=mem.rstd[:, bass.ds(t, 1)]).then_inc(h_ready, 1)
                    else:
                        act.wait_ge(neg_ready, t + 1)
                        act.activation(ex[u][:, :], neg[u][:, :], ACT.Exp).then_inc(ex_ready, 1)
                for u in two:
                    t = i * 2 + u
                    act.wait_ge(transposed, t + 1)
                    if not is_first(i):
                        act.wait_ge(products, t - 1)
                    act.copy(turned[u][:, :], turned_ps[u][:, 0:D]).then_inc(turned_ready, 1)
                for u in two:
                    t = i * 2 + u
                    act.wait_ge(products, t + 1)
                    if not is_first(i):
                        act.wait_ge(stored[u], i * 16)
                    act.copy(row[u][:, :], product_ps[u][:, 0:W]).then_inc(row_ready, 1)
            rounds(act, PAIRS, tiles)

        @block.vector
        def _(dve):
            dve.wait_ge(loaded, 16 * n_loaded)
            for k in two:
                dve.tensor_tensor(by_a[:, 2 * k, :], w_in[:, k, :], a_src[:, :], ALU.mult).then_inc(chain, 1)
                dve.tensor_tensor(by_a[:, 2 * k + 1, :], w_in[:, k, :], a_dst[:, :], ALU.mult).then_inc(chain, 1)
                dve.tensor_copy(att.by_head(w[:, k, 0:W])[:, :, 0:C],
                                w_in[:, k, :].rearrange("p (h c) -> p h c", c=C)).then_inc(chain, 1)
            dve.wait_ge(chain, 6)
            for k in two:
                dve.tensor_reduce(att.by_head(w[:, k, 0:W])[:, :, C],
                                  by_a[:, 2 * k, :].rearrange("p (h c) -> p h c", c=C), AX.X, ALU.add
                                  ).then_inc(chain, 1)
                dve.tensor_reduce(w[:, k, W:W + H], by_a[:, 2 * k + 1, :].rearrange("p (h c) -> p h c", c=C),
                                  AX.X, ALU.add).then_inc(w_ready, 1)
            dve.wait_ge(chain, 8)
            dve.wait_ge(w_ready, 2)

            def tiles(i):
                if before is not None:
                    CB = D // before.heads
                    for u in two:
                        t = i * 2 + u
                        sums = before.by_head(mem.acc[:, cols(t, ACCW, 0, before.width)])
                        if not is_first(i):
                            dve.wait_ge(scaled, t - 1)
                        dve.sem_inc(ph.turn, 1)
                        dve.reciprocal(inv[u][:, :], sums[:, :, CB]).then_inc(inv_ready, 1)
                    for u in two:
                        t = i * 2 + u
                        sums = before.by_head(mem.acc[:, cols(t, ACCW, 0, before.width)])
                        dve.wait_ge(inv_ready, t + 1)
                        if not is_first(i):
                            dve.wait_ge(h_ready, t - 1)
                        dve.tensor_tensor(v[u][:, :].rearrange("p (h c) -> p h c", c=CB), sums[:, :, 0:CB],
                                          inv[u][:, :].unsqueeze(2).broadcast_to([P, before.heads, CB]),
                                          ALU.mult).then_inc(scaled, 1)
                    for u in two:
                        t = i * 2 + u
                        dve.wait_ge(scaled, t + 1)
                        dve.tensor_tensor(v[u][:, :], v[u][:, :], bias[:, :], ALU.add).then_inc(v_ready, 1)
                    for u in two:
                        t = i * 2 + u
                        dve.wait_ge(v_ready, t + 1)
                        if not is_first(i):
                            dve.wait_ge(ex_ready, t - 1)
                        dve.tensor_scalar(neg[u][:, :], v[u][:, :], 0.0, None, ALU.min).then_inc(neg_ready, 1)
                    for u in two:
                        t = i * 2 + u
                        dve.wait_ge(ex_ready, t + 1)
                        dve.wait_ge(neg_ready, t + 1)
                        dve.tensor_scalar(v[u][:, :], v[u][:, :], 0.0, None, ALU.max).then_inc(positive, 1)
                    for u in two:
                        t = i * 2 + u
                        dve.wait_ge(positive, t + 1)
                        if not is_first(i):
                            dve.wait_ge(transposed, t - 1)
                        dve.scalar_tensor_tensor(h[u][:, :], ex[u][:, :], -1.0, v[u][:, :], ALU.add, ALU.add
                                                 ).then_inc(h_ready, 1)
                for u in two:
                    t = i * 2 + u
                    dve.wait_ge(row_ready, t + 1)
                    dve.tensor_scalar(mem.acc[:, cols(t, ACCW, 0, W)], product_ps[u][:, 0:W], 0.0, None, ALU.add
                                      ).then_inc(kept, 1)
                    dve.tensor_scalar(att.src[:, cols(t, H)], att.by_head(product_ps[u][:, 0:W])[:, :, C],
                                      0.0, None, ALU.add).then_inc(kept, 1)
                    dve.tensor_scalar(att.dst[:, cols(t, H)], product_ps[u][:, W:W + H], 0.0, None, ALU.add
                                      ).then_inc(kept, 1)
            rounds(dve, PAIRS, tiles)
            dve.wait_ge(kept, 3 * BUCKETS)
            acc = mem.acc[:, :].rearrange("p (t c) -> p t c", c=ACCW)
            for head in range(H):
                dve.memset(acc[:, :, head * (C + 1) + C], 1.0)
            dve.tensor_reduce(att.least[:, :], att.src[:, :].rearrange("p (t h) -> p h t", h=H), AX.X, ALU.min
                              ).then_inc(least_ready, 1)
            dve.wait_ge(least_turned, 1)
            dve.tensor_copy(least_t[:, :], least_ps[0:H, 0:P]).then_inc(own, 1)
            dve.wait_ge(own, 1)
            dve.tensor_reduce(least_h[:, :], least_t[:, :], AX.X, ALU.min).then_inc(own, 1)
            dve.wait_ge(own, 2)
            dve.tensor_scalar(diag[:, :], mem.ident[0:H, 0:H], least_h[:, :], None, ALU.mult).then_inc(diag_ready, 1)
            dve.wait_ge(wide_ready, 1)
            dve.tensor_copy(att.least[:, :], wide_ps[:, 0:H]).then_inc(own, 1)
            dve.wait_ge(own, 3)
            by_tile = [a[:, :].rearrange("p (t h) -> p t h", h=H) for a in (att.src, att.dst, att.top)]
            least = att.least[:, :].unsqueeze(1).broadcast_to([P, BUCKETS, H])
            dve.tensor_tensor(by_tile[0], by_tile[0], least, ALU.subtract).then_inc(own, 1)
            dve.tensor_tensor(by_tile[1], by_tile[1], least, ALU.add).then_inc(own, 1)
            dve.wait_ge(own, 5)
            dve.tensor_tensor(att.top[:, :], att.src[:, :], att.dst[:, :], ALU.add).then_inc(own, 1)
            dve.wait_ge(own, 6)
            dve.scalar_tensor_tensor(att.top[:, :], att.top[:, :], SLOPE, att.top[:, :], ALU.mult, ALU.max)


def attend(nc, mem, att, table):
    H, C, W = att.heads, D // att.heads, att.width
    n_rounds = NT // RING
    n_groups = NT // GROUP
    with Phase(nc, f"attend{att.n}") as ph:
        sb, sem = ph.sb, ph.sem
        rows = sb("rows", [P, RING, W])
        which = sb("which", [P, RING], I32)
        onehot = sb("onehot", [P, RING, P])
        src = sb("src", [P, 4, GROUP, H])
        spread = sb("spread", [P, GROUP, H * P])
        hot_t = sb("hot_t", [P, 2, GROUP, P])
        best = sb("best", [P, 2, GROUP, H])
        cand, leaky = sb("cand", [P, GROUP, H]), sb("leaky", [P, GROUP, H])
        pair = sb("pair", [P, 2, GROUP, 2 * H])
        drop, factor = sb("drop", [P, GROUP, H]), sb("factor", [P, 4, GROUP, H])
        score, low, gap = (sb(x, [P, GROUP, H]) for x in ("score", "low", "gap"))
        score_ps = [ph.psum(f"score_ps{k}", [P, 512]) for k in range(2)]
        turn_ps, edge_ps = ph.psum("turn_ps", [P, 512]), ph.psum("edge_ps", [P, 512])
        sums_ps = [ph.psum(f"sums_ps{k}", [P, 512]) for k in range(GROUP)]
        staged = [sem(f"staged{g}") for g in range(GROUPS)]
        landed = [sem(f"landed{g}") for g in range(GROUPS)]
        (onehots, src_ready, spreads, spread_done, turned, hot_t_ready, best_ready, dst_ready, cand_ready, leaky_ready,
         topped, kept, dropped, factors, edge_done, score_ready, low_ready, gap_ready, gap_cut, weights, weighted,
         products, added) = (
            sem(x) for x in ("onehots", "src_ready", "spreads", "spread_done", "turned", "hot_t_ready",
                             "best_ready", "dst_ready", "cand_ready", "leaky_ready", "topped", "kept", "dropped",
                             "factors", "edge_done", "score_ready", "low_ready", "gap_ready", "gap_cut", "weights",
                             "weighted", "products", "added"))
        block = ph.block()

        class Group:

            def __init__(self, i, g):
                self.i, self.g = (i, g) if g >= 0 else (i - 1, g + GROUPS)
                if self.g >= GROUPS:
                    self.i, self.g = i + 1, self.g - GROUPS
                self.q = self.i * GROUPS + self.g
                self.t = self.i * RING + self.g * GROUP
                self.exists = not isinstance(self.q, int) or 0 <= self.q < n_groups

            def after(self, n):
                return not isinstance(self.q, int) or self.q >= n

        def att_rows(n):
            return rows[:, cols(n.g, GROUP), :].rearrange("p k (h c) -> p k h c", c=C + 1)

        def over_groups(engine, step):
            def one_round(i):
                for g in range(GROUPS):
                    step(i, g)
            one_round(0)
            with engine.Fori(1, n_rounds - 1) as i:
                one_round(i)
            one_round(n_rounds - 1)

        @block.sync
        def _(sp):
            def stage(i):
                for g in range(GROUPS):
                    if not is_first(i):
                        sp.wait_ge(landed[g], i * (16 * GROUP))
                        sp.sem_inc(ph.turn, 1)
                    sp.dma_start(which[:, cols(g, GROUP)], mem.slot_src[:, cols(i, RING, g * GROUP, GROUP)]
                                 ).then_inc(staged[g], 16)
            rounds(sp, n_rounds, stage)

        @block.gpsimd
        def _(pool):
            def gather(i):
                for g in range(GROUPS):
                    pool.wait_ge(staged[g], (i + 1) * 16)
                    if not is_first(i):
                        pool.wait_ge(products, (i - 1) * RING + (g + 1) * GROUP)
                        pool.sem_inc(ph.turn, 1)
                    for k in range(g * GROUP, (g + 1) * GROUP):
                        pool.indirect_dma_start(rows[:, k, :], None, table,
                                                bass.IndirectOffsetOnAxis(which[:, k:k + 1], 0)
                                                ).then_inc(landed[g], 16)
            rounds(pool, n_rounds, gather)

        @block.scalar
        def _(act):
            def spread_of(n):
                act.wait_ge(src_ready, n.q + 1)
                if n.after(1):
                    act.wait_ge(spread_done, n.t)
                for k in range(GROUP):
                    for head in range(H):
                        ins = act.activation(spread[:, k, cols(head, P)], mem.ident[:, :], ACT.Copy,
                                             scale=src[:, n.g, k, head:head + 1])
                    ins.then_inc(spreads, 1)

            def turned_of(n):
                act.wait_ge(turned, n.t + GROUP)
                if n.after(2):
                    act.wait_ge(edge_done, n.q - 1)
                act.copy(hot_t[:, n.g % 2, :, :].rearrange("p k e -> p (k e)"), turn_ps[:, :]).then_inc(hot_t_ready, 1)

            def factors_of(n):
                act.wait_ge(dropped, n.t + GROUP)
                if n.after(4):
                    act.wait_ge(added, n.t - 3 * GROUP)
                act.activation(factor[:, n.g, :, :], drop[:, :, :], ACT.Exp).then_inc(factors, 1)

            def weights_of(n):
                act.wait_ge(gap_cut, n.q + 1)
                act.activation(att_rows(n)[:, :, :, C], gap[:, :, :], ACT.Exp).then_inc(weights, 1)

            def step(i, g):
                now, following = Group(i, g), Group(i, g + 1)
                if following.exists:
                    spread_of(following)
                factors_of(now)
                weights_of(now)
                if following.exists:
                    turned_of(following)
            spread_of(Group(0, 0))
            turned_of(Group(0, 0))
            over_groups(act, step)

        @block.tensor
        def _(pe):
            def scores_of(n):
                for k in range(GROUP):
                    pe.wait_ge(onehots, n.t + k + 1)
                    if k == 0 and n.after(1):
                        pe.wait_ge(hot_t_ready, n.q)
                    pe.transpose(turn_ps[:, cols(k, P)], onehot[:, n.g * GROUP + k, :], mem.ident[:, :]
                                 ).then_inc(turned, 1)
                for k in range(GROUP):
                    pe.wait_ge(spreads, n.t + k + 1)
                    if n.after(1) or k >= 2:
                        pe.wait_ge(best_ready, n.t + k - 1)
                    pe.matmul(score_ps[k % 2][:, 0:H * P], onehot[:, n.g * GROUP + k, :], spread[:, k, :],
                              start=True, stop=True).then_inc(spread_done, 1)

            def edges_of(n):
                pe.wait_ge(hot_t_ready, n.q + 1)
                if n.after(1):
                    pe.wait_ge(gap_ready, n.q)
                for k in range(GROUP):
                    pe.wait_ge(kept, n.t + k + 1)
                    ins = pe.matmul(edge_ps[:, cols(k, 2 * H)], hot_t[:, n.g % 2, k, :], pair[:, n.g % 2, k, :],
                                    start=True, stop=True)
                ins.then_inc(edge_done, 1)

            def sums_of(n):
                for k in range(GROUP):
                    pe.wait_ge(weighted, n.t + k + 1)
                    if n.after(1):
                        pe.wait_ge(added, n.t + k - GROUP + 1)
                    pe.matmul(sums_ps[k][:, 0:W], onehot[:, n.g * GROUP + k, :], rows[:, n.g * GROUP + k, :],
                              start=True, stop=True).then_inc(products, 1)

            def step(i, g):
                edges_of(Group(i, g))
                if Group(i, g - 1).exists:
                    sums_of(Group(i, g - 1))
                if Group(i, g + 1).exists:
                    scores_of(Group(i, g + 1))
            scores_of(Group(0, 0))
            over_groups(pe, step)
            sums_of(Group(n_rounds - 1, GROUPS - 1))

        @block.vector
        def _(dve):
            def tile_state(n, k):
                tile = dve.value_load(mem.tile_of_dst[0:1, bass.ds(n.t + k, 1)], min_val=0, max_val=BUCKETS - 1)
                return tile

            def slots_of(n):
                for k in range(GROUP):
                    dve.tensor_scalar(onehot[:, n.g * GROUP + k, :], mem.iota[:, :], mem.slot_node[:, bass.ds(n.t + k, 1)],
                                      None, ALU.is_equal).then_inc(onehots, 1)
                dve.wait_ge(landed[n.g], (n.i + 1) * (16 * GROUP))
                dve.tensor_tensor(src[:, n.g, :, :], att_rows(n)[:, :, :, C],
                                  att.least[:, :].unsqueeze(1).broadcast_to([P, GROUP, H]), ALU.subtract
                                  ).then_inc(src_ready, 1)

            def maxima_of(n):
                h2 = n.g % 2
                for k in range(GROUP):
                    dve.wait_ge(spread_done, n.t + k + 1)
                    dve.tensor_reduce(best[:, h2, k, :], score_ps[k % 2][:, 0:H * P].rearrange("p (h e) -> p h e", e=P),
                                      AX.X, ALU.max).then_inc(best_ready, 1)
                tiles = [tile_state(n, k) for k in range(GROUP)]
                if n.after(2):
                    dve.wait_ge(edge_done, n.q - 1)
                for k in range(GROUP):
                    dve.tensor_scalar(pair[:, h2, k, 0:H], att.dst[:, cols(tiles[k], H)], 0.0, None, ALU.add
                                      ).then_inc(dst_ready, 1)
                dve.wait_ge(best_ready, n.t + GROUP)
                dve.wait_ge(dst_ready, n.t + GROUP)
                dve.tensor_tensor(cand[:, :, :], best[:, h2, :, :], pair[:, h2, :, 0:H], ALU.add).then_inc(cand_ready, 1)
                dve.wait_ge(cand_ready, n.q + 1)
                dve.scalar_tensor_tensor(leaky[:, :, :], cand[:, :, :], SLOPE, cand[:, :, :], ALU.mult, ALU.max
                                         ).then_inc(leaky_ready, 1)
                dve.wait_ge(leaky_ready, n.q + 1)
                for k in range(GROUP):
                    top = att.top[:, cols(tiles[k], H)]
                    if n.after(1) or k:
                        dve.wait_ge(kept, n.t + k)
                    dve.tensor_tensor(pair[:, h2, k, H:2 * H], leaky[:, k, :], top, ALU.max).then_inc(topped, 1)
                    if n.after(1) and k == 0:
                        dve.wait_ge(factors, n.q)
                    dve.wait_ge(topped, n.t + k + 1)
                    dve.tensor_tensor(drop[:, k, :], top, pair[:, h2, k, H:2 * H], ALU.subtract).then_inc(dropped, 1)
                    dve.wait_ge(dropped, n.t + k + 1)
                    dve.tensor_scalar(top, pair[:, h2, k, H:2 * H], 0.0, None, ALU.add).then_inc(kept, 1)

            def gaps_of(n):
                edge = edge_ps[:, 0:GROUP * 2 * H].rearrange("p (k c) -> p k c", k=GROUP)
                dve.wait_ge(edge_done, n.q + 1)
                dve.tensor_tensor(score[:, :, :], src[:, n.g, :, :], edge[:, :, 0:H], ALU.add).then_inc(score_ready, 1)
                dve.wait_ge(score_ready, n.q + 1)
                dve.scalar_tensor_tensor(low[:, :, :], score[:, :, :], SLOPE, score[:, :, :], ALU.mult, ALU.max
                                         ).then_inc(low_ready, 1)
                dve.wait_ge(low_ready, n.q + 1)
                if n.after(1):
                    dve.wait_ge(weights, n.q)
                dve.tensor_tensor(gap[:, :, :], low[:, :, :], edge[:, :, H:2 * H], ALU.subtract).then_inc(gap_ready, 1)
                dve.wait_ge(gap_ready, n.q + 1)
                dve.tensor_scalar(gap[:, :, :], gap[:, :, :], 0.0, None, ALU.min).then_inc(gap_cut, 1)

            def weigh(n):
                dve.wait_ge(weights, n.q + 1)
                for k in range(GROUP):
                    row = att_rows(n)[:, k, :, :]
                    dve.tensor_tensor(row[:, :, 0:C], row[:, :, 0:C], row[:, :, C:C + 1].broadcast_to([P, H, C]),
                                      ALU.mult).then_inc(weighted, 1)

            def sum_up(n):
                tiles = [tile_state(n, k) for k in range(GROUP)]
                dve.wait_ge(factors, n.q + 1)
                for k in range(GROUP):
                    dve.wait_ge(products, n.t + k + 1)
                    if n.after(1) or k:
                        dve.wait_ge(added, n.t + k)
                    for head in range(H):
                        into = mem.acc[:, cols(tiles[k], ACCW, head * (C + 1), C + 1)]
                        ins = dve.scalar_tensor_tensor(into, into, factor[:, n.g, k, head:head + 1],
                                                       sums_ps[k][:, cols(head, C + 1)], ALU.mult, ALU.add)
                    ins.then_inc(added, 1)

            def step(i, g):
                if Group(i, g + 1).exists:
                    slots_of(Group(i, g + 1))
                maxima_of(Group(i, g))
                if Group(i, g - 1).exists:
                    weigh(Group(i, g - 1))
                gaps_of(Group(i, g))
                if Group(i, g - 2).exists:
                    sum_up(Group(i, g - 2))
            slots_of(Group(0, 0))
            over_groups(dve, step)
            last = Group(n_rounds - 1, GROUPS - 1)
            weigh(last)
            sum_up(Group(n_rounds - 1, GROUPS - 2))
            sum_up(last)


def finish(nc, mem, e, att, out):
    with Phase(nc, "finish") as ph:
        bias, inv = ph.sb("bias", [P, D]), ph.sb("inv", [P, BUCKETS])
        v = [ph.sb(f"v{u}", [P, D]) for u in range(2)]
        loaded, inv_ready, scaled, biased, ready = (ph.sem(x) for x in ("loaded", "inv_ready", "scaled", "biased", "ready"))
        stored = [ph.sem(f"stored{u}") for u in range(2)]
        block = ph.block()

        @block.sync
        def _(sp):
            sp.dma_start(bias[:, :], e["att_b"][att.n].partition_broadcast(P)).then_inc(loaded, 16)
            with sp.Fori(0, PAIRS) as i:
                for u in range(2):
                    t = i * 2 + u
                    sp.wait_ge(ready, t + 1)
                    sp.sem_inc(ph.turn, 1)
                    sp.dma_start(out[bass.ds(t * P, P), :], v[u][:, :]).then_inc(stored[u], 16)
            for u in range(2):
                sp.wait_ge(stored[u], 16 * PAIRS)

        @block.vector
        def _(dve):
            dve.wait_ge(loaded, 16)
            dve.reciprocal(inv[:, :], mem.acc[:, :].rearrange("p (t c) -> p t c", c=ACCW)[:, :, D]).then_inc(inv_ready, 1)
            dve.wait_ge(inv_ready, 1)

            def tiles(i):
                for u in range(2):
                    t = i * 2 + u
                    if not is_first(i):
                        dve.wait_ge(stored[u], i * 16)
                    dve.tensor_scalar(v[u][:, :], mem.acc[:, cols(t, ACCW, 0, D)], inv[:, bass.ds(t, 1)], None,
                                      ALU.mult).then_inc(scaled, 1)
                for u in range(2):
                    t = i * 2 + u
                    dve.wait_ge(scaled, t + 1)
                    dve.tensor_tensor(v[u][:, :], v[u][:, :], bias[:, :], ALU.add).then_inc(biased, 1)
                for u in range(2):
                    t = i * 2 + u
                    dve.wait_ge(biased, t + 1)
                    dve.tensor_tensor(v[u][:, :], v[u][:, :], mem.x[:, cols(t, D)], ALU.add).then_inc(ready, 1)
            rounds(dve, PAIRS, tiles)


def build(nc, e, out):
    def dram(name, shape, dt=F32):
        return nc.dram_tensor(name, shape, dt).ap()

    slots, edge_rows = dram("slots", (SLOTS, 4), I32), dram("edge_rows", (SLOTS, ECOLS))
    rel_table, table = dram("rel_table", (NPAD * REL, D)), dram("table", (NPAD, D))
    with ExitStack() as ctx:
        mem = Mem(nc, ctx)
        constants(nc, mem)
        load_nodes(nc, mem, e)
        build_slots(nc, mem, e, {"slots": slots})
        with ExitStack() as inner:
            halves = inner.enter_context(nc.sbuf_tensor("halves", [P, BUCKETS * 6], F32))
            first_stats(nc, mem, halves)
            finish_stats(nc, mem, "stats0", halves)
            for layer in range(3):
                relational_tables(nc, mem, e, layer, rel_table)
                aggregate(nc, mem, f"rel_sum{layer}", rel_table, mem.slot_rel, degree=(layer == 0))
            relational_end(nc, mem, halves)
            finish_stats(nc, mem, "stats1", halves)
            node_table(nc, mem, table)
            sort_edge_rows(nc, mem, e, {"edge_rows": edge_rows})
            aggregate(nc, mem, "mean_sum", table, mem.slot_src, weighted=True, edge_rows=edge_rows)
            conv_layers(nc, mem, e, table)
            mlp_layer(nc, mem, e, 0, halves)
            mlp_layer(nc, mem, e, 1, halves)
            finish_stats(nc, mem, "stats2", halves)
            edge_layer(nc, mem, e, halves)
            finish_stats(nc, mem, "stats3", halves)
        before = None
        for n, heads in enumerate((HEADS, 1)):
            att = Attention(nc, ctx, n, heads)
            att_table = dram(f"att_table{n}", (NPAD, att.width))
            attention_tables(nc, mem, e, att, att_table, before)
            attend(nc, mem, att, att_table)
            before = att
        finish(nc, mem, e, before, out)


def lay_out(inputs):
    def f32(name):
        return np.ascontiguousarray(inputs[name])

    def edges(name, fill):
        a = np.asarray(inputs[name])
        out = np.full((EPAD,) + a.shape[1:], fill, a.dtype)
        out[:N_EDGES] = a
        return out.reshape((P, COLS) + a.shape[1:])

    def split_rows(w):
        w = np.asarray(w)
        w = w.reshape(w.shape[:-2] + (w.shape[-2] // P, P, w.shape[-1]))
        return np.ascontiguousarray(np.moveaxis(w, -2, 0))

    x = np.zeros((NPAD, D), np.float32)
    x[:N_NODES] = inputs["x"]
    rel = np.concatenate([np.moveaxis(np.asarray(inputs["L0_gnn_weights"]), 1, 2).reshape(3, D, REL * D),
                          np.asarray(inputs["L0_gnn_roots"])], axis=2)
    conv = np.stack([np.moveaxis(np.asarray(inputs[n]), (0, 1, 2), (1, 2, 0)).reshape(D, 4 * D)
                     for n in ("L1_gnn_W_rel", "L1_gnn_W_root")])
    w = {
        "x": x,
        "src": edges("src", REAL * P), "dst": edges("dst", REAL * P), "rel": edges("edge_type_8", 0),
        "weight": edges("edge_weight", 0), "attr": edges("edge_attr_64", 0),
        "rel_w": split_rows(rel),
        "rel_b": f32("L0_gnn_biases"),
        "conv_w": split_rows(conv),
        "conv_b": f32("L1_gnn_b_rel").reshape(1, -1), "conv_g": f32("L1_gnn_ln_g").reshape(1, -1),
        "conv_n": f32("L1_gnn_ln_b").reshape(1, -1),
        "mlp_w": split_rows(np.stack([np.asarray(inputs["L1_gnn_W1"]).T, np.asarray(inputs["L1_gnn_W2"]).T])),
        "mlp_v": np.stack([np.asarray(inputs["L1_gnn_" + n]) for n in ("b1", "mg1", "mb1", "b2", "mg2", "mb2")]),
        "edge_w": split_rows(np.asarray(inputs["L2_gnn_W1"])[:D]),
        "edge_we": np.ascontiguousarray(np.asarray(inputs["L2_gnn_W1"])[D:D + EDGE_D]),
        "edge_wu": np.ascontiguousarray(np.asarray(inputs["L2_gnn_W1"])[D + EDGE_D:]),
        "edge_u": np.ascontiguousarray(np.asarray(inputs["L2_gnn_u"])[0:1].T),
        "edge_b1": f32("L2_gnn_b1").reshape(1, -1),
        "edge_w2": split_rows(inputs["L2_gnn_W2"]), "edge_b2": f32("L2_gnn_b2").reshape(1, -1),
        "att_w": split_rows(np.stack([np.asarray(inputs["L3_gnn_W1"]), np.asarray(inputs["L3_gnn_W2"])])),
        "att_src": np.stack([np.asarray(inputs[f"L3_gnn_a_src{n}"]).reshape(-1) for n in (1, 2)]),
        "att_dst": np.stack([np.asarray(inputs[f"L3_gnn_a_dst{n}"]).reshape(-1) for n in (1, 2)]),
        "att_b": np.stack([np.asarray(inputs[f"L3_gnn_b{n}"]) for n in (1, 2)]),
    }
    return w


def kernel(**inputs):
    import concourse.bacc as bacc
    from concourse.bass_utils import run_bass_kernel_spmd

    nc = bacc.Bacc("TRN2", target_bir_lowering=False, num_devices=1)
    arrays = lay_out(inputs)
    args = {n: nc.dram_tensor(f"in_{n}", a.shape, mybir.dt.from_np(a.dtype), kind="ExternalInput").ap()
            for n, a in arrays.items()}
    out = nc.dram_tensor("out", (NPAD, D), F32, kind="ExternalOutput").ap()
    build(nc, args, out)
    result = run_bass_kernel_spmd(nc, [{f"in_{n}": a for n, a in arrays.items()}], core_ids=[0])
    return result.results[0]["out"][:N_NODES]
```

```python
from contextlib import ExitStack

import numpy as np
import concourse.bass as bass
from concourse import mybir

ALU = mybir.AluOpType
ACT = mybir.ActivationFunctionType
AX = mybir.AxisListType
F32 = mybir.dt.float32
I32 = mybir.dt.int32

P = 128
N_NODES = 6250
N_EDGES = 100000
D = 256
REL = 8
EDGE_D = 64
HEADS = 4
EPS = 1e-5
SLOPE = 0.2

BUCKETS = 50
NPAD = BUCKETS * P
GROUP = 4
GROUPS = 4
RING = GROUP * GROUPS
COLS = -(-(-(-N_EDGES // P)) // RING) * RING
EPAD = COLS * P
REAL = -(-N_NODES // P)
NT = -(-((N_EDGES - REAL) // P + REAL + (EPAD - N_EDGES) // P) // RING) * RING
SLOTS = NT * P
ACCW = 260
ECOLS = EDGE_D + 1
NO_NODE = 255.0


def cols(t, width, lo=0, n=None):
    return bass.ds(t * width + lo, width if n is None else n)


def tiles_of(nc, dve, tile_of, t, n):
    _, values = nc.values_load_multi_w_load_instructions(
        tile_of[0:1, bass.ds(t, n)], engines=(dve.engine,), min_val=0, max_val=BUCKETS - 1)
    return values


def rounds(engine, n, body):
    body(0)
    with engine.Fori(1, n) as i:
        body(i)


def is_first(i):
    return isinstance(i, int) and i == 0


class Phase:

    def __init__(self, nc, name):
        self.nc, self.name, self.ctx, self.sems = nc, name, ExitStack(), []

    def __enter__(self):
        self.turn = self.sem("turn")
        return self

    def __exit__(self, kind, *rest):
        self.ctx.close()
        if kind is None and self.sems:
            self.nc.clear_and_free_semaphores(self.sems)
            self.nc.all_engine_barrier()

    def sb(self, name, shape, dt=F32):
        return self.ctx.enter_context(self.nc.sbuf_tensor(f"{self.name}_{name}", shape, dt))

    def psum(self, name, shape):
        return self.ctx.enter_context(self.nc.psum_tensor(f"{self.name}_{name}", shape, F32))

    def sem(self, name):
        self.sems.append(self.nc.alloc_semaphore(f"{self.name}_{name}"))
        return self.sems[-1]

    def block(self):
        return self.ctx.enter_context(self.nc.Block())


class Mem:

    def __init__(self, nc, ctx):
        def sb(name, shape, dt=F32):
            return ctx.enter_context(nc.sbuf_tensor(name, shape, dt))

        self.x = sb("x_nodes", [P, BUCKETS * D])
        self.acc = sb("acc", [P, BUCKETS * ACCW])
        self.edge_acc = sb("edge_acc", [P, BUCKETS * ECOLS])
        self.slot_rel = sb("slot_rel", [P, NT], I32)
        self.slot_src = sb("slot_src", [P, NT], I32)
        self.slot_weight = sb("slot_weight", [P, NT])
        self.slot_node = sb("slot_node", [P, NT + 2 * GROUP])
        self.tile_of_dst = sb("tile_of_dst", [1, NT], I32)
        self.tile_of_src = sb("tile_of_src", [1, NT], I32)
        self.iota = sb("iota_row", [P, P])
        self.ident = sb("ident", [P, P])
        self.ones = sb("ones", [P, P])
        self.mean_var = sb("mean_var", [P, BUCKETS * 2])
        self.rstd = sb("rstd", [P, BUCKETS])
        self.shift = sb("shift", [P, BUCKETS])
        self.inv_deg = sb("inv_deg", [P, BUCKETS])
        self.eps = sb("eps", [P, 1])


def sort_by_tile(nc, mem, name, key_dram, addr, loc, tile_of):
    with Phase(nc, name) as ph:
        sb, sem = ph.sb, ph.sem
        key, bucket_i = sb("key", [P, COLS], I32), sb("bucket_i", [P, COLS], I32)
        bucket, running, place = sb("bucket", [P, COLS]), sb("running", [P, COLS]), sb("place", [P, COLS])
        mask = sb("mask", [P, COLS], I32)
        count, tiles, ends, seed, zero = (sb(n, [P, BUCKETS]) for n in ("count", "tiles", "ends", "seed", "zero"))
        total_i, number, before = sb("total_i", [P, BUCKETS], I32), sb("number", [P, BUCKETS]), sb("before", [P, P])
        end_col, junk = sb("end_col", [P, 1]), sb("junk", [P, BUCKETS])
        tile_no, past = sb("tile_no", [REAL, NT]), sb("past", [REAL, NT])
        offset_ps = ph.psum("offset_ps", [P, BUCKETS])
        total_ps = ph.psum("total_ps", [P, BUCKETS])
        tile_ps = [ph.psum(f"tile_ps{h}", [1, NT // 2]) for h in range(2)]
        loaded, consts, chain, counted, offsets, past_ready, tiles_ready = (
            sem(n) for n in ("loaded", "consts", "chain", "counted", "offsets", "past_ready", "tiles_ready"))
        block = ph.block()

        @block.sync
        def _(sp):
            sp.dma_start(key[:, :], key_dram).then_inc(loaded, 16)

        @block.gpsimd
        def _(pool):
            pool.iota(number[:, :], [[1, BUCKETS]], base=0, channel_multiplier=0,
                      allow_small_or_imprecise_dtypes=True).then_inc(consts, 1)
            pool.iota(tile_no[:, :], [[1, NT]], base=0, channel_multiplier=0,
                      allow_small_or_imprecise_dtypes=True).then_inc(consts, 1)
            pool.memset(zero[:, :], 0.0).then_inc(consts, 1)
            pool.memset(before[:, :], 1.0).then_inc(consts, 1)
            pool.wait_ge(consts, 4)
            pool.affine_select(out=before[:, :], in_=before[:, :], compare_op=ALU.is_gt, fill=0.0,
                               base=0, pattern=[[1, P]], channel_multiplier=-1).then_inc(consts, 1)

        @block.tensor
        def _(pe):
            pe.wait_ge(consts, 5)
            pe.wait_ge(counted, BUCKETS)
            pe.matmul(offset_ps[:, :], before[:, :], count[:, :], start=True, stop=True).then_inc(offsets, 1)
            pe.matmul(total_ps[:, :], mem.ones[:, :], count[:, :], start=True, stop=True).then_inc(offsets, 1)
            pe.wait_ge(past_ready, 1)
            for h in range(2):
                pe.matmul(tile_ps[h][:, :], mem.ones[0:REAL, 0:1], past[:, cols(h, NT // 2)],
                          start=True, stop=True).then_inc(tiles_ready, 1)

        @block.vector
        def _(dve):
            steps = [0]

            def link(ins):
                steps[0] += 1
                ins.then_inc(chain, 1)
                dve.wait_ge(chain, steps[0])

            dve.wait_ge(loaded, 16)
            dve.wait_ge(consts, 5)
            link(dve.tensor_scalar(bucket_i[:, :], key[:, :], 7, None, ALU.logical_shift_right))
            link(dve.tensor_copy(bucket[:, :], bucket_i[:, :]))
            link(dve.tensor_scalar(mask[:, :], key[:, :], P - 1, None, ALU.bitwise_and))
            link(dve.tensor_copy(loc, mask[:, :]))
            with dve.Fori(0, BUCKETS) as b:
                dve.tensor_scalar(running[:, :], bucket[:, :], number[:, bass.ds(b, 1)], None, ALU.is_equal, ALU.add,
                                  accum_out=count[:, bass.ds(b, 1)]).then_inc(counted, 1)
                dve.wait_ge(counted, b + 1)
            dve.wait_ge(offsets, 2)
            link(dve.tensor_scalar(total_i[:, :], total_ps[:, :], float(P - 1), None, ALU.add))
            link(dve.tensor_scalar(total_i[:, :], total_i[:, :], 7, None, ALU.logical_shift_right))
            link(dve.tensor_copy(tiles[:, :], total_i[:, :]))
            link(dve.tensor_tensor_scan(ends[:, :], tiles[:, :], zero[:, :], 0.0, ALU.add, ALU.add))
            link(dve.tensor_tensor(seed[:, :], ends[:, :], tiles[:, :], ALU.subtract))
            link(dve.tensor_scalar(seed[:, :], seed[:, :], float(P), -1.0, ALU.mult, ALU.add))
            link(dve.tensor_tensor(seed[:, :], seed[:, :], offset_ps[:, :], ALU.add))
            link(dve.tensor_tensor_reduce(junk[:, :], ends[:, :], mem.ident[:, 0:BUCKETS], 1.0, 0.0,
                                          ALU.mult, ALU.add, end_col[:, :]))
            dve.tensor_scalar(past[:, :], tile_no[:, :], end_col[0:REAL, :], None, ALU.is_ge).then_inc(past_ready, 1)
            for h in range(2):
                dve.wait_ge(tiles_ready, h + 1)
                link(dve.tensor_copy(tile_of[:, cols(h, NT // 2)], tile_ps[h][:, :]))
            link(dve.memset(place[:, :], 0.0))
            at = steps[0]
            with dve.Fori(0, BUCKETS) as b:
                dve.tensor_scalar(mask[:, :], bucket[:, :], number[:, bass.ds(b, 1)], None,
                                  ALU.is_equal).then_inc(chain, 1)
                dve.wait_ge(chain, b * 4 + at + 1)
                dve.tensor_tensor_scan(running[:, :], mask[:, :], bucket[:, :], seed[:, bass.ds(b, 1)],
                                       ALU.add, ALU.bypass).then_inc(chain, 1)
                dve.wait_ge(chain, b * 4 + at + 2)
                dve.tensor_tensor(running[:, :], running[:, :], mask[:, :], ALU.mult).then_inc(chain, 1)
                dve.wait_ge(chain, b * 4 + at + 3)
                dve.tensor_tensor(place[:, :], place[:, :], running[:, :], ALU.add).then_inc(chain, 1)
                dve.wait_ge(chain, b * 4 + at + 4)
            steps[0] += 4 * BUCKETS
            link(dve.tensor_copy(bucket_i[:, :], place[:, :]))
            link(dve.tensor_scalar(mask[:, :], bucket_i[:, :], P - 1, None, ALU.bitwise_and))
            link(dve.tensor_scalar(bucket_i[:, :], bucket_i[:, :], 7, None, ALU.logical_shift_right))
            link(dve.scalar_tensor_tensor(addr, mask[:, :], float(NT), bucket_i[:, :], ALU.mult, ALU.add))


def constants(nc, mem):
    with Phase(nc, "consts") as ph:
        made = ph.sem("made")
        block = ph.block()

        @block.gpsimd
        def _(pool):
            pool.iota(mem.iota[:, :], [[1, P]], base=0, channel_multiplier=0,
                      allow_small_or_imprecise_dtypes=True).then_inc(made, 1)
            pool.memset(mem.ident[:, :], 0.0).then_inc(made, 1)
            pool.memset(mem.eps[:, :], EPS).then_inc(made, 1)
            pool.wait_ge(made, 3)
            pool.affine_select(out=mem.ident[:, :], in_=mem.ident[:, :], compare_op=ALU.not_equal, fill=1.0,
                               base=0, pattern=[[-1, P]], channel_multiplier=1).then_inc(made, 1)

        @block.vector
        def _(dve):
            dve.memset(mem.ones[:, :], 1.0)
            dve.memset(mem.acc[:, :], 0.0)
            dve.memset(mem.edge_acc[:, :], 0.0)
            dve.memset(mem.slot_node[:, NT:NT + 2 * GROUP], NO_NODE)


def scatter(nc, name, addr, table, pieces, labels=None, mem_ones=None):
    width = table.shape[1]
    with Phase(nc, name) as ph:
        sem = ph.sem
        rows = ph.sb("rows", [P, RING, width], table.dtype)
        where = ph.sb("where", [P, RING], I32)
        staged = [sem(f"staged{g}") for g in range(GROUPS)]
        written = [sem(f"written{g}") for g in range(GROUPS)]
        labelled, counts = sem("labelled"), sem("counts")
        n_staged = 1 + len(pieces(None, 0, GROUP, rows, 0))
        block = ph.block()

        @block.sync
        def _(sp):
            def stage(i):
                for g in range(GROUPS):
                    if not is_first(i):
                        sp.wait_ge(written[g], i * (16 * GROUP))
                        sp.sem_inc(ph.turn, 1)
                    sp.dma_start(where[:, cols(g, GROUP)], addr[:, cols(i, RING, g * GROUP, GROUP)]
                                 ).then_inc(staged[g], 16)
                    for load in pieces(sp, i * RING + g * GROUP, GROUP, rows, g * GROUP):
                        load().then_inc(staged[g], 16)
            rounds(sp, COLS // RING, stage)

        @block.scalar
        def _(act):
            def label(i):
                for g in range(GROUPS):
                    if not is_first(i):
                        act.wait_ge(written[g], i * (16 * GROUP))
                        act.sem_inc(ph.turn, 1)
                    act.copy(rows[:, cols(g, GROUP), 0], labels[:, cols(i, RING, g * GROUP, GROUP)]
                             ).then_inc(labelled, 1)
            if labels is not None:
                act.copy(rows[:, :, width - 1], mem_ones[:, 0:RING]).then_inc(counts, 1)
                rounds(act, COLS // RING, label)

        @block.gpsimd
        def _(pool):
            if labels is not None:
                pool.wait_ge(counts, 1)
            with pool.Fori(0, COLS // RING) as i:
                for g in range(GROUPS):
                    pool.wait_ge(staged[g], (i + 1) * (16 * n_staged))
                    if labels is not None:
                        pool.wait_ge(labelled, i * GROUPS + g + 1)
                    pool.sem_inc(ph.turn, 1)
                    for k in range(g * GROUP, (g + 1) * GROUP):
                        pool.indirect_dma_start(table, bass.IndirectOffsetOnAxis(where[:, k:k + 1], 0),
                                                rows[:, k, :], None).then_inc(written[g], 16)
            for g in range(GROUPS):
                pool.wait_ge(written[g], COLS // RING * GROUP * 16)


def build_slots(nc, mem, e, scratch):
    with ExitStack() as ctx:
        addr = ctx.enter_context(nc.sbuf_tensor("dst_addr", [P, COLS], I32))
        info = ctx.enter_context(nc.sbuf_tensor("info", [P, COLS, 4], I32))
        sort_by_tile(nc, mem, "dst", e["dst"], addr[:, :], info[:, :, 3].bitcast(F32), mem.tile_of_dst)
        with Phase(nc, "pack") as ph:
            src, rel = ph.sb("src", [P, COLS], I32), ph.sb("rel", [P, COLS], I32)
            weight = ph.sb("weight", [P, COLS])
            empty = ph.sb("empty", [P, NT, 4], I32)
            loaded, cleared, filled = (ph.sem(n) for n in ("loaded", "cleared", "filled"))
            block = ph.block()

            @block.sync
            def _(sp):
                sp.dma_start(src[:, :], e["src"]).then_inc(loaded, 16)
                sp.dma_start(rel[:, :], e["rel"]).then_inc(loaded, 16)
                sp.dma_start(weight[:, :], e["weight"]).then_inc(loaded, 16)
                sp.wait_ge(cleared, 2)
                sp.dma_start(scratch["slots"].rearrange("(p t) c -> p t c", p=P), empty[:, :, :]).then_inc(filled, 16)
                sp.wait_ge(filled, 16)

            @block.vector
            def _(dve):
                dve.memset(empty[:, :, 0:3], 0).then_inc(cleared, 1)
                dve.memset(empty[:, :, 3].bitcast(F32), NO_NODE).then_inc(cleared, 1)
                dve.wait_ge(loaded, 48)
                dve.scalar_tensor_tensor(info[:, :, 0], src[:, :], float(REL), rel[:, :], ALU.mult, ALU.add)
                dve.tensor_copy(info[:, :, 1], src[:, :])
                dve.tensor_copy(info[:, :, 2].bitcast(F32), weight[:, :])

        info_flat = info[:, :, :].rearrange("p t c -> p (t c)")

        def pieces(sp, t, n, rows, first):
            return [lambda: sp.dma_start(rows[:, first:first + n, :].rearrange("p t c -> p (t c)"),
                                         info_flat[:, bass.ds(t * 4, n * 4)])]

        scatter(nc, "info", addr, scratch["slots"], pieces)
    with Phase(nc, "unpack") as ph:
        back = ph.sb("back", [P, NT, 4], I32)
        loaded = ph.sem("loaded")
        block = ph.block()

        @block.sync
        def _(sp):
            sp.dma_start(back[:, :, :], scratch["slots"].rearrange("(p t) c -> p t c", p=P)).then_inc(loaded, 16)

        @block.vector
        def _(dve):
            dve.wait_ge(loaded, 16)
            dve.tensor_copy(mem.slot_rel[:, :], back[:, :, 0])
            dve.tensor_copy(mem.slot_src[:, :], back[:, :, 1])
            dve.tensor_copy(mem.slot_weight[:, :], back[:, :, 2].bitcast(F32))
            dve.tensor_copy(mem.slot_node[:, 0:NT], back[:, :, 3].bitcast(F32))


def sort_edge_rows(nc, mem, e, scratch):
    with ExitStack() as ctx:
        addr = ctx.enter_context(nc.sbuf_tensor("src_addr", [P, COLS], I32))
        node = ctx.enter_context(nc.sbuf_tensor("src_node", [P, COLS], F32))
        sort_by_tile(nc, mem, "src", e["src"], addr[:, :], node[:, :], mem.tile_of_src)
        with Phase(nc, "empty_rows") as ph:
            piece = NT // 16
            empty = ph.sb("empty", [P, piece, 1 + ECOLS])
            cleared, filled = ph.sem("cleared"), ph.sem("filled")
            block = ph.block()

            @block.vector
            def _(dve):
                dve.memset(empty[:, :, 1:1 + ECOLS], 0.0).then_inc(cleared, 1)
                dve.memset(empty[:, :, 0], NO_NODE).then_inc(cleared, 1)

            @block.sync
            def _(sp):
                sp.wait_ge(cleared, 2)
                for n in range(16):
                    sp.dma_start(scratch["edge_rows"].rearrange("(p t) c -> p t c", p=P)[:, n * piece:(n + 1) * piece, :],
                                 empty[:, :, :]).then_inc(filled, 16)
                sp.wait_ge(filled, 16 * 16)

        def pieces(sp, t, n, rows, first):
            return [lambda: sp.dma_start(rows[:, first:first + n, 1:1 + EDGE_D], e["attr"][:, bass.ds(t, n), :])]

        scatter(nc, "rows", addr, scratch["edge_rows"], pieces, node, mem.ones)


def load_nodes(nc, mem, e):
    with Phase(nc, "nodes") as ph:
        loaded = ph.sem("loaded")
        block = ph.block()

        @block.sync
        def _(sp):
            sp.dma_start(mem.x[:, :].rearrange("p (t d) -> p t d", d=D),
                         e["x"].rearrange("(t p) d -> p t d", p=P)).then_inc(loaded, 16)
            sp.wait_ge(loaded, 16)


def finish_stats(nc, mem, name, halves):
    with Phase(nc, name) as ph:
        mean, diff, var, std = (ph.sb(n, [P, BUCKETS]) for n in ("mean", "diff", "var", "std"))
        chain, var_ready, std_ready = ph.sem("chain"), ph.sem("var_ready"), ph.sem("std_ready")
        h = halves[:, :].rearrange("p (t s) -> p t s", s=6)
        block = ph.block()

        @block.scalar
        def _(act):
            act.wait_ge(var_ready, 1)
            act.activation(std[:, :], var[:, :], ACT.Sqrt, bias=mem.eps[:, :]).then_inc(std_ready, 1)

        @block.vector
        def _(dve):
            dve.tensor_tensor(mean[:, :], h[:, :, 1], h[:, :, 4], ALU.add).then_inc(chain, 1)
            dve.tensor_tensor(diff[:, :], h[:, :, 1], h[:, :, 4], ALU.subtract).then_inc(chain, 1)
            dve.tensor_tensor(var[:, :], h[:, :, 2], h[:, :, 5], ALU.add).then_inc(chain, 1)
            dve.wait_ge(chain, 2)
            dve.scalar_tensor_tensor(diff[:, :], diff[:, :], 0.25, diff[:, :], ALU.mult, ALU.mult).then_inc(chain, 1)
            dve.wait_ge(chain, 4)
            dve.scalar_tensor_tensor(var[:, :], var[:, :], 1.0 / D, diff[:, :], ALU.mult, ALU.add
                                     ).then_inc(var_ready, 1)
            dve.wait_ge(std_ready, 1)
            dve.reciprocal(mem.rstd[:, :], std[:, :]).then_inc(chain, 1)
            dve.wait_ge(chain, 5)
            dve.scalar_tensor_tensor(mem.shift[:, :], mean[:, :], -0.5, mem.rstd[:, :], ALU.mult, ALU.mult)


def first_stats(nc, mem, halves):
    with Phase(nc, "stats") as ph:
        block = ph.block()

        @block.vector
        def _(dve):
            with dve.Fori(0, BUCKETS) as t:
                dve.bn_stats(halves[:, cols(t, 6)], mem.x[:, cols(t, D)])


PAIRS = BUCKETS // 2


def relational_tables(nc, mem, e, layer, table):
    chunks = REL * D // 512
    with Phase(nc, f"rel{layer}") as ph:
        w = ph.sb("w", [P, 2, REL * D + D])
        bias = ph.sb("bias", [P, D])
        h = [ph.sb(f"h{u}", [P, D]) for u in range(2)]
        turned = [ph.sb(f"turned{u}", [P, D]) for u in range(2)]
        out = [ph.sb(f"out{u}", [P, REL * D]) for u in range(2)]
        turned_ps = [ph.psum(f"turned_ps{u}", [P, 512]) for u in range(2)]
        product_ps = [ph.psum(f"product_ps{c}", [P, 512]) for c in range(chunks + 1)]
        loaded, h_ready, transposed, turned_ready, products, act_out, dve_out = (
            ph.sem(n) for n in ("loaded", "h_ready", "transposed", "turned_ready", "products",
                                "act_out", "dve_out"))
        stored = [ph.sem(f"stored{u}") for u in range(2)]
        block = ph.block()

        @block.sync
        def _(sp):
            for k in range(2):
                sp.dma_start(w[:, k, :], e["rel_w"][:, layer, k, :]).then_inc(loaded, 16)
            sp.dma_start(bias[:, :], e["rel_b"][layer].partition_broadcast(P)).then_inc(loaded, 16)

            def store(i):
                for u in range(2):
                    t = i * 2 + u
                    sp.wait_ge(act_out, (t + 1) * 3)
                    sp.sem_inc(ph.turn, 1)
                    sp.wait_ge(dve_out, (t + 1) * 2)
                    sp.sem_inc(ph.turn, 1)
                    sp.dma_start(table.rearrange("(n r) d -> n (r d)", r=REL)[bass.ds(t * P, P), :],
                                 out[u][:, :]).then_inc(stored[u], 16)
            rounds(sp, PAIRS, store)
            for u in range(2):
                sp.wait_ge(stored[u], 16 * PAIRS)

        @block.scalar
        def _(act):
            def tiles(i):
                for u in range(2):
                    t = i * 2 + u
                    if not is_first(i):
                        act.wait_ge(transposed, t - 1)
                        act.sem_inc(ph.turn, 1)
                    if layer == 0:
                        ins = act.activation(h[u][:, :], mem.x[:, cols(t, D)], ACT.Relu,
                                             bias=mem.shift[:, bass.ds(t, 1)], scale=mem.rstd[:, bass.ds(t, 1)])
                    else:
                        ins = act.activation(h[u][:, :], mem.acc[:, cols(t, ACCW, 0, D)], ACT.Relu)
                    ins.then_inc(h_ready, 1)
                for u in range(2):
                    t = i * 2 + u
                    act.wait_ge(transposed, t + 1)
                    if not is_first(i):
                        act.wait_ge(products, (t - 1) * (chunks + 1))
                    act.copy(turned[u][:, :], turned_ps[u][:, 0:D]).then_inc(turned_ready, 1)
                for u in range(2):
                    t = i * 2 + u
                    if not is_first(i):
                        act.wait_ge(stored[u], i * 16)
                    for c in range(3):
                        act.wait_ge(products, t * (chunks + 1) + c + 1)
                        act.copy(out[u][:, cols(c, 512)], product_ps[c][:, :]).then_inc(act_out, 1)
            rounds(act, PAIRS, tiles)

        @block.tensor
        def _(pe):
            pe.wait_ge(loaded, 48)

            def tiles(i):
                for u in range(2):
                    t = i * 2 + u
                    pe.wait_ge(h_ready, t + 1)
                    if not is_first(i):
                        pe.wait_ge(turned_ready, t - 1)
                    for k in range(2):
                        ins = pe.transpose(turned_ps[u][:, cols(k, P)], h[u][:, cols(k, P)], mem.ident[:, :])
                    ins.then_inc(transposed, 1)
                for u in range(2):
                    t = i * 2 + u
                    pe.wait_ge(turned_ready, t + 1)
                    if not (is_first(i) and u == 0):
                        pe.wait_ge(act_out, t * 3)
                        pe.wait_ge(dve_out, t * 2)
                    for c in range(chunks + 1):
                        n = 512 if c < chunks else D
                        for k in range(2):
                            ins = pe.matmul(product_ps[c][:, 0:n], turned[u][:, cols(k, P)],
                                            w[:, k, c * 512:c * 512 + n], start=(k == 0), stop=(k == 1))
                        ins.then_inc(products, 1)
            rounds(pe, PAIRS, tiles)

        @block.vector
        def _(dve):
            dve.wait_ge(loaded, 48)

            def tiles(i):
                for u in range(2):
                    t = i * 2 + u
                    if not is_first(i):
                        dve.wait_ge(stored[u], i * 16)
                    dve.wait_ge(products, t * (chunks + 1) + chunks)
                    dve.tensor_copy(out[u][:, cols(3, 512)], product_ps[3][:, :]).then_inc(dve_out, 1)
                    dve.wait_ge(products, (t + 1) * (chunks + 1))
                    dve.tensor_tensor(mem.acc[:, cols(t, ACCW, 0, D)], product_ps[chunks][:, 0:D], bias[:, :],
                                      ALU.add).then_inc(dve_out, 1)
            rounds(dve, PAIRS, tiles)


class Group:

    def __init__(self, i, g):
        self.i, self.g = i + g // GROUPS, g % GROUPS
        self.q = self.i * GROUPS + self.g
        self.t = self.i * RING + self.g * GROUP
        self.exists = not isinstance(self.q, int) or 0 <= self.q < NT // GROUP

    def after(self, n):
        return not isinstance(self.q, int) or self.q >= n


def over_groups(engine, step, lead):
    def one_round(i, first=0):
        for g in range(first, GROUPS):
            step(i, g)
    one_round(-1, GROUPS - lead)
    one_round(0)
    with engine.Fori(1, NT // RING - 1) as i:
        one_round(i)
    one_round(NT // RING - 1)


def aggregate(nc, mem, name, table, slot_row, weighted=False, degree=False, edge_rows=None):
    width = D + (1 if degree else 0)
    n_rounds = NT // RING
    with Phase(nc, name) as ph:
        rows = ph.sb("rows", [P, RING, width])
        which = ph.sb("which", [P, RING], I32)
        onehot = ph.sb("onehot", [P, 2 * GROUP, P])
        sums_ps = [ph.psum(f"sums_ps{k}", [P, 512]) for k in range(GROUP)]
        staged = [ph.sem(f"staged{g}") for g in range(GROUPS)]
        landed = [ph.sem(f"landed{g}") for g in range(GROUPS)]
        onehots, products, added, filled = (
            ph.sem(n) for n in ("onehots", "products", "added", "filled"))
        if edge_rows is not None:
            erow = ph.sb("erow", [P, RING, 1 + ECOLS])
            ehot = ph.sb("ehot", [P, 2 * GROUP, P])
            esums_ps = [ph.psum(f"esums_ps{k}", [P, 512]) for k in range(GROUP)]
            eloaded = [ph.sem(f"eloaded{g}") for g in range(GROUPS)]
            ehots, eproducts, eadded = ph.sem("ehots"), ph.sem("eproducts"), ph.sem("eadded")
        block = ph.block()

        @block.sync
        def _(sp):
            def stage(i):
                for g in range(GROUPS):
                    if not is_first(i):
                        sp.wait_ge(landed[g], i * (16 * GROUP))
                        sp.sem_inc(ph.turn, 1)
                    sp.dma_start(which[:, cols(g, GROUP)], slot_row[:, cols(i, RING, g * GROUP, GROUP)]
                                 ).then_inc(staged[g], 16)
                    if edge_rows is not None:
                        if not is_first(i):
                            sp.wait_ge(eproducts, (i - 1) * RING + (g + 1) * GROUP)
                            sp.sem_inc(ph.turn, 1)
                        sp.dma_start(erow[:, cols(g, GROUP), :],
                                     edge_rows.rearrange("(p t) c -> p t c", p=P)[:, cols(i, RING, g * GROUP, GROUP), :]
                                     ).then_inc(eloaded[g], 16)
            rounds(sp, n_rounds, stage)

        @block.gpsimd
        def _(pool):
            def gather(i):
                for g in range(GROUPS):
                    pool.wait_ge(staged[g], (i + 1) * 16)
                    if not is_first(i):
                        pool.wait_ge(products, (i - 1) * RING + (g + 1) * GROUP)
                        pool.sem_inc(ph.turn, 1)
                    for k in range(g * GROUP, (g + 1) * GROUP):
                        pool.indirect_dma_start(rows[:, k, 0:D], None, table,
                                                bass.IndirectOffsetOnAxis(which[:, k:k + 1], 0)
                                                ).then_inc(landed[g], 16)
            rounds(pool, n_rounds, gather)

        @block.tensor
        def _(pe):
            if degree:
                pe.wait_ge(filled, 1)

            def step(i, g):
                n = Group(i, g)
                for k in range(GROUP):
                    if edge_rows is not None:
                        pe.wait_ge(ehots, n.t + k + 1)
                        if n.after(1):
                            pe.wait_ge(eadded, n.t + k - GROUP + 1)
                        pe.matmul(esums_ps[k][:, 0:ECOLS], ehot[:, g % 2 * GROUP + k, :],
                                  erow[:, g * GROUP + k, 1:1 + ECOLS], start=True, stop=True).then_inc(eproducts, 1)
                    if k == 0:
                        pe.wait_ge(landed[g], (n.i + 1) * (16 * GROUP))
                    pe.wait_ge(onehots, n.t + k + 1)
                    if n.after(1):
                        pe.wait_ge(added, n.t + k - GROUP + 1)
                    pe.matmul(sums_ps[k][:, 0:width], onehot[:, g % 2 * GROUP + k, :],
                              rows[:, g * GROUP + k, :], start=True, stop=True).then_inc(products, 1)
            over_groups(pe, step, 0)

        @block.vector
        def _(dve):
            tiles, edge_tiles = [], []

            def onehot_of(n, k):
                if n.after(2):
                    dve.wait_ge(products, n.t + k - 2 * GROUP + 1)
                node = mem.slot_node[:, bass.ds(n.t + k, 1)]
                out = onehot[:, n.g % 2 * GROUP + k, :]
                if weighted:
                    ins = dve.tensor_scalar(out, mem.iota[:, :], node, mem.slot_weight[:, bass.ds(n.t + k, 1)],
                                            ALU.is_equal, ALU.mult)
                else:
                    ins = dve.tensor_scalar(out, mem.iota[:, :], node, None, ALU.is_equal)
                ins.then_inc(onehots, 1)

            def edge_hot_of(n, k):
                if k == 0:
                    dve.wait_ge(eloaded[n.g], (n.i + 1) * 16)
                if n.after(2):
                    dve.wait_ge(eproducts, n.t + k - 2 * GROUP + 1)
                dve.tensor_scalar(ehot[:, n.g % 2 * GROUP + k, :], mem.iota[:, :], erow[:, n.g * GROUP + k, 0:1], None,
                                  ALU.is_equal).then_inc(ehots, 1)

            def add(n, k):
                into = mem.acc[:, cols(tiles[n.g * GROUP + k], ACCW, 0, width)]
                dve.wait_ge(products, n.t + k + 1)
                if n.after(1) or k:
                    dve.wait_ge(added, n.t + k)
                dve.tensor_tensor(into, into, sums_ps[k][:, 0:width], ALU.add).then_inc(added, 1)

            def edge_add(n, k):
                into = mem.edge_acc[:, cols(edge_tiles[n.g * GROUP + k], ECOLS)]
                dve.wait_ge(eproducts, n.t + k + 1)
                if n.after(1) or k:
                    dve.wait_ge(eadded, n.t + k)
                dve.tensor_tensor(into, into, esums_ps[k][:, 0:ECOLS], ALU.add).then_inc(eadded, 1)

            def step(i, g):
                now, following = Group(i, g), Group(i, g + 1)
                if now.exists and g == 0:
                    tiles[:] = tiles_of(nc, dve, mem.tile_of_dst, now.t, RING)
                if edge_rows is not None and now.exists and g % 2 == 0:
                    edge_tiles[g * GROUP:] = tiles_of(nc, dve, mem.tile_of_src, now.t, RING // 2)
                for k in range(GROUP):
                    if following.exists:
                        onehot_of(following, k)
                    if edge_rows is not None and now.exists:
                        edge_add(now, k)
                    if edge_rows is not None and following.exists:
                        edge_hot_of(following, k)
                    if now.exists:
                        add(now, k)
            if degree:
                dve.memset(rows[:, :, D], 1.0).then_inc(filled, 1)
            over_groups(dve, step, 1)


def relational_end(nc, mem, halves):
    with Phase(nc, "relend") as ph:
        s = [ph.sb(f"s{u}", [P, D]) for u in range(2)]
        sigmoids, x_ready = ph.sem("sigmoids"), ph.sem("x_ready")
        block = ph.block()

        @block.scalar
        def _(act):
            def tiles(i):
                for u in range(2):
                    t = i * 2 + u
                    if not is_first(i):
                        act.wait_ge(x_ready, t - 1)
                        act.sem_inc(ph.turn, 1)
                    act.activation(s[u][:, :], mem.acc[:, cols(t, ACCW, 0, D)], ACT.Sigmoid).then_inc(sigmoids, 1)
            rounds(act, PAIRS, tiles)

        @block.vector
        def _(dve):
            with dve.Fori(0, PAIRS) as i:
                for u in range(2):
                    t = i * 2 + u
                    x = mem.x[:, cols(t, D)]
                    dve.wait_ge(sigmoids, t + 1)
                    dve.tensor_tensor(x, x, s[u][:, :], ALU.add).then_inc(x_ready, 1)
                for u in range(2):
                    t = i * 2 + u
                    dve.wait_ge(x_ready, t + 1)
                    dve.sem_inc(ph.turn, 1)
                    dve.bn_stats(halves[:, cols(t, 6)], mem.x[:, cols(t, D)])


def node_table(nc, mem, table):
    with Phase(nc, "node_table") as ph:
        h = [ph.sb(f"h{u}", [P, D]) for u in range(2)]
        deg = ph.sb("deg", [P, BUCKETS])
        h_ready, chain = ph.sem("h_ready"), ph.sem("chain")
        stored = [ph.sem(f"stored{u}") for u in range(2)]
        block = ph.block()

        @block.scalar
        def _(act):
            def tiles(i):
                for u in range(2):
                    t = i * 2 + u
                    if not is_first(i):
                        act.wait_ge(stored[u], i * 16)
                        act.sem_inc(ph.turn, 1)
                    act.activation(h[u][:, :], mem.x[:, cols(t, D)], ACT.Relu, bias=mem.shift[:, bass.ds(t, 1)],
                                   scale=mem.rstd[:, bass.ds(t, 1)]).then_inc(h_ready, 1)
            rounds(act, PAIRS, tiles)

        @block.sync
        def _(sp):
            with sp.Fori(0, PAIRS) as i:
                for u in range(2):
                    sp.wait_ge(h_ready, i * 2 + u + 1)
                    sp.sem_inc(ph.turn, 1)
                    sp.dma_start(table[bass.ds((i * 2 + u) * P, P), :], h[u][:, :]).then_inc(stored[u], 16)
            for u in range(2):
                sp.wait_ge(stored[u], 16 * PAIRS)

        @block.vector
        def _(dve):
            acc = mem.acc[:, :].rearrange("p (t c) -> p t c", c=ACCW)
            dve.tensor_scalar(deg[:, :], acc[:, :, D], 1.0, None, ALU.max).then_inc(chain, 1)
            dve.wait_ge(chain, 1)
            dve.reciprocal(mem.inv_deg[:, :], deg[:, :])
            dve.memset(acc[:, :, 0:D], 0.0)


def conv_layers(nc, mem, e, table):
    L = 4
    with Phase(nc, "conv") as ph:
        sb, sem = ph.sb, ph.sem
        w = sb("w", [P, 2, 2, L * D])
        bias, gain, norm_b = (sb(n, [P, L * D]) for n in ("bias", "gain", "norm_b"))
        two = range(2)
        node, agg = [sb(f"node{u}", [P, D]) for u in two], [sb(f"agg{u}", [P, D]) for u in two]
        turned = [sb(f"turned{u}", [P, 4 * P]) for u in two]
        node_b = [sb(f"node_b{u}", [P, L * D]) for u in two]
        z = [sb(f"z{u}", [P, L * D]) for u in two]
        stats = [sb(f"stats{u}", [P, L * 6]) for u in two]
        mv = [sb(f"mv{u}", [P, L * 2]) for u in two]
        std, rstd, shift = ([sb(f"{n}{u}", [P, L]) for u in two] for n in ("std", "rstd", "shift"))
        turned_ps = [ph.psum(f"turned_ps{u}", [P, 512]) for u in two]
        z_ps = [[ph.psum(f"z_ps{u}{c}", [P, 512]) for c in two] for u in two]
        loaded = sem("loaded")
        node_loaded = [sem(f"node_loaded{u}") for u in two]
        (agg_ready, transposed, turned_ready, products, node_b_ready, z_ready, stats_ready, mv_ready, std_ready,
         rstd_ready, shift_ready, normed, gained, biased, positive, summed) = (
            sem(n) for n in ("agg_ready", "transposed", "turned_ready", "products", "node_b_ready", "z_ready",
                             "stats_ready", "mv_ready", "std_ready", "rstd_ready", "shift_ready", "normed",
                             "gained", "biased", "positive", "summed"))
        block = ph.block()

        @block.sync
        def _(sp):
            sp.dma_start(w[:, :, :, :], e["conv_w"]).then_inc(loaded, 16)
            for into, name in ((bias, "conv_b"), (gain, "conv_g"), (norm_b, "conv_n")):
                sp.dma_start(into[:, :], e[name][0].partition_broadcast(P)).then_inc(loaded, 16)

            def load(i):
                for u in two:
                    t = i * 2 + u
                    if not is_first(i):
                        sp.wait_ge(transposed, t - 1)
                        sp.sem_inc(ph.turn, 1)
                        sp.wait_ge(node_b_ready, t - 1)
                        sp.sem_inc(ph.turn, 1)
                    sp.dma_start(node[u][:, :], table[bass.ds(t * P, P), :]).then_inc(node_loaded[u], 16)
            rounds(sp, PAIRS, load)

        @block.gpsimd
        def _(pool):
            pool.wait_ge(loaded, 64)

            def tiles(i):
                for u in two:
                    t = i * 2 + u
                    pool.wait_ge(node_loaded[u], (i + 1) * 16)
                    if not is_first(i):
                        pool.wait_ge(z_ready, (t - 1) * 2)
                    pool.tensor_tensor(node_b[u][:, :].rearrange("p (l d) -> p l d", l=L),
                                       node[u][:, :].unsqueeze(1).broadcast_to([P, L, D]),
                                       bias[:, :].rearrange("p (l d) -> p l d", l=L), ALU.add).then_inc(node_b_ready, 1)
                for u in two:
                    t = i * 2 + u
                    pool.wait_ge(normed, (t + 1) * L)
                    pool.tensor_tensor(z[u][:, :], z[u][:, :], gain[:, :], ALU.mult).then_inc(gained, 1)
                    pool.wait_ge(gained, t + 1)
                    pool.tensor_tensor(z[u][:, :], z[u][:, :], norm_b[:, :], ALU.add).then_inc(biased, 1)
            rounds(pool, PAIRS, tiles)

        @block.tensor
        def _(pe):
            pe.wait_ge(loaded, 64)

            def tiles(i):
                for u in two:
                    t = i * 2 + u
                    pe.wait_ge(node_loaded[u], (i + 1) * 16)
                    pe.wait_ge(agg_ready, t + 1)
                    if not is_first(i):
                        pe.wait_ge(turned_ready, t - 1)
                    for k in range(4):
                        src = (agg, node)[k // 2][u]
                        ins = pe.transpose(turned_ps[u][:, cols(k, P)], src[:, cols(k % 2, P)], mem.ident[:, :])
                    ins.then_inc(transposed, 1)
                for u in two:
                    t = i * 2 + u
                    pe.wait_ge(turned_ready, t + 1)
                    if not is_first(i):
                        pe.wait_ge(z_ready, (t - 1) * 2)
                    for c in two:
                        for k in range(4):
                            ins = pe.matmul(z_ps[u][c][:, :], turned[u][:, cols(k, P)],
                                            w[:, k // 2, k % 2, cols(c, 512)], start=(k == 0), stop=(k == 3))
                        ins.then_inc(products, 1)
            rounds(pe, PAIRS, tiles)

        @block.scalar
        def _(act):
            def tiles(i):
                for u in two:
                    t = i * 2 + u
                    act.wait_ge(transposed, t + 1)
                    if not is_first(i):
                        act.wait_ge(products, (t - 1) * 2)
                    act.copy(turned[u][:, :], turned_ps[u][:, :]).then_inc(turned_ready, 1)
                for u in two:
                    t = i * 2 + u
                    act.wait_ge(mv_ready, (t + 1) * L)
                    act.activation(std[u][:, :], mv[u][:, :].rearrange("p (l s) -> p l s", s=2)[:, :, 1], ACT.Sqrt,
                                   bias=mem.eps[:, :]).then_inc(std_ready, 1)
                for u in two:
                    t = i * 2 + u
                    act.wait_ge(shift_ready, t + 1)
                    for n in range(L):
                        act.activation(z[u][:, cols(n, D)], z[u][:, cols(n, D)], ACT.Identity,
                                       bias=shift[u][:, n:n + 1], scale=rstd[u][:, n:n + 1]).then_inc(normed, 1)
                for u in two:
                    t = i * 2 + u
                    act.wait_ge(biased, t + 1)
                    act.activation(z[u][:, :], z[u][:, :], ACT.Relu).then_inc(positive, 1)
            rounds(act, PAIRS, tiles)

        @block.vector
        def _(dve):
            def tiles(i):
                for u in two:
                    t = i * 2 + u
                    if not is_first(i):
                        dve.wait_ge(transposed, t - 1)
                    dve.tensor_scalar(agg[u][:, :], mem.acc[:, cols(t, ACCW, 0, D)], mem.inv_deg[:, bass.ds(t, 1)],
                                      None, ALU.mult).then_inc(agg_ready, 1)
                for u in two:
                    t = i * 2 + u
                    dve.wait_ge(node_b_ready, t + 1)
                    if not is_first(i):
                        dve.wait_ge(summed, t - 1)
                    for c in two:
                        dve.wait_ge(products, t * 2 + c + 1)
                        dve.tensor_tensor(z[u][:, cols(c, 512)], z_ps[u][c][:, :], node_b[u][:, cols(c, 512)],
                                          ALU.add).then_inc(z_ready, 1)
                for u in two:
                    t = i * 2 + u
                    dve.wait_ge(z_ready, (t + 1) * 2)
                    for n in range(L):
                        dve.bn_stats(stats[u][:, cols(n, 6)], z[u][:, cols(n, D)]).then_inc(stats_ready, 1)
                for u in two:
                    t = i * 2 + u
                    dve.wait_ge(stats_ready, (t + 1) * L)
                    dve.sem_inc(ph.turn, 1)
                    for n in range(L):
                        dve.bn_aggr(mv[u][:, cols(n, 2)], stats[u][:, cols(n, 6)]).then_inc(mv_ready, 1)
                for u in two:
                    t = i * 2 + u
                    dve.wait_ge(std_ready, t + 1)
                    dve.reciprocal(rstd[u][:, :], std[u][:, :]).then_inc(rstd_ready, 1)
                for u in two:
                    t = i * 2 + u
                    dve.wait_ge(rstd_ready, t + 1)
                    dve.scalar_tensor_tensor(shift[u][:, :], mv[u][:, :].rearrange("p (l s) -> p l s", s=2)[:, :, 0],
                                             -1.0, rstd[u][:, :], ALU.mult, ALU.mult).then_inc(shift_ready, 1)
                for u in two:
                    t = i * 2 + u
                    dve.wait_ge(positive, t + 1)
                    dve.sem_inc(ph.turn, 1)
                    dve.tensor_reduce(mem.acc[:, cols(t, ACCW, 0, D)], z[u][:, :].rearrange("p (l d) -> p d l", l=L),
                                      AX.X, ALU.add).then_inc(summed, 1)
            rounds(dve, PAIRS, tiles)


def mlp_layer(nc, mem, e, n, halves):
    with Phase(nc, f"mlp{n}") as ph:
        sb, sem = ph.sb, ph.sem
        w = sb("w", [P, 2, D])
        bias, gain, norm_b = (sb(x, [P, D]) for x in ("bias", "gain", "norm_b"))
        two = range(2)
        h, turned, z = ([sb(f"{x}{u}", [P, D]) for u in two] for x in ("h", "turned", "z"))
        stats, mv = [sb(f"stats{u}", [P, 6]) for u in two], [sb(f"mv{u}", [P, 2]) for u in two]
        std, rstd, shift = ([sb(f"{x}{u}", [P, 1]) for u in two] for x in ("std", "rstd", "shift"))
        turned_ps = [ph.psum(f"turned_ps{u}", [P, 512]) for u in two]
        z_ps = [ph.psum(f"z_ps{u}", [P, 512]) for u in two]
        (loaded, h_ready, transposed, turned_ready, products, z_ready, stats_ready, mv_ready, std_ready,
         rstd_ready, shift_ready, normed, gained, biased, done) = (
            sem(x) for x in ("loaded", "h_ready", "transposed", "turned_ready", "products", "z_ready",
                             "stats_ready", "mv_ready", "std_ready", "rstd_ready", "shift_ready", "normed",
                             "gained", "biased", "done"))
        block = ph.block()

        @block.sync
        def _(sp):
            sp.dma_start(w[:, :, :], e["mlp_w"][:, n, :, :]).then_inc(loaded, 16)
            for into, row in ((bias, 0), (gain, 1), (norm_b, 2)):
                sp.dma_start(into[:, :], e["mlp_v"][3 * n + row].partition_broadcast(P)).then_inc(loaded, 16)

        @block.gpsimd
        def _(pool):
            pool.wait_ge(loaded, 64)
            with pool.Fori(0, PAIRS) as i:
                for u in two:
                    t = i * 2 + u
                    pool.wait_ge(normed, t + 1)
                    pool.tensor_tensor(z[u][:, :], z[u][:, :], gain[:, :], ALU.mult).then_inc(gained, 1)
                    pool.wait_ge(gained, t + 1)
                    pool.tensor_tensor(z[u][:, :], z[u][:, :], norm_b[:, :], ALU.add).then_inc(biased, 1)

        @block.tensor
        def _(pe):
            pe.wait_ge(loaded, 64)

            def tiles(i):
                for u in two:
                    t = i * 2 + u
                    pe.wait_ge(h_ready, t + 1)
                    if not is_first(i):
                        pe.wait_ge(turned_ready, t - 1)
                    for k in two:
                        ins = pe.transpose(turned_ps[u][:, cols(k, P)], h[u][:, cols(k, P)], mem.ident[:, :])
                    ins.then_inc(transposed, 1)
                for u in two:
                    t = i * 2 + u
                    pe.wait_ge(turned_ready, t + 1)
                    if not is_first(i):
                        pe.wait_ge(z_ready, t - 1)
                    for k in two:
                        ins = pe.matmul(z_ps[u][:, 0:D], turned[u][:, cols(k, P)], w[:, k, :],
                                        start=(k == 0), stop=(k == 1))
                    ins.then_inc(products, 1)
            rounds(pe, PAIRS, tiles)

        @block.scalar
        def _(act):
            def tiles(i):
                for u in two:
                    t = i * 2 + u
                    if not is_first(i):
                        act.wait_ge(transposed, t - 1)
                        act.sem_inc(ph.turn, 1)
                    act.copy(h[u][:, :], mem.acc[:, cols(t, ACCW, 0, D)]).then_inc(h_ready, 1)
                for u in two:
                    t = i * 2 + u
                    act.wait_ge(transposed, t + 1)
                    if not is_first(i):
                        act.wait_ge(products, t - 1)
                    act.copy(turned[u][:, :], turned_ps[u][:, 0:D]).then_inc(turned_ready, 1)
                for u in two:
                    t = i * 2 + u
                    act.wait_ge(mv_ready, t + 1)
                    act.activation(std[u][:, :], mv[u][:, 1:2], ACT.Sqrt, bias=mem.eps[:, :]).then_inc(std_ready, 1)
                for u in two:
                    t = i * 2 + u
                    act.wait_ge(shift_ready, t + 1)
                    act.activation(z[u][:, :], z[u][:, :], ACT.Identity, bias=shift[u][:, :], scale=rstd[u][:, :]
                                   ).then_inc(normed, 1)
            rounds(act, PAIRS, tiles)

        @block.vector
        def _(dve):
            dve.wait_ge(loaded, 64)

            def tiles(i):
                for u in two:
                    t = i * 2 + u
                    dve.wait_ge(products, t + 1)
                    if not is_first(i):
                        dve.wait_ge(done, t - 1)
                    dve.tensor_tensor(z[u][:, :], z_ps[u][:, 0:D], bias[:, :], ALU.add).then_inc(z_ready, 1)
                for u in two:
                    t = i * 2 + u
                    dve.wait_ge(z_ready, t + 1)
                    dve.bn_stats(stats[u][:, :], z[u][:, :]).then_inc(stats_ready, 1)
                for u in two:
                    t = i * 2 + u
                    dve.wait_ge(stats_ready, t + 1)
                    dve.sem_inc(ph.turn, 1)
                    dve.bn_aggr(mv[u][:, :], stats[u][:, :]).then_inc(mv_ready, 1)
                for u in two:
                    t = i * 2 + u
                    dve.wait_ge(std_ready, t + 1)
                    dve.reciprocal(rstd[u][:, :], std[u][:, :]).then_inc(rstd_ready, 1)
                for u in two:
                    t = i * 2 + u
                    dve.wait_ge(rstd_ready, t + 1)
                    dve.scalar_tensor_tensor(shift[u][:, :], mv[u][:, 0:1], -1.0, rstd[u][:, :], ALU.mult, ALU.mult
                                             ).then_inc(shift_ready, 1)
                for u in two:
                    t = i * 2 + u
                    dve.wait_ge(biased, t + 1)
                    if n == 0:
                        dve.tensor_scalar(mem.acc[:, cols(t, ACCW, 0, D)], z[u][:, :], 0.0, None, ALU.max
                                          ).then_inc(done, 1)
                    else:
                        x = mem.x[:, cols(t, D)]
                        dve.scalar_tensor_tensor(x, z[u][:, :], 0.0, x, ALU.max, ALU.add).then_inc(done, 1)
                if n == 1:
                    for u in two:
                        t = i * 2 + u
                        dve.wait_ge(done, t + 1)
                        dve.sem_inc(ph.turn, 1)
                        dve.bn_stats(halves[:, cols(t, 6)], mem.x[:, cols(t, D)])
            rounds(dve, PAIRS, tiles)


def edge_layer(nc, mem, e, halves):
    F = e["edge_w"].shape[2]
    with Phase(nc, "edge") as ph:
        sb, sem = ph.sb, ph.sem
        two = range(2)
        w1, w1e, w1u = sb("w1", [P, 2, F]), sb("w1e", [EDGE_D, F]), sb("w1u", [P, F])
        w2, b1, b2 = sb("w2", [P, F // P, D]), sb("b1", [P, F]), sb("b2", [P, D])
        u_col, u_wide = sb("u_col", [P, 1]), sb("u_wide", [P, P])
        count, inv_count = sb("count", [P, BUCKETS]), sb("inv_count", [P, BUCKETS])
        h, turned, out = ([sb(f"{x}{u}", [P, D]) for u in two] for x in ("h", "turned", "out"))
        mean, mean_t = [sb(f"mean{u}", [P, EDGE_D]) for u in two], [sb(f"mean_t{u}", [EDGE_D, P]) for u in two]
        hidden, hidden_t = ([sb(f"{x}{u}", [P, F]) for u in two] for x in ("hidden", "hidden_t"))
        turned_ps, hidden_ps, hidden_t_ps, out_ps = (
            [ph.psum(f"{x}{u}", [P, 512]) for u in two] for x in ("turned_ps", "hidden_ps", "hidden_t_ps", "out_ps"))
        (loaded, chain, u_ready, u_product, u_taken, h_ready, mean_ready, transposed, turned_ready, products,
         hidden_ready, positive, hidden_transposed, hidden_t_ready, out_products, out_ready, x_ready) = (
            sem(x) for x in ("loaded", "chain", "u_ready", "u_product", "u_taken", "h_ready", "mean_ready",
                             "transposed", "turned_ready", "products", "hidden_ready", "positive",
                             "hidden_transposed", "hidden_t_ready", "out_products", "out_ready", "x_ready"))
        block = ph.block()

        @block.sync
        def _(sp):
            for into, src in ((w1[:, :, :], e["edge_w"]), (w1e[:, :], e["edge_we"]), (w1u[:, :], e["edge_wu"]),
                              (w2[:, :, :], e["edge_w2"]), (u_col[:, :], e["edge_u"]),
                              (b1[:, :], e["edge_b1"][0].partition_broadcast(P)),
                              (b2[:, :], e["edge_b2"][0].partition_broadcast(P))):
                sp.dma_start(into, src).then_inc(loaded, 16)

        @block.tensor
        def _(pe):
            pe.wait_ge(loaded, 7 * 16)
            pe.wait_ge(u_ready, 1)
            pe.matmul(hidden_ps[0][:, :], u_wide[:, :], w1u[:, :], start=True, stop=True).then_inc(u_product, 1)
            pe.wait_ge(u_taken, 1)

            def tiles(i):
                for u in two:
                    t = i * 2 + u
                    pe.wait_ge(h_ready, t + 1)
                    pe.wait_ge(mean_ready, t + 1)
                    if not is_first(i):
                        pe.wait_ge(turned_ready, (t - 1) * 2)
                    for k in two:
                        pe.transpose(turned_ps[u][:, cols(k, P)], h[u][:, cols(k, P)], mem.ident[:, :])
                    pe.transpose(turned_ps[u][0:EDGE_D, cols(2, P)], mean[u][:, :], mem.ident[:, :]
                                 ).then_inc(transposed, 1)
                for u in two:
                    t = i * 2 + u
                    pe.wait_ge(turned_ready, (t + 1) * 2)
                    if not is_first(i):
                        pe.wait_ge(hidden_ready, t - 1)
                    for k in two:
                        pe.matmul(hidden_ps[u][:, :], turned[u][:, cols(k, P)], w1[:, k, :], start=(k == 0), stop=False)
                    pe.matmul(hidden_ps[u][:, :], mean_t[u][:, :], w1e[:, :], start=False, stop=True
                              ).then_inc(products, 1)
                for u in two:
                    t = i * 2 + u
                    pe.wait_ge(positive, t + 1)
                    if not is_first(i):
                        pe.wait_ge(hidden_t_ready, t - 1)
                    for k in range(F // P):
                        ins = pe.transpose(hidden_t_ps[u][:, cols(k, P)], hidden[u][:, cols(k, P)], mem.ident[:, :])
                    ins.then_inc(hidden_transposed, 1)
                for u in two:
                    t = i * 2 + u
                    pe.wait_ge(hidden_t_ready, t + 1)
                    if not is_first(i):
                        pe.wait_ge(out_ready, t - 1)
                    for k in range(F // P):
                        ins = pe.matmul(out_ps[u][:, 0:D], hidden_t[u][:, cols(k, P)], w2[:, k, :],
                                        start=(k == 0), stop=(k == F // P - 1))
                    ins.then_inc(out_products, 1)
            rounds(pe, PAIRS, tiles)

        @block.scalar
        def _(act):
            def tiles(i):
                for u in two:
                    t = i * 2 + u
                    if not is_first(i):
                        act.wait_ge(transposed, t - 1)
                        act.sem_inc(ph.turn, 1)
                    act.activation(h[u][:, :], mem.x[:, cols(t, D)], ACT.Relu, bias=mem.shift[:, bass.ds(t, 1)],
                                   scale=mem.rstd[:, bass.ds(t, 1)]).then_inc(h_ready, 1)
                for u in two:
                    t = i * 2 + u
                    act.wait_ge(transposed, t + 1)
                    if not is_first(i):
                        act.wait_ge(products, t - 1)
                    act.copy(turned[u][:, :], turned_ps[u][:, 0:D]).then_inc(turned_ready, 1)
                    act.copy(mean_t[u][:, :], turned_ps[u][0:EDGE_D, cols(2, P)]).then_inc(turned_ready, 1)
                for u in two:
                    t = i * 2 + u
                    act.wait_ge(hidden_ready, t + 1)
                    act.activation(hidden[u][:, :], hidden[u][:, :], ACT.Relu).then_inc(positive, 1)
                for u in two:
                    t = i * 2 + u
                    act.wait_ge(hidden_transposed, t + 1)
                    if not is_first(i):
                        act.wait_ge(out_products, t - 1)
                    act.copy(hidden_t[u][:, :], hidden_t_ps[u][:, :]).then_inc(hidden_t_ready, 1)
            rounds(act, PAIRS, tiles)

        @block.vector
        def _(dve):
            edges = mem.edge_acc[:, :].rearrange("p (t c) -> p t c", c=ECOLS)
            dve.tensor_scalar(count[:, :], edges[:, :, EDGE_D], 1.0, None, ALU.max).then_inc(chain, 1)
            dve.wait_ge(loaded, 7 * 16)
            dve.tensor_scalar(u_wide[:, :], mem.ones[:, :], u_col[:, :], None, ALU.mult).then_inc(u_ready, 1)
            dve.wait_ge(chain, 1)
            dve.reciprocal(inv_count[:, :], count[:, :]).then_inc(chain, 1)
            dve.wait_ge(u_product, 1)
            dve.tensor_tensor(b1[:, :], b1[:, :], hidden_ps[0][:, :], ALU.add).then_inc(u_taken, 1)
            dve.wait_ge(chain, 2)
            dve.wait_ge(u_taken, 1)

            def tiles(i):
                for u in two:
                    t = i * 2 + u
                    if not is_first(i):
                        dve.wait_ge(transposed, t - 1)
                    dve.tensor_scalar(mean[u][:, :], mem.edge_acc[:, cols(t, ECOLS, 0, EDGE_D)],
                                      inv_count[:, bass.ds(t, 1)], None, ALU.mult).then_inc(mean_ready, 1)
                for u in two:
                    t = i * 2 + u
                    dve.wait_ge(products, t + 1)
                    if not is_first(i):
                        dve.wait_ge(hidden_transposed, t - 1)
                    dve.tensor_tensor(hidden[u][:, :], hidden_ps[u][:, :], b1[:, :], ALU.add).then_inc(hidden_ready, 1)
                for u in two:
                    t = i * 2 + u
                    dve.wait_ge(out_products, t + 1)
                    if not is_first(i):
                        dve.wait_ge(x_ready, t - 1)
                    dve.tensor_tensor(out[u][:, :], out_ps[u][:, 0:D], b2[:, :], ALU.add).then_inc(out_ready, 1)
                for u in two:
                    t = i * 2 + u
                    x = mem.x[:, cols(t, D)]
                    dve.wait_ge(out_ready, t + 1)
                    dve.tensor_tensor(x, x, out[u][:, :], ALU.add).then_inc(x_ready, 1)
                for u in two:
                    t = i * 2 + u
                    dve.wait_ge(x_ready, t + 1)
                    dve.sem_inc(ph.turn, 1)
                    dve.bn_stats(halves[:, cols(t, 6)], mem.x[:, cols(t, D)])
            rounds(dve, PAIRS, tiles)


class Attention:

    def __init__(self, nc, ctx, n, heads):
        def sb(name, shape):
            return ctx.enter_context(nc.sbuf_tensor(f"att{n}_{name}", shape, F32))

        self.n, self.heads, self.part = n, heads, D // heads + 1
        self.width = heads * self.part
        self.src = sb("src", [P, BUCKETS * heads])
        self.dst = sb("dst", [P, BUCKETS * heads])
        self.top = sb("top", [P, BUCKETS * heads])
        self.pair = sb("pair", [P, BUCKETS, 2 * heads])
        self.slot_src = sb("slot_src", [P, NT * heads])
        self.least = sb("least", [P, heads])

    def by_head(self, ap):
        return ap.rearrange("p (h c) -> p h c", c=self.part)


def attention_tables(nc, mem, e, att, table, alphas, before=None):
    H, C = att.heads, D // att.heads
    with Phase(nc, f"att_table{att.n}") as ph:
        sb, sem = ph.sb, ph.sem
        two = range(2)
        w_in, a_src, a_dst = sb("w_in", [P, 2, D]), sb("a_src", [P, D]), sb("a_dst", [P, D])
        w = sb("w", [P, 2, D + 2 * H])
        by_a = sb("by_a", [P, 4, D])
        h, turned = ([sb(f"{x}{u}", [P, D]) for u in two] for x in ("h", "turned"))
        row = [sb(f"row{u}", [P, D]) for u in two]
        least_t, least_h, diag = sb("least_t", [H, P]), sb("least_h", [H, 1]), sb("diag", [H, H])
        turned_ps, product_ps = ([ph.psum(f"{x}{u}", [P, 512]) for u in two] for x in ("turned_ps", "product_ps"))
        least_ps, wide_ps = ph.psum("least_ps", [P, 512]), ph.psum("wide_ps", [P, 512])
        (loaded, chain, w_ready, h_ready, transposed, turned_ready, products, row_ready, kept, least_ready,
         least_turned, diag_ready, wide_ready, own, counted, alphas_stored) = (
            sem(x) for x in ("loaded", "chain", "w_ready", "h_ready", "transposed", "turned_ready", "products",
                             "row_ready", "kept", "least_ready", "least_turned", "diag_ready", "wide_ready", "own",
                             "counted", "alphas_stored"))
        stored = [sem(f"stored{u}") for u in two]
        if before is not None:
            bias = sb("bias", [P, D])
            v, neg, ex = ([sb(f"{x}{u}", [P, D]) for u in two] for x in ("v", "neg", "ex"))
            inv = [sb(f"inv{u}", [P, before.heads]) for u in two]
            inv_ready, scaled, v_ready, neg_ready, ex_ready, positive = (
                sem(x) for x in ("inv_ready", "scaled", "v_ready", "neg_ready", "ex_ready", "positive"))
        n_loaded = 3 + (before is not None)
        block = ph.block()

        @block.sync
        def _(sp):
            sp.dma_start(w_in[:, :, :], e["att_w"][:, att.n, :, :]).then_inc(loaded, 16)
            sp.dma_start(a_src[:, :], e["att_src"][att.n].partition_broadcast(P)).then_inc(loaded, 16)
            sp.dma_start(a_dst[:, :], e["att_dst"][att.n].partition_broadcast(P)).then_inc(loaded, 16)
            if before is not None:
                sp.dma_start(bias[:, :], e["att_b"][before.n].partition_broadcast(P)).then_inc(loaded, 16)
            with sp.Fori(0, PAIRS) as i:
                for u in two:
                    sp.wait_ge(row_ready, i * 2 + u + 1)
                    sp.sem_inc(ph.turn, 1)
                    sp.dma_start(table[bass.ds((i * 2 + u) * P, P), :], row[u][:, :]).then_inc(stored[u], 16)
            for u in two:
                sp.wait_ge(stored[u], 16 * PAIRS)
            sp.wait_ge(counted, 1)
            sp.dma_start(alphas.rearrange("(t p) h -> p t h", p=P),
                         att.src[:, :].rearrange("p (t h) -> p t h", h=H),
                         allow_slow_non_contiguous=True).then_inc(alphas_stored, 16)
            sp.wait_ge(alphas_stored, 16)

        @block.tensor
        def _(pe):
            pe.wait_ge(w_ready, 4)

            def tiles(i):
                for u in two:
                    t = i * 2 + u
                    pe.wait_ge(h_ready, t + 1)
                    if not is_first(i):
                        pe.wait_ge(turned_ready, t - 1)
                    for k in two:
                        ins = pe.transpose(turned_ps[u][:, cols(k, P)], h[u][:, cols(k, P)], mem.ident[:, :])
                    ins.then_inc(transposed, 1)
                for u in two:
                    t = i * 2 + u
                    pe.wait_ge(turned_ready, t + 1)
                    if not is_first(i):
                        pe.wait_ge(row_ready, t - 1)
                        pe.wait_ge(kept, (t - 1) * 3)
                    for k in two:
                        ins = pe.matmul(product_ps[u][:, 0:D + 2 * H], turned[u][:, cols(k, P)], w[:, k, :],
                                        start=(k == 0), stop=(k == 1))
                    ins.then_inc(products, 1)
            rounds(pe, PAIRS, tiles)
            pe.wait_ge(least_ready, 1)
            pe.transpose(least_ps[0:H, 0:P], att.least[:, :], mem.ident[:, :]).then_inc(least_turned, 1)
            pe.wait_ge(diag_ready, 1)
            pe.matmul(wide_ps[:, 0:H], mem.ones[0:H, :], diag[:, :], start=True, stop=True).then_inc(wide_ready, 1)

        @block.scalar
        def _(act):
            def tiles(i):
                for u in two:
                    t = i * 2 + u
                    if before is None:
                        if not is_first(i):
                            act.wait_ge(transposed, t - 1)
                            act.sem_inc(ph.turn, 1)
                        act.activation(h[u][:, :], mem.x[:, cols(t, D)], ACT.Relu, bias=mem.shift[:, bass.ds(t, 1)],
                                       scale=mem.rstd[:, bass.ds(t, 1)]).then_inc(h_ready, 1)
                    else:
                        act.wait_ge(neg_ready, t + 1)
                        act.activation(ex[u][:, :], neg[u][:, :], ACT.Exp).then_inc(ex_ready, 1)
                for u in two:
                    t = i * 2 + u
                    act.wait_ge(transposed, t + 1)
                    if not is_first(i):
                        act.wait_ge(products, t - 1)
                    act.copy(turned[u][:, :], turned_ps[u][:, 0:D]).then_inc(turned_ready, 1)
                for u in two:
                    t = i * 2 + u
                    act.wait_ge(products, t + 1)
                    if not is_first(i):
                        act.wait_ge(stored[u], i * 16)
                    act.copy(row[u][:, :], product_ps[u][:, 0:D]).then_inc(row_ready, 1)
            rounds(act, PAIRS, tiles)

        @block.vector
        def _(dve):
            dve.wait_ge(loaded, 16 * n_loaded)
            for k in two:
                dve.tensor_tensor(by_a[:, 2 * k, :], w_in[:, k, :], a_src[:, :], ALU.mult).then_inc(chain, 1)
                dve.tensor_tensor(by_a[:, 2 * k + 1, :], w_in[:, k, :], a_dst[:, :], ALU.mult).then_inc(chain, 1)
                dve.tensor_copy(w[:, k, 0:D], w_in[:, k, :]).then_inc(chain, 1)
            dve.wait_ge(chain, 6)
            for k in two:
                for a in two:
                    dve.tensor_reduce(w[:, k, D + a * H:D + (a + 1) * H],
                                      by_a[:, 2 * k + a, :].rearrange("p (h c) -> p h c", c=C), AX.X, ALU.add
                                      ).then_inc(w_ready, 1)

            def tiles(i):
                if before is not None:
                    CB = D // before.heads
                    for u in two:
                        t = i * 2 + u
                        sums = before.by_head(mem.acc[:, cols(t, ACCW, 0, before.width)])
                        if not is_first(i):
                            dve.wait_ge(scaled, t - 1)
                        dve.sem_inc(ph.turn, 1)
                        dve.reciprocal(inv[u][:, :], sums[:, :, CB]).then_inc(inv_ready, 1)
                    for u in two:
                        t = i * 2 + u
                        sums = before.by_head(mem.acc[:, cols(t, ACCW, 0, before.width)])
                        dve.wait_ge(inv_ready, t + 1)
                        if not is_first(i):
                            dve.wait_ge(h_ready, t - 1)
                        dve.tensor_tensor(v[u][:, :].rearrange("p (h c) -> p h c", c=CB), sums[:, :, 0:CB],
                                          inv[u][:, :].unsqueeze(2).broadcast_to([P, before.heads, CB]),
                                          ALU.mult).then_inc(scaled, 1)
                    for u in two:
                        t = i * 2 + u
                        dve.wait_ge(scaled, t + 1)
                        dve.tensor_tensor(v[u][:, :], v[u][:, :], bias[:, :], ALU.add).then_inc(v_ready, 1)
                    for u in two:
                        t = i * 2 + u
                        dve.wait_ge(v_ready, t + 1)
                        if not is_first(i):
                            dve.wait_ge(ex_ready, t - 1)
                        dve.tensor_scalar(neg[u][:, :], v[u][:, :], 0.0, None, ALU.min).then_inc(neg_ready, 1)
                    for u in two:
                        t = i * 2 + u
                        dve.wait_ge(ex_ready, t + 1)
                        dve.wait_ge(neg_ready, t + 1)
                        dve.tensor_scalar(v[u][:, :], v[u][:, :], 0.0, None, ALU.max).then_inc(positive, 1)
                    for u in two:
                        t = i * 2 + u
                        dve.wait_ge(positive, t + 1)
                        if not is_first(i):
                            dve.wait_ge(transposed, t - 1)
                        dve.scalar_tensor_tensor(h[u][:, :], ex[u][:, :], -1.0, v[u][:, :], ALU.add, ALU.add
                                                 ).then_inc(h_ready, 1)
                for u in two:
                    t = i * 2 + u
                    dve.wait_ge(row_ready, t + 1)
                    dve.tensor_scalar(att.by_head(mem.acc[:, cols(t, ACCW, 0, att.width)])[:, :, 0:C],
                                      product_ps[u][:, 0:D].rearrange("p (h c) -> p h c", c=C), 0.0, None, ALU.add
                                      ).then_inc(kept, 1)
                    for a, of_nodes in enumerate((att.src, att.dst)):
                        dve.tensor_scalar(of_nodes[:, cols(t, H)], product_ps[u][:, D + a * H:D + (a + 1) * H],
                                          0.0, None, ALU.add).then_inc(kept, 1)
            rounds(dve, PAIRS, tiles)
            dve.wait_ge(kept, 3 * BUCKETS)
            acc = mem.acc[:, :].rearrange("p (t c) -> p t c", c=ACCW)
            for head in range(H):
                dve.memset(acc[:, :, head * (C + 1) + C], 1.0)
            dve.tensor_reduce(att.least[:, :], att.src[:, :].rearrange("p (t h) -> p h t", h=H), AX.X, ALU.min
                              ).then_inc(least_ready, 1)
            dve.wait_ge(least_turned, 1)
            dve.tensor_copy(least_t[:, :], least_ps[0:H, 0:P]).then_inc(own, 1)
            dve.wait_ge(own, 1)
            dve.tensor_reduce(least_h[:, :], least_t[:, :], AX.X, ALU.min).then_inc(own, 1)
            dve.wait_ge(own, 2)
            dve.tensor_scalar(diag[:, :], mem.ident[0:H, 0:H], least_h[:, :], None, ALU.mult).then_inc(diag_ready, 1)
            dve.wait_ge(wide_ready, 1)
            dve.tensor_copy(att.least[:, :], wide_ps[:, 0:H]).then_inc(own, 1)
            dve.wait_ge(own, 3)
            src, dst = (a[:, :].rearrange("p (t h) -> p t h", h=H) for a in (att.src, att.dst))
            least = att.least[:, :].unsqueeze(1).broadcast_to([P, BUCKETS, H])
            dve.tensor_tensor(src, src, least, ALU.subtract).then_inc(counted, 1)
            dve.tensor_tensor(dst, dst, least, ALU.add)
            dve.wait_ge(counted, 1)
            dve.tensor_copy(att.top[:, :], att.src[:, :])


def attention_maxima(nc, mem, att, alphas):
    H = att.heads
    per_bank = 4 // H
    banks = GROUP // per_bank
    with Phase(nc, f"maxima{att.n}") as ph:
        sb, sem = ph.sb, ph.sem
        which = sb("which", [P, RING], I32)
        alpha = sb("alpha", [P, RING, H])
        onehot = sb("onehot", [P, 2 * GROUP, P])
        spread = sb("spread", [P, 2 * GROUP, H * P])
        best = sb("best", [P, 2 * GROUP, H])
        score_ps = [ph.psum(f"score_ps{b}", [P, 512]) for b in range(2 * banks)]
        staged = [sem(f"staged{g}") for g in range(GROUPS)]
        landed = [sem(f"landed{g}") for g in range(GROUPS)]
        onehots, spreads, copies, spread_done, best_ready, raised = (
            sem(x) for x in ("onehots", "spreads", "copies", "spread_done", "best_ready", "raised"))
        block = ph.block()

        @block.sync
        def _(sp):
            def stage(i):
                for g in range(GROUPS):
                    if not is_first(i):
                        sp.wait_ge(landed[g], i * (16 * GROUP))
                        sp.sem_inc(ph.turn, 1)
                    sp.dma_start(which[:, cols(g, GROUP)], mem.slot_src[:, cols(i, RING, g * GROUP, GROUP)]
                                 ).then_inc(staged[g], 16)
            rounds(sp, NT // RING, stage)

        @block.gpsimd
        def _(pool):
            def gather(i):
                for g in range(GROUPS):
                    n = Group(i, g)
                    pool.wait_ge(staged[g], (i + 1) * 16)
                    if not is_first(i):
                        pool.wait_ge(copies, n.q - GROUPS + 1)
                        pool.wait_ge(spreads, n.t - RING + GROUP)
                        pool.sem_inc(ph.turn, 1)
                    for k in range(g * GROUP, (g + 1) * GROUP):
                        pool.indirect_dma_start(alpha[:, k, :], None, alphas,
                                                bass.IndirectOffsetOnAxis(which[:, k:k + 1], 0)
                                                ).then_inc(landed[g], 16)
            rounds(pool, NT // RING, gather)

        @block.scalar
        def _(act):
            def step(i, g):
                n = Group(i, g)
                act.wait_ge(landed[n.g], (n.i + 1) * (16 * GROUP))
                act.sem_inc(ph.turn, 1)
                act.copy(att.slot_src[:, cols(i, RING * H, g * GROUP * H, GROUP * H)],
                         alpha[:, cols(g, GROUP), :].rearrange("p k h -> p (k h)")).then_inc(copies, 1)
                for k in range(GROUP):
                    if n.after(2):
                        act.wait_ge(spread_done, n.t + k - 2 * GROUP + 1)
                    for head in range(H):
                        ins = act.activation(spread[:, g % 2 * GROUP + k, cols(head, P)], mem.ident[:, :], ACT.Copy,
                                             scale=alpha[:, g * GROUP + k, head:head + 1])
                    ins.then_inc(spreads, 1)
            over_groups(act, step, 0)

        @block.tensor
        def _(pe):
            def step(i, g):
                n = Group(i, g)
                for k in range(GROUP):
                    pe.wait_ge(onehots, n.t + k + 1)
                    pe.wait_ge(spreads, n.t + k + 1)
                    if n.after(2) and k % per_bank == 0:
                        pe.wait_ge(best_ready, (n.q - 2) * banks + k // per_bank + 1)
                    bank = score_ps[g % 2 * banks + k // per_bank]
                    pe.matmul(bank[:, cols(k % per_bank, H * P)], onehot[:, g % 2 * GROUP + k, :],
                              spread[:, g % 2 * GROUP + k, :], start=True, stop=True).then_inc(spread_done, 1)
            over_groups(pe, step, 0)

        @block.vector
        def _(dve):
            tiles = []

            def step(i, g):
                now, following = Group(i, g), Group(i, g + 1)
                if now.exists and g == 0:
                    tiles[:] = tiles_of(nc, dve, mem.tile_of_dst, now.t, RING)
                for k in range(GROUP):
                    if now.exists and k % per_bank == 0:
                        b = k // per_bank
                        dve.wait_ge(spread_done, now.t + k + per_bank)
                        if now.after(2):
                            dve.wait_ge(raised, now.t - GROUP)
                        dve.tensor_reduce(best[:, g % 2 * GROUP + k:g % 2 * GROUP + k + per_bank, :]
                                          .rearrange("p k h -> p (k h)"),
                                          score_ps[g % 2 * banks + b][:, :].rearrange("p (h e) -> p h e", e=P),
                                          AX.X, ALU.max).then_inc(best_ready, 1)
                    if following.exists:
                        if following.after(2):
                            dve.wait_ge(spread_done, following.t + k - 2 * GROUP + 1)
                        dve.tensor_scalar(onehot[:, following.g % 2 * GROUP + k, :], mem.iota[:, :],
                                          mem.slot_node[:, bass.ds(following.t + k, 1)], None, ALU.is_equal
                                          ).then_inc(onehots, 1)
                    if now.exists:
                        top = att.top[:, cols(tiles[g * GROUP + k], H)]
                        dve.wait_ge(best_ready, now.q * banks + k // per_bank + 1)
                        if now.after(1) or k:
                            dve.wait_ge(raised, now.t + k)
                        dve.tensor_tensor(top, top, best[:, g % 2 * GROUP + k, :], ALU.max).then_inc(raised, 1)
            over_groups(dve, step, 1)


def attention_start(nc, mem, att):
    H = att.heads
    with Phase(nc, f"start{att.n}") as ph:
        own, low, gap, weight = (ph.sb(x, [P, BUCKETS * H]) for x in ("own", "low", "gap", "weight"))
        chain, weights = ph.sem("chain"), ph.sem("weights")
        pair = [att.pair[:, :, a * H:(a + 1) * H] for a in range(2)]
        by_tile = [a[:, :].rearrange("p (t h) -> p t h", h=H) for a in (att.dst, att.top, low, gap)]
        dst, top, low_t, gap_t = by_tile
        block = ph.block()

        @block.scalar
        def _(act):
            act.wait_ge(chain, 5)
            act.activation(weight[:, :], gap[:, :], ACT.Exp).then_inc(weights, 1)

        @block.vector
        def _(dve):
            dve.tensor_tensor(own[:, :], att.src[:, :], att.dst[:, :], ALU.add).then_inc(chain, 1)
            dve.tensor_tensor(att.top[:, :], att.top[:, :], att.dst[:, :], ALU.add).then_inc(chain, 1)
            dve.tensor_copy(pair[0], dst)
            dve.wait_ge(chain, 2)
            dve.scalar_tensor_tensor(low[:, :], own[:, :], SLOPE, own[:, :], ALU.mult, ALU.max).then_inc(chain, 1)
            dve.scalar_tensor_tensor(pair[1], top, SLOPE, top, ALU.mult, ALU.max).then_inc(chain, 1)
            dve.wait_ge(chain, 4)
            dve.tensor_tensor(gap_t, low_t, pair[1], ALU.subtract).then_inc(chain, 1)
            dve.wait_ge(weights, 1)
            if att.width == ACCW:
                sums = mem.acc[:, :].rearrange("p (t c) -> p t c", c=att.part)
                dve.tensor_tensor(sums, sums, weight[:, :].unsqueeze(2).broadcast_to([P, BUCKETS * H, att.part]),
                                  ALU.mult)
            else:
                sums = mem.acc[:, :].rearrange("p (t c) -> p t c", c=ACCW)[:, :, 0:att.width]
                dve.tensor_tensor(sums, sums, weight[:, :].unsqueeze(2).broadcast_to([P, BUCKETS, att.width]),
                                  ALU.mult)


def attend(nc, mem, att, table):
    H, C, W = att.heads, D // att.heads, att.width
    by_row = H > 1
    with Phase(nc, f"attend{att.n}") as ph:
        sb, sem = ph.sb, ph.sem
        which = sb("which", [P, RING], I32)
        rows = sb("rows", [P, RING, D if by_row else W])
        onehot = sb("onehot", [P, RING, P])
        hot_t = sb("hot_t", [P, 2, GROUP * P])
        pair = sb("pair", [P, 2, GROUP, 2 * H])
        score, low, gap, cut = (sb(x, [P, GROUP * H]) for x in ("score", "low", "gap", "cut"))
        if by_row:
            weighed = sb("weighed", [P, 2 * GROUP, W])
        else:
            weighed = sb("weighed", [P, 2 * GROUP, P])
            weight = sb("weight", [P, 2 * GROUP])
        turn_ps = [ph.psum(f"turn_ps{b}", [P, 512]) for b in range(2)]
        look_ps = [ph.psum(f"look_ps{b}", [P, 512]) for b in range(2)]
        sums_ps = [ph.psum(f"sums_ps{k}", [P, 512]) for k in range(GROUP)]
        staged = [sem(f"staged{g}") for g in range(GROUPS)]
        landed = [sem(f"landed{g}") for g in range(GROUPS)]
        (onehots, turned, hot_t_ready, pairs, looked, score_ready, low_ready, gap_ready, cut_ready, weights,
         weighings, products, added, filled) = (
            sem(x) for x in ("onehots", "turned", "hot_t_ready", "pairs", "looked", "score_ready", "low_ready",
                             "gap_ready", "cut_ready", "weights", "weighings", "products", "added", "filled"))
        block = ph.block()

        @block.sync
        def _(sp):
            def stage(i):
                for g in range(GROUPS):
                    if not is_first(i):
                        sp.wait_ge(landed[g], i * (16 * GROUP))
                        sp.sem_inc(ph.turn, 1)
                    sp.dma_start(which[:, cols(g, GROUP)], mem.slot_src[:, cols(i, RING, g * GROUP, GROUP)]
                                 ).then_inc(staged[g], 16)
            rounds(sp, NT // RING, stage)

        @block.gpsimd
        def _(pool):
            used = weighings if by_row else products

            def gather(i):
                for g in range(GROUPS):
                    pool.wait_ge(staged[g], (i + 1) * 16)
                    if not is_first(i):
                        pool.wait_ge(used, (i - 1) * RING + (g + 1) * GROUP)
                        pool.sem_inc(ph.turn, 1)
                    for k in range(g * GROUP, (g + 1) * GROUP):
                        pool.indirect_dma_start(rows[:, k, 0:D], None, table,
                                                bass.IndirectOffsetOnAxis(which[:, k:k + 1], 0)
                                                ).then_inc(landed[g], 16)
            rounds(pool, NT // RING, gather)

        @block.scalar
        def _(act):
            def pairs_of(n):
                tiles = tiles_of(nc, act, mem.tile_of_dst, n.t, GROUP)
                if n.after(2):
                    act.wait_ge(looked, n.q - 1)
                    act.sem_inc(ph.turn, 1)
                for k in range(GROUP):
                    ins = act.copy(pair[:, n.g % 2, k, :], att.pair[:, bass.ds(tiles[k], 1), :]
                                   .rearrange("p t h -> p (t h)"))
                ins.then_inc(pairs, 1)

            def weights_of(n):
                act.wait_ge(cut_ready, n.q + 1)
                if n.after(2):
                    act.wait_ge(products, n.t - GROUP)
                if by_row:
                    into = weighed[:, cols(n.g % 2, GROUP), :].rearrange("p k (h c) -> p (k h) c", c=C + 1)[:, :, C]
                else:
                    into = weight[:, cols(n.g % 2, GROUP)]
                act.activation(into, cut[:, :], ACT.Exp).then_inc(weights, 1)

            def turned_of(n):
                act.wait_ge(turned, n.t + GROUP)
                if n.after(2):
                    act.wait_ge(looked, n.q - 1)
                act.copy(hot_t[:, n.g % 2, :], turn_ps[n.g % 2][:, :]).then_inc(hot_t_ready, 1)

            def step(i, g):
                if Group(i, g + 4).exists:
                    pairs_of(Group(i, g + 4))
                if Group(i, g + 2).exists:
                    weights_of(Group(i, g + 2))
                if Group(i, g + 4).exists:
                    turned_of(Group(i, g + 4))
            over_groups(act, step, 4)

        @block.tensor
        def _(pe):
            if not by_row:
                pe.wait_ge(filled, 1)

            def step(i, g):
                sums, looks, turns = Group(i, g + 1), Group(i, g + 3), Group(i, g + 4)
                if looks.exists:
                    pe.wait_ge(hot_t_ready, looks.q + 1)
                    pe.wait_ge(pairs, looks.q + 1)
                    if looks.after(2):
                        pe.wait_ge(gap_ready, looks.q - 1)
                    for k in range(GROUP):
                        ins = pe.matmul(look_ps[looks.g % 2][:, cols(k, 2 * H)], hot_t[:, looks.g % 2, cols(k, P)],
                                        pair[:, looks.g % 2, k, :], start=True, stop=True)
                    ins.then_inc(looked, 1)
                for k in range(GROUP):
                    if turns.exists:
                        pe.wait_ge(onehots, turns.t + k + 1)
                        if turns.after(2) and k == 0:
                            pe.wait_ge(hot_t_ready, turns.q - 1)
                        pe.transpose(turn_ps[turns.g % 2][:, cols(k, P)], onehot[:, turns.g * GROUP + k, :],
                                     mem.ident[:, :]).then_inc(turned, 1)
                    if sums.exists:
                        if not by_row and k == 0:
                            pe.wait_ge(landed[sums.g], (sums.i + 1) * (16 * GROUP))
                        pe.wait_ge(weighings, sums.t + k + 1)
                        if sums.after(1):
                            pe.wait_ge(added, sums.t + k - GROUP + 1)
                        row, hot = sums.g * GROUP + k, sums.g % 2 * GROUP + k
                        left, right = ((onehot[:, row, :], weighed[:, hot, :]) if by_row else
                                       (weighed[:, hot, :], rows[:, row, :]))
                        pe.matmul(sums_ps[k][:, 0:W], left, right, start=True, stop=True).then_inc(products, 1)
            over_groups(pe, step, 4)

        @block.vector
        def _(dve):
            tiles = []
            if not by_row:
                dve.memset(rows[:, :, D], 1.0).then_inc(filled, 1)

            def add(n, k):
                into = mem.acc[:, cols(tiles[n.g * GROUP + k], ACCW, 0, W)]
                dve.wait_ge(products, n.t + k + 1)
                if n.after(1) or k:
                    dve.wait_ge(added, n.t + k)
                dve.tensor_tensor(into, into, sums_ps[k][:, 0:W], ALU.add).then_inc(added, 1)

            def onehot_of(n, k):
                if n.after(4):
                    dve.wait_ge(products, n.t + k - RING + 1)
                dve.tensor_scalar(onehot[:, n.g * GROUP + k, :], mem.iota[:, :], mem.slot_node[:, bass.ds(n.t + k, 1)],
                                  None, ALU.is_equal).then_inc(onehots, 1)

            def weigh(n, k):
                dve.wait_ge(weights, n.q + 1)
                if by_row:
                    if k == 0:
                        dve.wait_ge(landed[n.g], (n.i + 1) * (16 * GROUP))
                    into = att.by_head(weighed[:, n.g % 2 * GROUP + k, :])
                    dve.tensor_tensor(into[:, :, 0:C],
                                      rows[:, n.g * GROUP + k, :].rearrange("p (h c) -> p h c", c=C),
                                      into[:, :, C:C + 1].broadcast_to([P, H, C]), ALU.mult).then_inc(weighings, 1)
                else:
                    if n.after(2):
                        dve.wait_ge(products, n.t + k - 2 * GROUP + 1)
                    dve.tensor_scalar(weighed[:, n.g % 2 * GROUP + k, :], mem.iota[:, :],
                                      mem.slot_node[:, bass.ds(n.t + k, 1)],
                                      weight[:, n.g % 2 * GROUP + k:n.g % 2 * GROUP + k + 1],
                                      ALU.is_equal, ALU.mult).then_inc(weighings, 1)

            def gaps_of(n, k):
                look = look_ps[n.g % 2][:, 0:GROUP * 2 * H].rearrange("p (k c) -> p k c", k=GROUP)
                by_tile = [a[:, :].rearrange("p (k h) -> p k h", h=H) for a in (score, low, gap)]
                if k == 0:
                    dve.wait_ge(looked, n.q + 1)
                    if n.after(1):
                        dve.wait_ge(low_ready, n.q)
                    slots = att.slot_src[:, cols(n.i, RING * H, n.g * GROUP * H, GROUP * H)]
                    dve.tensor_tensor(by_tile[0], slots.rearrange("p (k h) -> p k h", h=H), look[:, :, 0:H], ALU.add
                                      ).then_inc(score_ready, 1)
                if k == 1:
                    dve.wait_ge(score_ready, n.q + 1)
                    if n.after(1):
                        dve.wait_ge(gap_ready, n.q)
                    dve.scalar_tensor_tensor(low[:, :], score[:, :], SLOPE, score[:, :], ALU.mult, ALU.max
                                             ).then_inc(low_ready, 1)
                if k == 2:
                    dve.wait_ge(low_ready, n.q + 1)
                    if n.after(1):
                        dve.wait_ge(cut_ready, n.q)
                    dve.tensor_tensor(by_tile[2], by_tile[1], look[:, :, H:2 * H], ALU.subtract).then_inc(gap_ready, 1)

            def cut_of(n):
                dve.wait_ge(gap_ready, n.q + 1)
                if n.after(1):
                    dve.wait_ge(weights, n.q)
                dve.tensor_scalar(cut[:, :], gap[:, :], 0.0, None, ALU.min).then_inc(cut_ready, 1)

            def step(i, g):
                now = Group(i, g)
                if now.exists and g == 0:
                    tiles[:] = tiles_of(nc, dve, mem.tile_of_dst, now.t, RING)
                for k in range(GROUP):
                    if Group(i, g + 2).exists:
                        gaps_of(Group(i, g + 2), k)
                    if now.exists:
                        add(now, k)
                    if Group(i, g + 4).exists:
                        onehot_of(Group(i, g + 4), k)
                    if k == 2 and Group(i, g + 2).exists:
                        cut_of(Group(i, g + 2))
                    if Group(i, g + 1).exists:
                        weigh(Group(i, g + 1), k)
            over_groups(dve, step, 4)


def finish(nc, mem, e, att, out):
    with Phase(nc, "finish") as ph:
        bias, inv = ph.sb("bias", [P, D]), ph.sb("inv", [P, BUCKETS])
        v = [ph.sb(f"v{u}", [P, D]) for u in range(2)]
        loaded, inv_ready, scaled, biased, ready = (ph.sem(x) for x in ("loaded", "inv_ready", "scaled", "biased", "ready"))
        stored = [ph.sem(f"stored{u}") for u in range(2)]
        block = ph.block()

        @block.sync
        def _(sp):
            sp.dma_start(bias[:, :], e["att_b"][att.n].partition_broadcast(P)).then_inc(loaded, 16)
            with sp.Fori(0, PAIRS) as i:
                for u in range(2):
                    t = i * 2 + u
                    sp.wait_ge(ready, t + 1)
                    sp.sem_inc(ph.turn, 1)
                    sp.dma_start(out[bass.ds(t * P, P), :], v[u][:, :]).then_inc(stored[u], 16)
            for u in range(2):
                sp.wait_ge(stored[u], 16 * PAIRS)

        @block.vector
        def _(dve):
            dve.wait_ge(loaded, 16)
            dve.reciprocal(inv[:, :], mem.acc[:, :].rearrange("p (t c) -> p t c", c=ACCW)[:, :, D]).then_inc(inv_ready, 1)
            dve.wait_ge(inv_ready, 1)

            def tiles(i):
                for u in range(2):
                    t = i * 2 + u
                    if not is_first(i):
                        dve.wait_ge(stored[u], i * 16)
                    dve.tensor_scalar(v[u][:, :], mem.acc[:, cols(t, ACCW, 0, D)], inv[:, bass.ds(t, 1)], None,
                                      ALU.mult).then_inc(scaled, 1)
                for u in range(2):
                    t = i * 2 + u
                    dve.wait_ge(scaled, t + 1)
                    dve.tensor_tensor(v[u][:, :], v[u][:, :], bias[:, :], ALU.add).then_inc(biased, 1)
                for u in range(2):
                    t = i * 2 + u
                    dve.wait_ge(biased, t + 1)
                    dve.tensor_tensor(v[u][:, :], v[u][:, :], mem.x[:, cols(t, D)], ALU.add).then_inc(ready, 1)
            rounds(dve, PAIRS, tiles)


def build(nc, e, out):
    def dram(name, shape, dt=F32):
        return nc.dram_tensor(name, shape, dt).ap()

    slots, edge_rows = dram("slots", (SLOTS, 4), I32), dram("edge_rows", (SLOTS, 1 + ECOLS))
    rel_table, table = dram("rel_table", (NPAD * REL, D)), dram("table", (NPAD, D))
    with ExitStack() as ctx:
        mem = Mem(nc, ctx)
        constants(nc, mem)
        load_nodes(nc, mem, e)
        build_slots(nc, mem, e, {"slots": slots})
        with ExitStack() as inner:
            halves = inner.enter_context(nc.sbuf_tensor("halves", [P, BUCKETS * 6], F32))
            first_stats(nc, mem, halves)
            finish_stats(nc, mem, "stats0", halves)
            for layer in range(3):
                relational_tables(nc, mem, e, layer, rel_table)
                aggregate(nc, mem, f"rel_sum{layer}", rel_table, mem.slot_rel, degree=(layer == 0))
            relational_end(nc, mem, halves)
            finish_stats(nc, mem, "stats1", halves)
            node_table(nc, mem, table)
            sort_edge_rows(nc, mem, e, {"edge_rows": edge_rows})
            aggregate(nc, mem, "mean_sum", table, mem.slot_src, weighted=True, edge_rows=edge_rows)
            conv_layers(nc, mem, e, table)
            mlp_layer(nc, mem, e, 0, halves)
            mlp_layer(nc, mem, e, 1, halves)
            finish_stats(nc, mem, "stats2", halves)
            edge_layer(nc, mem, e, halves)
            finish_stats(nc, mem, "stats3", halves)
        before = None
        for n, heads in enumerate((HEADS, 1)):
            att = Attention(nc, ctx, n, heads)
            alphas = dram(f"alphas{n}", (NPAD, heads))
            attention_tables(nc, mem, e, att, table, alphas, before)
            attention_maxima(nc, mem, att, alphas)
            attention_start(nc, mem, att)
            attend(nc, mem, att, table)
            before = att
        finish(nc, mem, e, before, out)


def lay_out(inputs):
    def f32(name):
        return np.ascontiguousarray(inputs[name])

    def edges(name, fill):
        a = np.asarray(inputs[name])
        out = np.full((EPAD,) + a.shape[1:], fill, a.dtype)
        out[:N_EDGES] = a
        return out.reshape((P, COLS) + a.shape[1:])

    def split_rows(w):
        w = np.asarray(w)
        w = w.reshape(w.shape[:-2] + (w.shape[-2] // P, P, w.shape[-1]))
        return np.ascontiguousarray(np.moveaxis(w, -2, 0))

    x = np.zeros((NPAD, D), np.float32)
    x[:N_NODES] = inputs["x"]
    rel = np.concatenate([np.moveaxis(np.asarray(inputs["L0_gnn_weights"]), 1, 2).reshape(3, D, REL * D),
                          np.asarray(inputs["L0_gnn_roots"])], axis=2)
    conv = np.stack([np.moveaxis(np.asarray(inputs[n]), (0, 1, 2), (1, 2, 0)).reshape(D, 4 * D)
                     for n in ("L1_gnn_W_rel", "L1_gnn_W_root")])
    w = {
        "x": x,
        "src": edges("src", REAL * P), "dst": edges("dst", REAL * P), "rel": edges("edge_type_8", 0),
        "weight": edges("edge_weight", 0), "attr": edges("edge_attr_64", 0),
        "rel_w": split_rows(rel),
        "rel_b": f32("L0_gnn_biases"),
        "conv_w": split_rows(conv),
        "conv_b": f32("L1_gnn_b_rel").reshape(1, -1), "conv_g": f32("L1_gnn_ln_g").reshape(1, -1),
        "conv_n": f32("L1_gnn_ln_b").reshape(1, -1),
        "mlp_w": split_rows(np.stack([np.asarray(inputs["L1_gnn_W1"]).T, np.asarray(inputs["L1_gnn_W2"]).T])),
        "mlp_v": np.stack([np.asarray(inputs["L1_gnn_" + n]) for n in ("b1", "mg1", "mb1", "b2", "mg2", "mb2")]),
        "edge_w": split_rows(np.asarray(inputs["L2_gnn_W1"])[:D]),
        "edge_we": np.ascontiguousarray(np.asarray(inputs["L2_gnn_W1"])[D:D + EDGE_D]),
        "edge_wu": np.ascontiguousarray(np.asarray(inputs["L2_gnn_W1"])[D + EDGE_D:]),
        "edge_u": np.ascontiguousarray(np.asarray(inputs["L2_gnn_u"])[0:1].T),
        "edge_b1": f32("L2_gnn_b1").reshape(1, -1),
        "edge_w2": split_rows(inputs["L2_gnn_W2"]), "edge_b2": f32("L2_gnn_b2").reshape(1, -1),
        "att_w": split_rows(np.stack([np.asarray(inputs["L3_gnn_W1"]), np.asarray(inputs["L3_gnn_W2"])])),
        "att_src": np.stack([np.asarray(inputs[f"L3_gnn_a_src{n}"]).reshape(-1) for n in (1, 2)]),
        "att_dst": np.stack([np.asarray(inputs[f"L3_gnn_a_dst{n}"]).reshape(-1) for n in (1, 2)]),
        "att_b": np.stack([np.asarray(inputs[f"L3_gnn_b{n}"]) for n in (1, 2)]),
    }
    return w


def kernel(**inputs):
    import concourse.bacc as bacc
    from concourse.bass_utils import run_bass_kernel_spmd

    nc = bacc.Bacc("TRN2", target_bir_lowering=False, num_devices=1)
    arrays = lay_out(inputs)
    args = {n: nc.dram_tensor(f"in_{n}", a.shape, mybir.dt.from_np(a.dtype), kind="ExternalInput").ap()
            for n, a in arrays.items()}
    out = nc.dram_tensor("out", (NPAD, D), F32, kind="ExternalOutput").ap()
    build(nc, args, out)
    result = run_bass_kernel_spmd(nc, [{f"in_{n}": a for n, a in arrays.items()}], core_ids=[0])
    return result.results[0]["out"][:N_NODES]
```

```python
from contextlib import ExitStack

import numpy as np
import concourse.bass as bass
from concourse import mybir

ALU = mybir.AluOpType
ACT = mybir.ActivationFunctionType
AX = mybir.AxisListType
F32 = mybir.dt.float32
I32 = mybir.dt.int32

P = 128
N_NODES = 6250
N_EDGES = 100000
D = 256
REL = 8
EDGE_D = 64
HEADS = 4
EPS = 1e-5
SLOPE = 0.2

BUCKETS = 50
NPAD = BUCKETS * P
GROUP = 4
GROUPS = 4
RING = GROUP * GROUPS
COLS = -(-(-(-N_EDGES // P)) // RING) * RING
EPAD = COLS * P
REAL = -(-N_NODES // P)
NT = -(-((N_EDGES - REAL) // P + REAL + (EPAD - N_EDGES) // P) // RING) * RING
SLOTS = NT * P
ACCW = 260
ECOLS = EDGE_D + 1
NO_NODE = 255.0


def cols(t, width, lo=0, n=None):
    return bass.ds(t * width + lo, width if n is None else n)


def tiles_of(nc, engine, tile_of, i, first, n):
    _, values = nc.values_load_multi_w_load_instructions(
        tile_of[0:1, bass.ds(i, 1), first:first + n].rearrange("p i k -> p (i k)"), engines=(engine.engine,),
        min_val=0, max_val=BUCKETS - 1,
        skip_runtime_bounds_check_because="a slot tile's node tile is a sum of REAL = BUCKETS - 1 zeros and ones")
    return values


def rounds(engine, n, body):
    body(0)
    with engine.Fori(1, n) as i:
        body(i)


def is_first(i):
    return isinstance(i, int) and i == 0


class Phase:

    def __init__(self, nc, name):
        self.nc, self.name, self.ctx, self.sems = nc, name, ExitStack(), []

    def __enter__(self):
        self.turn = self.sem("turn")
        return self

    def __exit__(self, kind, *rest):
        self.ctx.close()
        if kind is None and self.sems:
            self.nc.clear_and_free_semaphores(self.sems)
            self.nc.all_engine_barrier()

    def sb(self, name, shape, dt=F32):
        return self.ctx.enter_context(self.nc.sbuf_tensor(f"{self.name}_{name}", shape, dt))

    def psum(self, name, shape):
        return self.ctx.enter_context(self.nc.psum_tensor(f"{self.name}_{name}", shape, F32))

    def sem(self, name):
        self.sems.append(self.nc.alloc_semaphore(f"{self.name}_{name}"))
        return self.sems[-1]

    def block(self):
        return self.ctx.enter_context(self.nc.Block())


class Mem:

    def __init__(self, nc, ctx):
        def sb(name, shape, dt=F32):
            return ctx.enter_context(nc.sbuf_tensor(name, shape, dt))

        self.x = sb("x_nodes", [P, BUCKETS * D])
        self.acc = sb("acc", [P, BUCKETS * ACCW])
        self.slot_row = sb("slot_row", [P, NT], I32)
        self.slot_weight = sb("slot_weight", [P, NT])
        self.slot_node = sb("slot_node", [P, NT + 2 * GROUP])
        self.tile_of = sb("tile_of", [1, NT // RING, 2 * RING], I32)
        self.iota = sb("iota_row", [P, P])
        self.ident = sb("ident", [P, P])
        self.ones = sb("ones", [P, P])
        self.rstd = sb("rstd", [P, BUCKETS])
        self.shift = sb("shift", [P, BUCKETS])
        self.inv_deg = sb("inv_deg", [P, BUCKETS])
        self.eps = sb("eps", [P, 1])


def constants(nc, mem):
    with Phase(nc, "consts") as ph:
        made = ph.sem("made")
        block = ph.block()

        @block.gpsimd
        def _(pool):
            pool.iota(mem.iota[:, :], [[1, P]], base=0, channel_multiplier=0,
                      allow_small_or_imprecise_dtypes=True).then_inc(made, 1)
            pool.memset(mem.ident[:, :], 0.0).then_inc(made, 1)
            pool.memset(mem.eps[:, :], EPS).then_inc(made, 1)
            pool.wait_ge(made, 3)
            pool.affine_select(out=mem.ident[:, :], in_=mem.ident[:, :], compare_op=ALU.not_equal, fill=1.0,
                               base=0, pattern=[[-1, P]], channel_multiplier=1).then_inc(made, 1)

        @block.vector
        def _(dve):
            dve.memset(mem.ones[:, :], 1.0)
            dve.memset(mem.acc[:, :], 0.0)
            dve.memset(mem.slot_node[:, NT:NT + 2 * GROUP], NO_NODE)


class TileSort:

    def __init__(self, nc, ctx, name, key_dram, tile_of, node=None):
        def sb(what, shape, dt=F32):
            return ctx.enter_context(nc.sbuf_tensor(f"{name}_{what}", shape, dt))

        self.name, self.key_dram, self.tile_of = name, key_dram, tile_of
        self.bucket = sb("bucket", [P, COLS])
        self.addr = self.bucket[:, :].bitcast(I32)
        self.node = sb("node", [P, COLS])[:, :] if node is None else node
        self.number, self.seed = sb("number", [P, BUCKETS]), sb("seed", [P, BUCKETS])
        self.place = sb("place", [P, COLS])


def count_edges(nc, mem, sort, empty_rows=None):
    with Phase(nc, f"{sort.name}_count") as ph:
        sb, sem = ph.sb, ph.sem
        key, low_bits = sb("key", [P, COLS], I32), sb("low_bits", [P, COLS], I32)
        junk = [sb(f"junk{u}", [P, COLS]) for u in range(2)]
        count, tiles, ends, zero = (sb(n, [P, BUCKETS]) for n in ("count", "tiles", "ends", "zero"))
        total_i, before = sb("total_i", [P, BUCKETS], I32), sb("before", [P, P])
        end_col, ends_own = sb("end_col", [P, 1]), sb("ends_own", [P, BUCKETS])
        tile_no, past = sb("tile_no", [REAL, NT]), sb("past", [REAL, NT])
        offset_ps = ph.psum("offset_ps", [P, BUCKETS])
        total_ps = ph.psum("total_ps", [P, BUCKETS])
        tile_ps = [ph.psum(f"tile_ps{h}", [1, NT // 2]) for h in range(2)]
        loaded, consts, chain, counted, offsets, past_ready, tiles_ready, cleared, filled = (
            sem(n) for n in ("loaded", "consts", "chain", "counted", "offsets", "past_ready", "tiles_ready",
                             "cleared", "filled"))
        pieces = 16
        if empty_rows is not None:
            empty = sb("empty", [P, NT // pieces, empty_rows.shape[1]])
        block = ph.block()

        @block.sync
        def _(sp):
            sp.dma_start(key[:, :], sort.key_dram).then_inc(loaded, 16)
            if empty_rows is not None:
                sp.wait_ge(cleared, 2)
                by_tile = empty_rows.rearrange("(p t) c -> p t c", p=P)
                for n in range(pieces):
                    sp.dma_start(by_tile[:, cols(n, NT // pieces), :], empty[:, :, :]).then_inc(filled, 16)
                sp.wait_ge(filled, 16 * pieces)

        @block.gpsimd
        def _(pool):
            pool.iota(sort.number[:, :], [[1, BUCKETS]], base=0, channel_multiplier=0,
                      allow_small_or_imprecise_dtypes=True).then_inc(consts, 1)
            pool.iota(tile_no[:, :], [[1, NT]], base=0, channel_multiplier=0,
                      allow_small_or_imprecise_dtypes=True).then_inc(consts, 1)
            pool.memset(zero[:, :], 0.0).then_inc(consts, 1)
            pool.memset(before[:, :], 1.0).then_inc(consts, 1)
            pool.wait_ge(consts, 4)
            pool.affine_select(out=before[:, :], in_=before[:, :], compare_op=ALU.is_gt, fill=0.0,
                               base=0, pattern=[[1, P]], channel_multiplier=-1).then_inc(consts, 1)

        @block.tensor
        def _(pe):
            pe.wait_ge(consts, 5)
            pe.wait_ge(counted, BUCKETS)
            pe.matmul(offset_ps[:, :], before[:, :], count[:, :], start=True, stop=True).then_inc(offsets, 1)
            pe.matmul(total_ps[:, :], mem.ones[:, :], count[:, :], start=True, stop=True).then_inc(offsets, 1)
            pe.wait_ge(past_ready, 1)
            for h in range(2):
                pe.matmul(tile_ps[h][:, :], mem.ones[0:REAL, 0:1], past[:, cols(h, NT // 2)],
                          start=True, stop=True).then_inc(tiles_ready, 1)

        @block.vector
        def _(dve):
            steps = [0]

            def link(ins):
                steps[0] += 1
                ins.then_inc(chain, 1)
                dve.wait_ge(chain, steps[0])

            if empty_rows is not None:
                dve.memset(empty[:, :, 1:], 0.0).then_inc(cleared, 1)
                dve.memset(empty[:, :, 0], NO_NODE).then_inc(cleared, 1)
            dve.wait_ge(loaded, 16)
            dve.wait_ge(consts, 5)
            link(dve.tensor_scalar(low_bits[:, :], key[:, :], 7, None, ALU.logical_shift_right))
            link(dve.tensor_copy(sort.bucket[:, :], low_bits[:, :]))
            link(dve.tensor_scalar(low_bits[:, :], key[:, :], P - 1, None, ALU.bitwise_and))
            link(dve.tensor_copy(sort.node, low_bits[:, :]))

            def count_of(b, u):
                dve.tensor_scalar(junk[u][:, :], sort.bucket[:, :], sort.number[:, bass.ds(b, 1)], None,
                                  ALU.is_equal, ALU.add, accum_out=count[:, bass.ds(b, 1)]).then_inc(counted, 1)
            for u in range(2):
                count_of(u, u)
            with dve.Fori(1, BUCKETS // 10) as i:
                for n in range(10):
                    dve.wait_ge(counted, i * 10 + n - 9)
                    count_of(i * 10 + n - 8, n % 2)
            for b in range(BUCKETS - 8, BUCKETS):
                dve.wait_ge(counted, b - 1)
                count_of(b, b % 2)
            dve.wait_ge(offsets, 2)
            link(dve.tensor_scalar(total_i[:, :], total_ps[:, :], float(P - 1), None, ALU.add))
            link(dve.tensor_scalar(total_i[:, :], total_i[:, :], 7, None, ALU.logical_shift_right))
            link(dve.tensor_copy(tiles[:, :], total_i[:, :]))
            link(dve.tensor_tensor_scan(ends[:, :], tiles[:, :], zero[:, :], 0.0, ALU.add, ALU.add))
            seed = sort.seed
            link(dve.tensor_tensor(seed[:, :], ends[:, :], tiles[:, :], ALU.subtract))
            link(dve.tensor_scalar(seed[:, :], seed[:, :], float(P), -1.0, ALU.mult, ALU.add))
            link(dve.tensor_tensor(seed[:, :], seed[:, :], offset_ps[:, :], ALU.add))
            link(dve.tensor_tensor_reduce(ends_own[:, :], ends[:, :], mem.ident[:, 0:BUCKETS], 1.0, 0.0,
                                          ALU.mult, ALU.add, end_col[:, :]))
            dve.tensor_scalar(past[:, :], tile_no[:, :], end_col[0:REAL, :], None, ALU.is_ge).then_inc(past_ready, 1)
            for h in range(2):
                dve.wait_ge(tiles_ready, h + 1)
                half = NT // RING // 2
                dve.tensor_copy(sort.tile_of[:, cols(h, half), :],
                                tile_ps[h][:, :].rearrange("p (i k) -> p i k", k=RING))


class Ranks:

    def __init__(self, ph, sort, lanes):
        self.sort, self.lanes = sort, lanes
        self.mask = [ph.sb(f"mask{u}", [P, COLS], I32) for u in range(lanes)]
        self.rank = [ph.sb(f"rank{u}", [P, COLS]) for u in range(lanes)]
        self.stepped = [ph.sem(f"stepped{u}") for u in range(lanes)]
        self.placed = ph.sem("placed")

    def begin(self, dve):
        dve.memset(self.sort.place[:, :], 0.0).then_inc(self.placed, 1)

    def step(self, dve, turn, lane, step):
        sort, b = self.sort, turn * self.lanes + lane
        mask, rank, stepped = self.mask[lane][:, :], self.rank[lane][:, :], self.stepped[lane]
        place = sort.place[:, :]
        if step > 0:
            dve.wait_ge(stepped, turn * 3 + step)
        if step == 0:
            ins = dve.tensor_scalar(mask, sort.bucket[:, :], sort.number[:, bass.ds(b, 1)], None, ALU.is_equal)
        if step == 1:
            ins = dve.tensor_tensor_scan(rank, mask, sort.bucket[:, :], sort.seed[:, bass.ds(b, 1)],
                                         ALU.add, ALU.bypass)
        if step == 2:
            ins = dve.tensor_tensor(rank, rank, mask, ALU.mult)
        if step == 3:
            dve.wait_ge(self.placed, b + 1)
            ins = dve.tensor_tensor(place, place, rank, ALU.add)
        ins.then_inc(stepped if step < 3 else self.placed, 1)


def rank_edges(nc, sort):
    with Phase(nc, f"{sort.name}_rank") as ph:
        lanes = 5
        ranks = Ranks(ph, sort, lanes)
        block = ph.block()

        @block.vector
        def _(dve):
            ranks.begin(dve)
            with dve.Fori(0, BUCKETS // lanes) as turn:
                for step in range(4):
                    for lane in range(lanes):
                        ranks.step(dve, turn, lane, step)


def end_sort(nc, sort):
    with Phase(nc, f"{sort.name}_end") as ph:
        slot, low_bits = ph.sb("slot", [P, COLS], I32), ph.sb("low_bits", [P, COLS], I32)
        chain = ph.sem("chain")
        block = ph.block()

        @block.vector
        def _(dve):
            dve.tensor_copy(slot[:, :], sort.place[:, :]).then_inc(chain, 1)
            dve.wait_ge(chain, 1)
            dve.tensor_scalar(low_bits[:, :], slot[:, :], P - 1, None, ALU.bitwise_and).then_inc(chain, 1)
            dve.wait_ge(chain, 2)
            dve.tensor_scalar(slot[:, :], slot[:, :], 7, None, ALU.logical_shift_right).then_inc(chain, 1)
            dve.wait_ge(chain, 3)
            dve.scalar_tensor_tensor(sort.addr, low_bits[:, :], float(NT), slot[:, :], ALU.mult, ALU.add)


HALF = RING // 2


class Scatter:

    def __init__(self, ph, table, addr, first, n_rounds, info=None, attr=None, node=None):
        self.turn, self.table, self.addr, self.first, self.rounds = ph.turn, table, addr, first, n_rounds
        self.info, self.attr, self.node = info, attr, node
        self.width = table.shape[1]
        self.where = ph.sb("where", [P, RING], I32)
        self.rows = ph.sb("edge_rows", [P, RING, self.width], table.dtype)
        self.staged = [ph.sem(f"staged{h}") for h in range(2)]
        self.written = [ph.sem(f"written{h}") for h in range(2)]
        self.copied = ph.sem("copied")

    def load_attributes(self, sp, i):
        for h in range(2):
            if not is_first(i):
                sp.wait_ge(self.written[h], i * (16 * HALF))
                sp.sem_inc(self.turn, 1)
            sp.dma_start(self.rows[:, cols(h, HALF), 1:1 + EDGE_D],
                         self.attr[:, cols(i + self.first, RING, h * HALF, HALF), :]).then_inc(self.staged[h], 16)

    def write(self, pool):
        if self.node is not None:
            pool.memset(self.rows[:, :, self.width - 1], 1.0).then_inc(self.copied, 1)
            pool.wait_ge(self.copied, 1)
            pool.sem_inc(self.turn, 1)
        ones = 0 if self.node is None else 1

        def one_round(i):
            for h in range(2):
                if not is_first(i):
                    pool.wait_ge(self.written[h], i * (16 * HALF))
                    pool.sem_inc(self.turn, 1)
                columns = cols(i + self.first, RING, h * HALF, HALF)
                pool.tensor_copy(self.where[:, cols(h, HALF)], self.addr[:, columns]).then_inc(self.copied, 1)
                if self.info is not None:
                    pool.tensor_copy(self.rows[:, cols(h, HALF), :], self.info[:, columns, :]).then_inc(self.copied, 1)
                else:
                    pool.tensor_copy(self.rows[:, cols(h, HALF), 0], self.node[:, columns]).then_inc(self.copied, 1)
                    pool.wait_ge(self.staged[h], (i + 1) * 16)
                    pool.sem_inc(self.turn, 1)
                pool.wait_ge(self.copied, (i * 2 + h + 1) * 2 + ones)
                pool.sem_inc(self.turn, 1)
                for k in range(h * HALF, (h + 1) * HALF):
                    pool.indirect_dma_start(self.table, bass.IndirectOffsetOnAxis(self.where[:, k:k + 1], 0),
                                            self.rows[:, k, :], None).then_inc(self.written[h], 16)
        rounds(pool, self.rounds, one_round)
        for h in range(2):
            pool.wait_ge(self.written[h], self.rounds * HALF * 16)


def pack_info(nc, e, info, slots):
    with Phase(nc, "pack") as ph:
        src, rel = ph.sb("src", [P, COLS], I32), ph.sb("rel", [P, COLS], I32)
        weight = ph.sb("weight", [P, COLS])
        empty = ph.sb("empty", [P, NT, 3], I32)
        loaded, cleared, filled = (ph.sem(n) for n in ("loaded", "cleared", "filled"))
        block = ph.block()

        @block.sync
        def _(sp):
            sp.dma_start(src[:, :], e["src"]).then_inc(loaded, 16)
            sp.dma_start(rel[:, :], e["rel"]).then_inc(loaded, 16)
            sp.dma_start(weight[:, :], e["weight"]).then_inc(loaded, 16)
            sp.wait_ge(cleared, 2)
            sp.dma_start(slots.rearrange("(p t) c -> p t c", p=P), empty[:, :, :]).then_inc(filled, 16)
            sp.wait_ge(filled, 16)

        @block.vector
        def _(dve):
            dve.memset(empty[:, :, 0:2], 0).then_inc(cleared, 1)
            dve.memset(empty[:, :, 2].bitcast(F32), NO_NODE).then_inc(cleared, 1)
            dve.wait_ge(loaded, 48)
            dve.scalar_tensor_tensor(info[:, :, 0], src[:, :], float(REL), rel[:, :], ALU.mult, ALU.add)
            dve.tensor_copy(info[:, :, 1].bitcast(F32), weight[:, :])


def unpack_slots(nc, mem, slots):
    with Phase(nc, "unpack") as ph:
        back = ph.sb("back", [P, NT, 3], I32)
        loaded = ph.sem("loaded")
        block = ph.block()

        @block.sync
        def _(sp):
            sp.dma_start(back[:, :, :], slots.rearrange("(p t) c -> p t c", p=P)).then_inc(loaded, 16)

        @block.vector
        def _(dve):
            dve.wait_ge(loaded, 16)
            dve.tensor_copy(mem.slot_row[:, :], back[:, :, 0])
            dve.tensor_copy(mem.slot_weight[:, :], back[:, :, 1].bitcast(F32))
            dve.tensor_copy(mem.slot_node[:, 0:NT], back[:, :, 2].bitcast(F32))


def load_nodes(nc, mem, e):
    with Phase(nc, "nodes") as ph:
        loaded = ph.sem("loaded")
        block = ph.block()

        @block.sync
        def _(sp):
            sp.dma_start(mem.x[:, :].rearrange("p (t d) -> p t d", d=D),
                         e["x"].rearrange("(t p) d -> p t d", p=P)).then_inc(loaded, 16)
            sp.wait_ge(loaded, 16)


def finish_stats(nc, mem, name, halves):
    with Phase(nc, name) as ph:
        mean, diff, var, std = (ph.sb(n, [P, BUCKETS]) for n in ("mean", "diff", "var", "std"))
        chain, var_ready, std_ready = ph.sem("chain"), ph.sem("var_ready"), ph.sem("std_ready")
        h = halves[:, :].rearrange("p (t s) -> p t s", s=6)
        block = ph.block()

        @block.scalar
        def _(act):
            act.wait_ge(var_ready, 1)
            act.activation(std[:, :], var[:, :], ACT.Sqrt, bias=mem.eps[:, :]).then_inc(std_ready, 1)

        @block.vector
        def _(dve):
            dve.tensor_tensor(mean[:, :], h[:, :, 1], h[:, :, 4], ALU.add).then_inc(chain, 1)
            dve.tensor_tensor(diff[:, :], h[:, :, 1], h[:, :, 4], ALU.subtract).then_inc(chain, 1)
            dve.tensor_tensor(var[:, :], h[:, :, 2], h[:, :, 5], ALU.add).then_inc(chain, 1)
            dve.wait_ge(chain, 2)
            dve.scalar_tensor_tensor(diff[:, :], diff[:, :], 0.25, diff[:, :], ALU.mult, ALU.mult).then_inc(chain, 1)
            dve.wait_ge(chain, 4)
            dve.scalar_tensor_tensor(var[:, :], var[:, :], 1.0 / D, diff[:, :], ALU.mult, ALU.add
                                     ).then_inc(var_ready, 1)
            dve.wait_ge(std_ready, 1)
            dve.reciprocal(mem.rstd[:, :], std[:, :]).then_inc(chain, 1)
            dve.wait_ge(chain, 5)
            dve.scalar_tensor_tensor(mem.shift[:, :], mean[:, :], -0.5, mem.rstd[:, :], ALU.mult, ALU.mult)


def first_stats(nc, mem, halves):
    with Phase(nc, "stats") as ph:
        block = ph.block()

        @block.vector
        def _(dve):
            dve.memset(mem.edge_acc[:, :], 0.0)
            with dve.Fori(0, BUCKETS) as t:
                dve.bn_stats(halves[:, cols(t, 6)], mem.x[:, cols(t, D)])


PAIRS = BUCKETS // 2


AWAY = 5


def over_pairs(engine, step):
    for i in (-1, 0, 1):
        step(i)
    with engine.Fori(2, PAIRS - 1) as i:
        step(i)
    for i in (PAIRS - 1, PAIRS):
        step(i)


def is_pair(i):
    return not isinstance(i, int) or 0 <= i < PAIRS


def relational_tables(nc, mem, e, layer, table, edges_to=None):
    chunks = REL * D // 512
    with Phase(nc, f"rel{layer}") as ph:
        w = ph.sb("w", [P, 2, REL * D + D])
        bias = ph.sb("bias", [P, D])
        h = [ph.sb(f"h{u}", [P, D]) for u in range(2)]
        turned = [ph.sb(f"turned{u}", [P, D]) for u in range(2)]
        out = [ph.sb(f"out{u}", [P, REL * D]) for u in range(2)]
        turned_ps = [ph.psum(f"turned_ps{u}", [P, 512]) for u in range(2)]
        product_ps = [ph.psum(f"product_ps{c}", [P, 512]) for c in range(chunks + 1)]
        loaded, h_ready, transposed, turned_ready, products, act_out, dve_out = (
            ph.sem(n) for n in ("loaded", "h_ready", "transposed", "turned_ready", "products",
                                "act_out", "dve_out"))
        stored = [ph.sem(f"stored{u}") for u in range(2)]
        scatter = None if edges_to is None else Scatter(ph, **edges_to)
        block = ph.block()

        @block.gpsimd
        def _(pool):
            if scatter is not None:
                scatter.write(pool)

        @block.sync
        def _(sp):
            for k in range(2):
                sp.dma_start(w[:, k, :], e["rel_w"][:, layer, k, :]).then_inc(loaded, 16)
            sp.dma_start(bias[:, :], e["rel_b"][layer].partition_broadcast(P)).then_inc(loaded, 16)

            def store(i):
                for u in range(2):
                    t = i * 2 + u
                    sp.wait_ge(act_out, (t + 1) * 3)
                    sp.sem_inc(ph.turn, 1)
                    sp.wait_ge(dve_out, (t + 1) * 2)
                    sp.sem_inc(ph.turn, 1)
                    sp.dma_start(table.rearrange("(n r) d -> n (r d)", r=REL)[bass.ds(t * P, P), :],
                                 out[u][:, :]).then_inc(stored[u], 16)

            def load_and_store(i):
                scatter.load_attributes(sp, i)
                store(i)
            if scatter is None or scatter.attr is None:
                rounds(sp, PAIRS, store)
            else:
                rounds(sp, scatter.rounds, load_and_store)
                for i in range(scatter.rounds, PAIRS):
                    store(i)
            for u in range(2):
                sp.wait_ge(stored[u], 16 * PAIRS)

        @block.scalar
        def _(act):
            def step(i):
                if is_pair(i + 1):
                    for u in range(2):
                        t = (i + 1) * 2 + u
                        if not is_first(i + 1):
                            act.wait_ge(transposed, t - 1)
                            act.sem_inc(ph.turn, 1)
                        if layer == 0:
                            ins = act.activation(h[u][:, :], mem.x[:, cols(t, D)], ACT.Relu,
                                                 bias=mem.shift[:, bass.ds(t, 1)], scale=mem.rstd[:, bass.ds(t, 1)])
                        else:
                            ins = act.activation(h[u][:, :], mem.acc[:, cols(t, ACCW, 0, D)], ACT.Relu)
                        ins.then_inc(h_ready, 1)
                for u in range(2):
                    if is_pair(i):
                        t = i * 2 + u
                        if not is_first(i):
                            act.wait_ge(stored[u], i * 16)
                        for c in range(3):
                            act.wait_ge(products, t * (chunks + 1) + c + 1)
                            act.copy(out[u][:, cols(c, 512)], product_ps[c][:, :]).then_inc(act_out, 1)
                    if is_pair(i + 1):
                        t = (i + 1) * 2 + u
                        act.wait_ge(transposed, t + 1)
                        if not is_first(i + 1):
                            act.wait_ge(products, (t - 1) * (chunks + 1))
                        act.copy(turned[u][:, :], turned_ps[u][:, 0:D]).then_inc(turned_ready, 1)
            over_pairs(act, step)

        @block.tensor
        def _(pe):
            pe.wait_ge(loaded, 48)

            def step(i):
                for u in range(2):
                    if is_pair(i):
                        t = i * 2 + u
                        pe.wait_ge(turned_ready, t + 1)
                        for c in range(chunks + 1):
                            if not (is_first(i) and u == 0):
                                if c < 3:
                                    pe.wait_ge(act_out, (t - 1) * 3 + c + 1)
                                else:
                                    pe.wait_ge(dve_out, (t - 1) * 2 + c - 2)
                            n = 512 if c < chunks else D
                            for k in range(2):
                                ins = pe.matmul(product_ps[c][:, 0:n], turned[u][:, cols(k, P)],
                                                w[:, k, c * 512:c * 512 + n], start=(k == 0), stop=(k == 1))
                            ins.then_inc(products, 1)
                    if is_pair(i + 1):
                        t = (i + 1) * 2 + u
                        pe.wait_ge(h_ready, t + 1)
                        if not is_first(i + 1):
                            pe.wait_ge(turned_ready, t - 1)
                        for k in range(2):
                            ins = pe.transpose(turned_ps[u][:, cols(k, P)], h[u][:, cols(k, P)], mem.ident[:, :])
                        ins.then_inc(transposed, 1)
            over_pairs(pe, step)

        @block.vector
        def _(dve):
            dve.wait_ge(loaded, 48)

            def tiles(i):
                for u in range(2):
                    t = i * 2 + u
                    if not is_first(i):
                        dve.wait_ge(stored[u], i * 16)
                    dve.wait_ge(products, t * (chunks + 1) + chunks)
                    dve.tensor_copy(out[u][:, cols(3, 512)], product_ps[3][:, :]).then_inc(dve_out, 1)
                    dve.wait_ge(products, (t + 1) * (chunks + 1))
                    dve.tensor_tensor(mem.acc[:, cols(t, ACCW, 0, D)], product_ps[chunks][:, 0:D], bias[:, :],
                                      ALU.add).then_inc(dve_out, 1)
            rounds(dve, PAIRS, tiles)


class Group:

    def __init__(self, i, g, groups=GROUPS):
        self.i, self.g = i + g // groups, g % groups
        self.q = self.i * groups + self.g
        self.t = self.i * (groups * GROUP) + self.g * GROUP
        self.exists = not isinstance(self.q, int) or 0 <= self.q < NT // GROUP

    def after(self, n):
        return not isinstance(self.q, int) or self.q >= n


def over_groups(engine, step, lead):
    def one_round(i, first=0):
        for g in range(first, GROUPS):
            step(i, g)
    one_round(-1, GROUPS - lead)
    one_round(0)
    with engine.Fori(1, NT // RING - 1) as i:
        one_round(i)
    one_round(NT // RING - 1)


def aggregate(nc, mem, name, table, slot_row, weighted=False, degree=False, edge_rows=None, ranked=None):
    width = D + (1 if degree else 0)
    n_rounds = NT // RING
    with Phase(nc, name) as ph:
        rows = ph.sb("rows", [P, RING, width])
        which = ph.sb("which", [P, RING], I32)
        onehot = ph.sb("onehot", [P, 2 * GROUP, P])
        sums_ps = [ph.psum(f"sums_ps{k}", [P, 512]) for k in range(GROUP)]
        staged = [ph.sem(f"staged{g}") for g in range(GROUPS)]
        landed = [ph.sem(f"landed{g}") for g in range(GROUPS)]
        onehots, products, added, filled = (
            ph.sem(n) for n in ("onehots", "products", "added", "filled"))
        if edge_rows is not None:
            erow = ph.sb("erow", [P, RING, 1 + ECOLS])
            ehot = ph.sb("ehot", [P, 2 * GROUP, P])
            esums_ps = [ph.psum(f"esums_ps{k}", [P, 512]) for k in range(GROUP)]
            eloaded = [ph.sem(f"eloaded{g}") for g in range(GROUPS)]
            ehots, eproducts, eadded = ph.sem("ehots"), ph.sem("eproducts"), ph.sem("eadded")
        ranks = None if ranked is None else Ranks(ph, ranked, 1)
        assert ranks is None or n_rounds - 2 == BUCKETS
        block = ph.block()

        @block.sync
        def _(sp):
            def stage(i):
                for g in range(GROUPS):
                    if not is_first(i):
                        sp.wait_ge(landed[g], i * (16 * GROUP))
                        sp.sem_inc(ph.turn, 1)
                    sp.dma_start(which[:, cols(g, GROUP)], slot_row[:, cols(i, RING, g * GROUP, GROUP)]
                                 ).then_inc(staged[g], 16)
                    if edge_rows is not None:
                        if not is_first(i):
                            sp.wait_ge(eproducts, (i - 1) * RING + (g + 1) * GROUP)
                            sp.sem_inc(ph.turn, 1)
                        sp.dma_start(erow[:, cols(g, GROUP), :],
                                     edge_rows.rearrange("(p t) c -> p t c", p=P)[:, cols(i, RING, g * GROUP, GROUP), :]
                                     ).then_inc(eloaded[g], 16)
            rounds(sp, n_rounds, stage)

        @block.gpsimd
        def _(pool):
            def gather(i):
                for g in range(GROUPS):
                    pool.wait_ge(staged[g], (i + 1) * 16)
                    if not is_first(i):
                        pool.wait_ge(products, (i - 1) * RING + (g + 1) * GROUP)
                        pool.sem_inc(ph.turn, 1)
                    for k in range(g * GROUP, (g + 1) * GROUP):
                        pool.indirect_dma_start(rows[:, k, 0:D], None, table,
                                                bass.IndirectOffsetOnAxis(which[:, k:k + 1], 0)
                                                ).then_inc(landed[g], 16)
            rounds(pool, n_rounds, gather)

        @block.tensor
        def _(pe):
            if degree:
                pe.wait_ge(filled, 1)

            def step(i, g):
                n = Group(i, g)
                for k in range(GROUP):
                    if edge_rows is not None:
                        pe.wait_ge(ehots, n.t + k + 1)
                        if n.after(1):
                            pe.wait_ge(eadded, n.t + k - GROUP + 1)
                        pe.matmul(esums_ps[k][:, 0:ECOLS], ehot[:, g % 2 * GROUP + k, :],
                                  erow[:, g * GROUP + k, 1:1 + ECOLS], start=True, stop=True).then_inc(eproducts, 1)
                    if k == 0:
                        pe.wait_ge(landed[g], (n.i + 1) * (16 * GROUP))
                    pe.wait_ge(onehots, n.t + k + 1)
                    if n.after(1):
                        pe.wait_ge(added, n.t + k - GROUP + 1)
                    pe.matmul(sums_ps[k][:, 0:width], onehot[:, g % 2 * GROUP + k, :],
                              rows[:, g * GROUP + k, :], start=True, stop=True).then_inc(products, 1)
            over_groups(pe, step, 0)

        @block.vector
        def _(dve):
            tiles = []

            def onehot_of(n, k):
                if n.after(2):
                    dve.wait_ge(products, n.t + k - 2 * GROUP + 1)
                node = mem.slot_node[:, bass.ds(n.t + k, 1)]
                out = onehot[:, n.g % 2 * GROUP + k, :]
                if weighted:
                    ins = dve.tensor_scalar(out, mem.iota[:, :], node, mem.slot_weight[:, bass.ds(n.t + k, 1)],
                                            ALU.is_equal, ALU.mult)
                else:
                    ins = dve.tensor_scalar(out, mem.iota[:, :], node, None, ALU.is_equal)
                ins.then_inc(onehots, 1)

            def edge_hot_of(n, k):
                if k == 0:
                    dve.wait_ge(eloaded[n.g], (n.i + 1) * 16)
                if n.after(2):
                    dve.wait_ge(eproducts, n.t + k - 2 * GROUP + 1)
                dve.tensor_scalar(ehot[:, n.g % 2 * GROUP + k, :], mem.iota[:, :], erow[:, n.g * GROUP + k, 0:1], None,
                                  ALU.is_equal).then_inc(ehots, 1)

            def add(n, k):
                into = mem.acc[:, cols(tiles[n.g * GROUP + k], ACCW, 0, width)]
                dve.wait_ge(products, n.t + k + 1)
                if n.after(1) or k:
                    dve.wait_ge(added, n.t + k)
                dve.tensor_tensor(into, into, sums_ps[k][:, 0:width], ALU.add).then_inc(added, 1)

            def edge_add(n, k):
                into = mem.edge_acc[:, cols(tiles[RING + n.g * GROUP + k], ECOLS)]
                dve.wait_ge(eproducts, n.t + k + 1)
                if n.after(1) or k:
                    dve.wait_ge(eadded, n.t + k)
                dve.tensor_tensor(into, into, esums_ps[k][:, 0:ECOLS], ALU.add).then_inc(eadded, 1)

            def step(i, g):
                now, following = Group(i, g), Group(i, g + 1)
                if now.exists and g == 0:
                    tiles[:] = tiles_of(nc, dve, mem.tile_of, i, 0, RING * (1 if edge_rows is None else 2))
                if ranks is not None and now.exists and not isinstance(i, int):
                    ranks.step(dve, i - 1, 0, g)
                for k in range(GROUP):
                    if following.exists:
                        onehot_of(following, k)
                    if edge_rows is not None and now.exists:
                        edge_add(now, k)
                    if edge_rows is not None and following.exists:
                        edge_hot_of(following, k)
                    if now.exists:
                        add(now, k)
            if degree:
                dve.memset(rows[:, :, D], 1.0).then_inc(filled, 1)
            if ranks is not None:
                ranks.begin(dve)
            over_groups(dve, step, 1)


def relational_end(nc, mem, halves):
    with Phase(nc, "relend") as ph:
        s = [ph.sb(f"s{u}", [P, D]) for u in range(2)]
        sigmoids, x_ready = ph.sem("sigmoids"), ph.sem("x_ready")
        block = ph.block()

        @block.scalar
        def _(act):
            def tiles(i):
                for u in range(2):
                    t = i * 2 + u
                    if not is_first(i):
                        act.wait_ge(x_ready, t - 1)
                        act.sem_inc(ph.turn, 1)
                    act.activation(s[u][:, :], mem.acc[:, cols(t, ACCW, 0, D)], ACT.Sigmoid).then_inc(sigmoids, 1)
            rounds(act, PAIRS, tiles)

        @block.vector
        def _(dve):
            with dve.Fori(0, PAIRS) as i:
                for u in range(2):
                    t = i * 2 + u
                    x = mem.x[:, cols(t, D)]
                    dve.wait_ge(sigmoids, t + 1)
                    dve.tensor_tensor(x, x, s[u][:, :], ALU.add).then_inc(x_ready, 1)
                for u in range(2):
                    t = i * 2 + u
                    dve.wait_ge(x_ready, t + 1)
                    dve.sem_inc(ph.turn, 1)
                    dve.bn_stats(halves[:, cols(t, 6)], mem.x[:, cols(t, D)])


def slot_sources(nc, mem):
    with Phase(nc, "sources") as ph:
        block = ph.block()

        @block.vector
        def _(dve):
            dve.tensor_scalar(mem.slot_row[:, :], mem.slot_row[:, :], REL.bit_length() - 1, None,
                              ALU.logical_shift_right)


def node_table(nc, mem, table):
    with Phase(nc, "node_table") as ph:
        h = [ph.sb(f"h{u}", [P, D]) for u in range(AWAY)]
        deg = ph.sb("deg", [P, BUCKETS])
        h_ready, chain = ph.sem("h_ready"), ph.sem("chain")
        stored = [ph.sem(f"stored{u}") for u in range(AWAY)]
        block = ph.block()

        @block.scalar
        def _(act):
            def tiles(i):
                for u in range(AWAY):
                    t = i * AWAY + u
                    if not is_first(i):
                        act.wait_ge(stored[u], i * 16)
                        act.sem_inc(ph.turn, 1)
                    act.activation(h[u][:, :], mem.x[:, cols(t, D)], ACT.Relu, bias=mem.shift[:, bass.ds(t, 1)],
                                   scale=mem.rstd[:, bass.ds(t, 1)]).then_inc(h_ready, 1)
            rounds(act, BUCKETS // AWAY, tiles)

        @block.sync
        def _(sp):
            with sp.Fori(0, BUCKETS // AWAY) as i:
                for u in range(AWAY):
                    sp.wait_ge(h_ready, i * AWAY + u + 1)
                    sp.sem_inc(ph.turn, 1)
                    sp.dma_start(table[bass.ds((i * AWAY + u) * P, P), :], h[u][:, :]).then_inc(stored[u], 16)
            for u in range(AWAY):
                sp.wait_ge(stored[u], 16 * BUCKETS // AWAY)

        @block.vector
        def _(dve):
            acc = mem.acc[:, :].rearrange("p (t c) -> p t c", c=ACCW)
            dve.tensor_scalar(deg[:, :], acc[:, :, D], 1.0, None, ALU.max).then_inc(chain, 1)
            dve.wait_ge(chain, 1)
            dve.reciprocal(mem.inv_deg[:, :], deg[:, :])
            dve.memset(acc[:, :, 0:D], 0.0)


def conv_layers(nc, mem, e, table):
    L = 4
    with Phase(nc, "conv") as ph:
        sb, sem = ph.sb, ph.sem
        w = sb("w", [P, 2, 2, L * D])
        bias, gain, norm_b = (sb(n, [P, L * D]) for n in ("bias", "gain", "norm_b"))
        two = range(2)
        node, agg = [sb(f"node{u}", [P, D]) for u in two], [sb(f"agg{u}", [P, D]) for u in two]
        turned = [sb(f"turned{u}", [P, 4 * P]) for u in two]
        node_b = [sb(f"node_b{u}", [P, L * D]) for u in two]
        z = [sb(f"z{u}", [P, L * D]) for u in two]
        stats = [sb(f"stats{u}", [P, L * 6]) for u in two]
        mv = [sb(f"mv{u}", [P, L * 2]) for u in two]
        std, rstd, shift = ([sb(f"{n}{u}", [P, L]) for u in two] for n in ("std", "rstd", "shift"))
        turned_ps = [ph.psum(f"turned_ps{u}", [P, 512]) for u in two]
        z_ps = [[ph.psum(f"z_ps{u}{c}", [P, 512]) for c in two] for u in two]
        loaded = sem("loaded")
        node_loaded = [sem(f"node_loaded{u}") for u in two]
        (agg_ready, transposed, turned_ready, products, node_b_ready, z_ready, stats_ready, mv_ready, std_ready,
         rstd_ready, shift_ready, normed, gained, biased, positive, summed) = (
            sem(n) for n in ("agg_ready", "transposed", "turned_ready", "products", "node_b_ready", "z_ready",
                             "stats_ready", "mv_ready", "std_ready", "rstd_ready", "shift_ready", "normed",
                             "gained", "biased", "positive", "summed"))
        block = ph.block()

        @block.sync
        def _(sp):
            sp.dma_start(w[:, :, :, :], e["conv_w"]).then_inc(loaded, 16)
            for into, name in ((bias, "conv_b"), (gain, "conv_g"), (norm_b, "conv_n")):
                sp.dma_start(into[:, :], e[name][0].partition_broadcast(P)).then_inc(loaded, 16)

            def load(i):
                for u in two:
                    t = i * 2 + u
                    if not is_first(i):
                        sp.wait_ge(transposed, t - 1)
                        sp.sem_inc(ph.turn, 1)
                        sp.wait_ge(node_b_ready, t - 1)
                        sp.sem_inc(ph.turn, 1)
                    sp.dma_start(node[u][:, :], table[bass.ds(t * P, P), :]).then_inc(node_loaded[u], 16)
            rounds(sp, PAIRS, load)

        @block.gpsimd
        def _(pool):
            pool.wait_ge(loaded, 64)

            def step(i):
                if is_pair(i):
                    for u in two:
                        t = i * 2 + u
                        pool.wait_ge(node_loaded[u], (i + 1) * 16)
                        if not is_first(i):
                            pool.wait_ge(z_ready, (t - 1) * 2)
                        pool.tensor_tensor(node_b[u][:, :].rearrange("p (l d) -> p l d", l=L),
                                           node[u][:, :].unsqueeze(1).broadcast_to([P, L, D]),
                                           bias[:, :].rearrange("p (l d) -> p l d", l=L), ALU.add
                                           ).then_inc(node_b_ready, 1)
                if is_pair(i - 1):
                    for u in two:
                        pool.wait_ge(gained, (i - 1) * 2 + u + 1)
                        pool.tensor_tensor(z[u][:, :], z[u][:, :], norm_b[:, :], ALU.add).then_inc(biased, 1)
            over_pairs(pool, step)

        @block.tensor
        def _(pe):
            pe.wait_ge(loaded, 64)

            def step(i):
                for u in two:
                    if is_pair(i):
                        t = i * 2 + u
                        pe.wait_ge(turned_ready, t + 1)
                        if not is_first(i):
                            pe.wait_ge(z_ready, (t - 1) * 2)
                        for c in two:
                            for k in range(4):
                                ins = pe.matmul(z_ps[u][c][:, :], turned[u][:, cols(k, P)],
                                                w[:, k // 2, k % 2, cols(c, 512)], start=(k == 0), stop=(k == 3))
                            ins.then_inc(products, 1)
                    if is_pair(i + 1):
                        t = (i + 1) * 2 + u
                        pe.wait_ge(node_loaded[u], (i + 2) * 16)
                        pe.wait_ge(agg_ready, t + 1)
                        if not is_first(i + 1):
                            pe.wait_ge(turned_ready, t - 1)
                        for k in range(4):
                            src = (agg, node)[k // 2][u]
                            ins = pe.transpose(turned_ps[u][:, cols(k, P)], src[:, cols(k % 2, P)], mem.ident[:, :])
                        ins.then_inc(transposed, 1)
            over_pairs(pe, step)

        @block.scalar
        def _(act):
            def step(i):
                def turn(u):
                    t = (i + 1) * 2 + u
                    act.wait_ge(transposed, t + 1)
                    if not is_first(i + 1):
                        act.wait_ge(products, (t - 1) * 2)
                    act.copy(turned[u][:, :], turned_ps[u][:, :]).then_inc(turned_ready, 1)

                if is_pair(i - 1):
                    for u in two:
                        t = (i - 1) * 2 + u
                        act.wait_ge(mv_ready, (t + 1) * L)
                        act.activation(std[u][:, :], mv[u][:, :].rearrange("p (l s) -> p l s", s=2)[:, :, 1], ACT.Sqrt,
                                       bias=mem.eps[:, :]).then_inc(std_ready, 1)
                    for u in two:
                        t = (i - 1) * 2 + u
                        act.wait_ge(shift_ready, t + 1)
                        for n in range(L):
                            act.activation(z[u][:, cols(n, D)], z[u][:, cols(n, D)], ACT.Identity,
                                           bias=shift[u][:, n:n + 1], scale=rstd[u][:, n:n + 1]).then_inc(normed, 1)
                if is_pair(i + 1):
                    turn(0)
                if is_pair(i - 1):
                    for u in two:
                        t = (i - 1) * 2 + u
                        act.wait_ge(biased, t + 1)
                        act.activation(z[u][:, :], z[u][:, :], ACT.Relu).then_inc(positive, 1)
                if is_pair(i + 1):
                    turn(1)
            over_pairs(act, step)

        @block.vector
        def _(dve):
            dve.wait_ge(loaded, 64)

            def step(i):
                for u in two:
                    if is_pair(i + 1):
                        t = (i + 1) * 2 + u
                        if not is_first(i + 1):
                            dve.wait_ge(transposed, t - 1)
                        dve.tensor_scalar(agg[u][:, :], mem.acc[:, cols(t, ACCW, 0, D)], mem.inv_deg[:, bass.ds(t, 1)],
                                          None, ALU.mult).then_inc(agg_ready, 1)
                if is_pair(i - 1):
                    tails = [(u, (i - 1) * 2 + u) for u in two]
                    for u, t in tails:
                        dve.wait_ge(z_ready, (t + 1) * 2)
                        for n in range(L):
                            dve.bn_stats(stats[u][:, cols(n, 6)], z[u][:, cols(n, D)]).then_inc(stats_ready, 1)
                    for u, t in tails:
                        dve.wait_ge(stats_ready, (t + 1) * L)
                        dve.sem_inc(ph.turn, 1)
                        for n in range(L):
                            dve.bn_aggr(mv[u][:, cols(n, 2)], stats[u][:, cols(n, 6)]).then_inc(mv_ready, 1)
                    for u, t in tails:
                        dve.wait_ge(std_ready, t + 1)
                        dve.reciprocal(rstd[u][:, :], std[u][:, :]).then_inc(rstd_ready, 1)
                    for u, t in tails:
                        dve.wait_ge(rstd_ready, t + 1)
                        dve.scalar_tensor_tensor(shift[u][:, :], mv[u][:, :].rearrange("p (l s) -> p l s", s=2)[:, :, 0],
                                                 -1.0, rstd[u][:, :], ALU.mult, ALU.mult).then_inc(shift_ready, 1)
                    for u, t in tails:
                        dve.wait_ge(normed, (t + 1) * L)
                        dve.tensor_tensor(z[u][:, :], z[u][:, :], gain[:, :], ALU.mult).then_inc(gained, 1)
                    for u, t in tails:
                        dve.wait_ge(positive, t + 1)
                        dve.sem_inc(ph.turn, 1)
                        dve.tensor_reduce(mem.acc[:, cols(t, ACCW, 0, D)], z[u][:, :].rearrange("p (l d) -> p d l", l=L),
                                          AX.X, ALU.add).then_inc(summed, 1)
                if is_pair(i):
                    for u in two:
                        t = i * 2 + u
                        dve.wait_ge(node_b_ready, t + 1)
                        if not is_first(i):
                            dve.wait_ge(summed, t - 1)
                        for c in two:
                            dve.wait_ge(products, t * 2 + c + 1)
                            dve.tensor_tensor(z[u][:, cols(c, 512)], z_ps[u][c][:, :], node_b[u][:, cols(c, 512)],
                                              ALU.add).then_inc(z_ready, 1)
            over_pairs(dve, step)


def mlp_layer(nc, mem, e, n, halves):
    with Phase(nc, f"mlp{n}") as ph:
        sb, sem = ph.sb, ph.sem
        w = sb("w", [P, 2, D])
        bias, gain, norm_b = (sb(x, [P, D]) for x in ("bias", "gain", "norm_b"))
        two = range(2)
        h, turned, z, v = ([sb(f"{x}{u}", [P, D]) for u in two] for x in ("h", "turned", "z", "v"))
        stats, mv = [sb(f"stats{u}", [P, 6]) for u in two], [sb(f"mv{u}", [P, 2]) for u in two]
        std, rstd, shift = ([sb(f"{x}{u}", [P, 1]) for u in two] for x in ("std", "rstd", "shift"))
        turned_ps = [ph.psum(f"turned_ps{u}", [P, 512]) for u in two]
        z_ps = [ph.psum(f"z_ps{u}", [P, 512]) for u in two]
        (loaded, h_ready, transposed, turned_ready, products, z_ready, stats_ready, mv_ready, std_ready,
         rstd_ready, shift_ready, normed, gained, biased, done) = (
            sem(x) for x in ("loaded", "h_ready", "transposed", "turned_ready", "products", "z_ready",
                             "stats_ready", "mv_ready", "std_ready", "rstd_ready", "shift_ready", "normed",
                             "gained", "biased", "done"))
        block = ph.block()

        @block.sync
        def _(sp):
            sp.dma_start(w[:, :, :], e["mlp_w"][:, n, :, :]).then_inc(loaded, 16)
            for into, row in ((bias, 0), (gain, 1), (norm_b, 2)):
                sp.dma_start(into[:, :], e["mlp_v"][3 * n + row].partition_broadcast(P)).then_inc(loaded, 16)

        @block.gpsimd
        def _(pool):
            pool.wait_ge(loaded, 64)
            with pool.Fori(0, PAIRS) as i:
                for u in two:
                    t = i * 2 + u
                    pool.wait_ge(gained, t + 1)
                    pool.tensor_tensor(v[u][:, :], v[u][:, :], norm_b[:, :], ALU.add).then_inc(biased, 1)

        @block.tensor
        def _(pe):
            pe.wait_ge(loaded, 64)

            def step(i):
                for u in two:
                    if is_pair(i):
                        t = i * 2 + u
                        pe.wait_ge(turned_ready, t + 1)
                        if not is_first(i):
                            pe.wait_ge(z_ready, t - 1)
                        for k in two:
                            ins = pe.matmul(z_ps[u][:, 0:D], turned[u][:, cols(k, P)], w[:, k, :],
                                            start=(k == 0), stop=(k == 1))
                        ins.then_inc(products, 1)
                    if is_pair(i + 1):
                        t = (i + 1) * 2 + u
                        pe.wait_ge(h_ready, t + 1)
                        if not is_first(i + 1):
                            pe.wait_ge(turned_ready, t - 1)
                        for k in two:
                            ins = pe.transpose(turned_ps[u][:, cols(k, P)], h[u][:, cols(k, P)], mem.ident[:, :])
                        ins.then_inc(transposed, 1)
            over_pairs(pe, step)

        @block.scalar
        def _(act):
            def step(i):
                if is_pair(i + 1):
                    for u in two:
                        t = (i + 1) * 2 + u
                        if not is_first(i + 1):
                            act.wait_ge(transposed, t - 1)
                            act.sem_inc(ph.turn, 1)
                        act.copy(h[u][:, :], mem.acc[:, cols(t, ACCW, 0, D)]).then_inc(h_ready, 1)
                if is_pair(i - 1):
                    for u in two:
                        act.wait_ge(mv_ready, (i - 1) * 2 + u + 1)
                        act.activation(std[u][:, :], mv[u][:, 1:2], ACT.Sqrt, bias=mem.eps[:, :]).then_inc(std_ready, 1)
                if is_pair(i - 1):
                    for u in two:
                        act.wait_ge(shift_ready, (i - 1) * 2 + u + 1)
                        if not is_first(i - 1):
                            act.wait_ge(done, (i - 1) * 2 + u - 1)
                        act.activation(v[u][:, :], z[u][:, :], ACT.Identity, bias=shift[u][:, :], scale=rstd[u][:, :]
                                       ).then_inc(normed, 1)
                if is_pair(i + 1):
                    for u in two:
                        t = (i + 1) * 2 + u
                        act.wait_ge(transposed, t + 1)
                        if not is_first(i + 1):
                            act.wait_ge(products, t - 1)
                        act.copy(turned[u][:, :], turned_ps[u][:, 0:D]).then_inc(turned_ready, 1)
            over_pairs(act, step)

        @block.vector
        def _(dve):
            dve.wait_ge(loaded, 64)

            def step(i):
                if is_pair(i - 1):
                    tails = [(u, (i - 1) * 2 + u) for u in two]
                    for u, t in tails:
                        dve.wait_ge(z_ready, t + 1)
                        dve.bn_stats(stats[u][:, :], z[u][:, :]).then_inc(stats_ready, 1)
                    for u, t in tails:
                        dve.wait_ge(stats_ready, t + 1)
                        dve.sem_inc(ph.turn, 1)
                        dve.bn_aggr(mv[u][:, :], stats[u][:, :]).then_inc(mv_ready, 1)
                    for u, t in tails:
                        dve.wait_ge(std_ready, t + 1)
                        dve.reciprocal(rstd[u][:, :], std[u][:, :]).then_inc(rstd_ready, 1)
                    for u, t in tails:
                        dve.wait_ge(rstd_ready, t + 1)
                        dve.scalar_tensor_tensor(shift[u][:, :], mv[u][:, 0:1], -1.0, rstd[u][:, :], ALU.mult, ALU.mult
                                                 ).then_inc(shift_ready, 1)
                    for u, t in tails:
                        dve.wait_ge(normed, t + 1)
                        dve.tensor_tensor(v[u][:, :], v[u][:, :], gain[:, :], ALU.mult).then_inc(gained, 1)
                if is_pair(i):
                    for u in two:
                        t = i * 2 + u
                        dve.wait_ge(products, t + 1)
                        if not is_first(i):
                            dve.wait_ge(normed, t - 1)
                        dve.tensor_tensor(z[u][:, :], z_ps[u][:, 0:D], bias[:, :], ALU.add).then_inc(z_ready, 1)
                if is_pair(i - 1):
                    for u, t in tails:
                        dve.wait_ge(biased, t + 1)
                        if n == 0:
                            dve.tensor_scalar(mem.acc[:, cols(t, ACCW, 0, D)], v[u][:, :], 0.0, None, ALU.max
                                              ).then_inc(done, 1)
                        else:
                            x = mem.x[:, cols(t, D)]
                            dve.scalar_tensor_tensor(x, v[u][:, :], 0.0, x, ALU.max, ALU.add).then_inc(done, 1)
                if n == 1 and is_pair(i - 1):
                    for u, t in tails:
                        dve.wait_ge(done, t + 1)
                        dve.sem_inc(ph.turn, 1)
                        dve.bn_stats(halves[:, cols(t, 6)], mem.x[:, cols(t, D)])
            over_pairs(dve, step)


def edge_layer(nc, mem, e, halves):
    F = e["edge_w"].shape[2]
    with Phase(nc, "edge") as ph:
        sb, sem = ph.sb, ph.sem
        two = range(2)
        w1, w1e, w1u = sb("w1", [P, 2, F]), sb("w1e", [EDGE_D, F]), sb("w1u", [P, F])
        w2, b1, b2 = sb("w2", [P, F // P, D]), sb("b1", [P, F]), sb("b2", [P, D])
        u_col, u_wide = sb("u_col", [P, 1]), sb("u_wide", [P, P])
        count, inv_count = sb("count", [P, BUCKETS]), sb("inv_count", [P, BUCKETS])
        h, turned, out = ([sb(f"{x}{u}", [P, D]) for u in two] for x in ("h", "turned", "out"))
        mean, mean_t = [sb(f"mean{u}", [P, EDGE_D]) for u in two], [sb(f"mean_t{u}", [EDGE_D, P]) for u in two]
        hidden, hidden_t = ([sb(f"{x}{u}", [P, F]) for u in two] for x in ("hidden", "hidden_t"))
        turned_ps, hidden_ps, hidden_t_ps, out_ps = (
            [ph.psum(f"{x}{u}", [P, 512]) for u in two] for x in ("turned_ps", "hidden_ps", "hidden_t_ps", "out_ps"))
        (loaded, chain, u_ready, u_product, u_taken, h_ready, mean_ready, transposed, turned_ready, products,
         hidden_ready, positive, hidden_transposed, hidden_t_ready, out_products, out_ready, x_ready) = (
            sem(x) for x in ("loaded", "chain", "u_ready", "u_product", "u_taken", "h_ready", "mean_ready",
                             "transposed", "turned_ready", "products", "hidden_ready", "positive",
                             "hidden_transposed", "hidden_t_ready", "out_products", "out_ready", "x_ready"))
        block = ph.block()

        @block.sync
        def _(sp):
            for into, src in ((w1[:, :, :], e["edge_w"]), (w1e[:, :], e["edge_we"]), (w1u[:, :], e["edge_wu"]),
                              (w2[:, :, :], e["edge_w2"]), (u_col[:, :], e["edge_u"]),
                              (b1[:, :], e["edge_b1"][0].partition_broadcast(P)),
                              (b2[:, :], e["edge_b2"][0].partition_broadcast(P))):
                sp.dma_start(into, src).then_inc(loaded, 16)

        @block.tensor
        def _(pe):
            pe.wait_ge(loaded, 7 * 16)
            pe.wait_ge(u_ready, 1)
            pe.matmul(hidden_ps[0][:, :], u_wide[:, :], w1u[:, :], start=True, stop=True).then_inc(u_product, 1)
            pe.wait_ge(u_taken, 1)

            def step(i):
                for u in two:
                    if is_pair(i - 1):
                        t = (i - 1) * 2 + u
                        pe.wait_ge(positive, t + 1)
                        if not is_first(i - 1):
                            pe.wait_ge(hidden_t_ready, t - 1)
                        for k in range(F // P):
                            ins = pe.transpose(hidden_t_ps[u][:, cols(k, P)], hidden[u][:, cols(k, P)], mem.ident[:, :])
                        ins.then_inc(hidden_transposed, 1)
                    if is_pair(i):
                        t = i * 2 + u
                        pe.wait_ge(turned_ready, (t + 1) * 2)
                        if not is_first(i):
                            pe.wait_ge(hidden_ready, t - 1)
                        for k in two:
                            pe.matmul(hidden_ps[u][:, :], turned[u][:, cols(k, P)], w1[:, k, :],
                                      start=(k == 0), stop=False)
                        pe.matmul(hidden_ps[u][:, :], mean_t[u][:, :], w1e[:, :], start=False, stop=True
                                  ).then_inc(products, 1)
                for u in two:
                    if is_pair(i - 1):
                        t = (i - 1) * 2 + u
                        pe.wait_ge(hidden_t_ready, t + 1)
                        if not is_first(i - 1):
                            pe.wait_ge(out_ready, t - 1)
                        for k in range(F // P):
                            ins = pe.matmul(out_ps[u][:, 0:D], hidden_t[u][:, cols(k, P)], w2[:, k, :],
                                            start=(k == 0), stop=(k == F // P - 1))
                        ins.then_inc(out_products, 1)
                    if is_pair(i + 1):
                        t = (i + 1) * 2 + u
                        pe.wait_ge(h_ready, t + 1)
                        pe.wait_ge(mean_ready, t + 1)
                        if not is_first(i + 1):
                            pe.wait_ge(turned_ready, (t - 1) * 2)
                        for k in two:
                            pe.transpose(turned_ps[u][:, cols(k, P)], h[u][:, cols(k, P)], mem.ident[:, :])
                        pe.transpose(turned_ps[u][0:EDGE_D, cols(2, P)], mean[u][:, :], mem.ident[:, :]
                                     ).then_inc(transposed, 1)
            over_pairs(pe, step)

        @block.scalar
        def _(act):
            def step(i):
                if is_pair(i + 1):
                    for u in two:
                        t = (i + 1) * 2 + u
                        if not is_first(i + 1):
                            act.wait_ge(transposed, t - 1)
                            act.sem_inc(ph.turn, 1)
                        act.activation(h[u][:, :], mem.x[:, cols(t, D)], ACT.Relu, bias=mem.shift[:, bass.ds(t, 1)],
                                       scale=mem.rstd[:, bass.ds(t, 1)]).then_inc(h_ready, 1)
                for u in two:
                    if is_pair(i - 1):
                        t = (i - 1) * 2 + u
                        act.wait_ge(hidden_transposed, t + 1)
                        if not is_first(i - 1):
                            act.wait_ge(out_products, t - 1)
                        act.copy(hidden_t[u][:, :], hidden_t_ps[u][:, :]).then_inc(hidden_t_ready, 1)
                for u in two:
                    if is_pair(i):
                        act.wait_ge(hidden_ready, i * 2 + u + 1)
                        act.activation(hidden[u][:, :], hidden[u][:, :], ACT.Relu).then_inc(positive, 1)
                for u in two:
                    if is_pair(i + 1):
                        t = (i + 1) * 2 + u
                        act.wait_ge(transposed, t + 1)
                        if not is_first(i + 1):
                            act.wait_ge(products, t - 1)
                        act.copy(turned[u][:, :], turned_ps[u][:, 0:D]).then_inc(turned_ready, 1)
                        act.copy(mean_t[u][:, :], turned_ps[u][0:EDGE_D, cols(2, P)]).then_inc(turned_ready, 1)
            over_pairs(act, step)

        @block.vector
        def _(dve):
            edges = mem.edge_acc[:, :].rearrange("p (t c) -> p t c", c=ECOLS)
            dve.tensor_scalar(count[:, :], edges[:, :, EDGE_D], 1.0, None, ALU.max).then_inc(chain, 1)
            dve.wait_ge(loaded, 7 * 16)
            dve.tensor_scalar(u_wide[:, :], mem.ones[:, :], u_col[:, :], None, ALU.mult).then_inc(u_ready, 1)
            dve.wait_ge(chain, 1)
            dve.reciprocal(inv_count[:, :], count[:, :]).then_inc(chain, 1)
            dve.wait_ge(u_product, 1)
            dve.tensor_tensor(b1[:, :], b1[:, :], hidden_ps[0][:, :], ALU.add).then_inc(u_taken, 1)
            dve.wait_ge(chain, 2)
            dve.wait_ge(u_taken, 1)

            def step(i):
                for u in two:
                    if is_pair(i + 1):
                        t = (i + 1) * 2 + u
                        if not is_first(i + 1):
                            dve.wait_ge(transposed, t - 1)
                        dve.tensor_scalar(mean[u][:, :], mem.edge_acc[:, cols(t, ECOLS, 0, EDGE_D)],
                                          inv_count[:, bass.ds(t, 1)], None, ALU.mult).then_inc(mean_ready, 1)
                for u in two:
                    if is_pair(i):
                        t = i * 2 + u
                        dve.wait_ge(products, t + 1)
                        if not is_first(i):
                            dve.wait_ge(hidden_transposed, t - 1)
                        dve.tensor_tensor(hidden[u][:, :], hidden_ps[u][:, :], b1[:, :], ALU.add
                                          ).then_inc(hidden_ready, 1)
                if is_pair(i - 1):
                    tails = [(u, (i - 1) * 2 + u) for u in two]
                    for u, t in tails:
                        dve.wait_ge(out_products, t + 1)
                        if not is_first(i - 1):
                            dve.wait_ge(x_ready, t - 1)
                        dve.tensor_tensor(out[u][:, :], out_ps[u][:, 0:D], b2[:, :], ALU.add).then_inc(out_ready, 1)
                    for u, t in tails:
                        x = mem.x[:, cols(t, D)]
                        dve.wait_ge(out_ready, t + 1)
                        dve.tensor_tensor(x, x, out[u][:, :], ALU.add).then_inc(x_ready, 1)
                    for u, t in tails:
                        dve.wait_ge(x_ready, t + 1)
                        dve.sem_inc(ph.turn, 1)
                        dve.bn_stats(halves[:, cols(t, 6)], mem.x[:, cols(t, D)])
            over_pairs(dve, step)


class Attention:

    def __init__(self, nc, ctx, n, heads):
        def sb(name, shape):
            return ctx.enter_context(nc.sbuf_tensor(f"att{n}_{name}", shape, F32))

        at_once = heads == 1
        self.n, self.heads, self.part = n, heads, D // heads + 1
        self.width = heads * self.part
        self.src = sb("src", [P, BUCKETS * heads])
        self.dst = sb("dst", [P, BUCKETS * heads])
        self.top = sb("top", [P, BUCKETS * heads])
        if not at_once:
            self.pair = sb("pair", [P, BUCKETS, 2 * heads])
            self.slot_src = sb("slot_src", [P, NT * heads])
        self.least = sb("least", [P, heads])

    def by_head(self, ap):
        return ap.rearrange("p (h c) -> p h c", c=self.part)


def attention_tables(nc, mem, e, att, table, alphas, before=None):
    H, C = att.heads, D // att.heads
    with Phase(nc, f"att_table{att.n}") as ph:
        sb, sem = ph.sb, ph.sem
        two = range(2)
        w_in, a_src, a_dst = sb("w_in", [P, 2, D]), sb("a_src", [P, D]), sb("a_dst", [P, D])
        w = sb("w", [P, 2, D + 2 * H])
        by_a = sb("by_a", [P, 4, D])
        h, turned = ([sb(f"{x}{u}", [P, D]) for u in two] for x in ("h", "turned"))
        row = [sb(f"row{u}", [P, table.shape[1]]) for u in two]
        least_t, least_h, diag = sb("least_t", [H, P]), sb("least_h", [H, 1]), sb("diag", [H, H])
        turned_ps, product_ps = ([ph.psum(f"{x}{u}", [P, 512]) for u in two] for x in ("turned_ps", "product_ps"))
        least_ps, wide_ps = ph.psum("least_ps", [P, 512]), ph.psum("wide_ps", [P, 512])
        (loaded, chain, w_ready, h_ready, transposed, turned_ready, products, row_ready, kept, least_ready,
         least_turned, diag_ready, wide_ready, own, counted, alphas_stored) = (
            sem(x) for x in ("loaded", "chain", "w_ready", "h_ready", "transposed", "turned_ready", "products",
                             "row_ready", "kept", "least_ready", "least_turned", "diag_ready", "wide_ready", "own",
                             "counted", "alphas_stored"))
        stored = [sem(f"stored{u}") for u in two]
        if before is not None:
            bias = sb("bias", [P, D])
            v, neg, ex = ([sb(f"{x}{u}", [P, D]) for u in two] for x in ("v", "neg", "ex"))
            inv = [sb(f"inv{u}", [P, before.heads]) for u in two]
            inv_ready, scaled, v_ready, neg_ready, ex_ready, positive = (
                sem(x) for x in ("inv_ready", "scaled", "v_ready", "neg_ready", "ex_ready", "positive"))
        n_loaded = 3 + (before is not None)
        block = ph.block()

        @block.sync
        def _(sp):
            sp.dma_start(w_in[:, :, :], e["att_w"][:, att.n, :, :]).then_inc(loaded, 16)
            sp.dma_start(a_src[:, :], e["att_src"][att.n].partition_broadcast(P)).then_inc(loaded, 16)
            sp.dma_start(a_dst[:, :], e["att_dst"][att.n].partition_broadcast(P)).then_inc(loaded, 16)
            if before is not None:
                sp.dma_start(bias[:, :], e["att_b"][before.n].partition_broadcast(P)).then_inc(loaded, 16)
            with sp.Fori(0, PAIRS) as i:
                for u in two:
                    sp.wait_ge(row_ready, i * 2 + u + 1)
                    sp.sem_inc(ph.turn, 1)
                    sp.dma_start(table[bass.ds((i * 2 + u) * P, P), :], row[u][:, :]).then_inc(stored[u], 16)
            for u in two:
                sp.wait_ge(stored[u], 16 * PAIRS)
            if alphas is not None:
                sp.wait_ge(counted, 1)
                sp.dma_start(alphas.rearrange("(t p) h -> p t h", p=P),
                             att.src[:, :].rearrange("p (t h) -> p t h", h=H),
                             allow_slow_non_contiguous=True).then_inc(alphas_stored, 16)
                sp.wait_ge(alphas_stored, 16)

        @block.tensor
        def _(pe):
            pe.wait_ge(w_ready, 4)

            def step(i):
                for u in two:
                    if is_pair(i):
                        t = i * 2 + u
                        pe.wait_ge(turned_ready, t + 1)
                        if not is_first(i):
                            pe.wait_ge(row_ready, t - 1)
                            pe.wait_ge(kept, (t - 1) * 3)
                        for k in two:
                            ins = pe.matmul(product_ps[u][:, 0:D + 2 * H], turned[u][:, cols(k, P)], w[:, k, :],
                                            start=(k == 0), stop=(k == 1))
                        ins.then_inc(products, 1)
                    if is_pair(i + 1):
                        t = (i + 1) * 2 + u
                        pe.wait_ge(h_ready, t + 1)
                        if not is_first(i + 1):
                            pe.wait_ge(turned_ready, t - 1)
                        for k in two:
                            ins = pe.transpose(turned_ps[u][:, cols(k, P)], h[u][:, cols(k, P)], mem.ident[:, :])
                        ins.then_inc(transposed, 1)
            over_pairs(pe, step)
            pe.wait_ge(least_ready, 1)
            pe.transpose(least_ps[0:H, 0:P], att.least[:, :], mem.ident[:, :]).then_inc(least_turned, 1)
            pe.wait_ge(diag_ready, 1)
            pe.matmul(wide_ps[:, 0:H], mem.ones[0:H, :], diag[:, :], start=True, stop=True).then_inc(wide_ready, 1)

        @block.scalar
        def _(act):
            def step(i):
                if is_pair(i + 1):
                    for u in two:
                        t = (i + 1) * 2 + u
                        if before is None:
                            if not is_first(i + 1):
                                act.wait_ge(transposed, t - 1)
                                act.sem_inc(ph.turn, 1)
                            act.activation(h[u][:, :], mem.x[:, cols(t, D)], ACT.Relu, bias=mem.shift[:, bass.ds(t, 1)],
                                           scale=mem.rstd[:, bass.ds(t, 1)]).then_inc(h_ready, 1)
                        else:
                            act.wait_ge(neg_ready, t + 1)
                            act.activation(ex[u][:, :], neg[u][:, :], ACT.Exp).then_inc(ex_ready, 1)
                for u in two:
                    if is_pair(i):
                        t = i * 2 + u
                        act.wait_ge(products, t + 1)
                        if not is_first(i):
                            act.wait_ge(stored[u], i * 16)
                        act.copy(row[u][:, :], product_ps[u][:, 0:table.shape[1]]).then_inc(row_ready, 1)
                    if is_pair(i + 1):
                        t = (i + 1) * 2 + u
                        act.wait_ge(transposed, t + 1)
                        if not is_first(i + 1):
                            act.wait_ge(products, t - 1)
                        act.copy(turned[u][:, :], turned_ps[u][:, 0:D]).then_inc(turned_ready, 1)
            over_pairs(act, step)

        @block.vector
        def _(dve):
            dve.wait_ge(loaded, 16 * n_loaded)
            for k in two:
                dve.tensor_tensor(by_a[:, 2 * k, :], w_in[:, k, :], a_src[:, :], ALU.mult).then_inc(chain, 1)
                dve.tensor_tensor(by_a[:, 2 * k + 1, :], w_in[:, k, :], a_dst[:, :], ALU.mult).then_inc(chain, 1)
                dve.tensor_copy(w[:, k, 0:D], w_in[:, k, :]).then_inc(chain, 1)
            dve.wait_ge(chain, 6)
            for k in two:
                for a in two:
                    dve.tensor_reduce(w[:, k, D + a * H:D + (a + 1) * H],
                                      by_a[:, 2 * k + a, :].rearrange("p (h c) -> p h c", c=C), AX.X, ALU.add
                                      ).then_inc(w_ready, 1)

            def step(i):
                if before is not None and is_pair(i + 1):
                    CB = D // before.heads
                    heads = [(u, (i + 1) * 2 + u) for u in two]
                    sums = [before.by_head(mem.acc[:, cols(t, ACCW, 0, before.width)]) for u, t in heads]
                    for u, t in heads:
                        if not is_first(i + 1):
                            dve.wait_ge(scaled, t - 1)
                        dve.sem_inc(ph.turn, 1)
                        dve.reciprocal(inv[u][:, :], sums[u][:, :, CB]).then_inc(inv_ready, 1)
                    for u, t in heads:
                        dve.wait_ge(inv_ready, t + 1)
                        if not is_first(i + 1):
                            dve.wait_ge(h_ready, t - 1)
                        dve.tensor_tensor(v[u][:, :].rearrange("p (h c) -> p h c", c=CB), sums[u][:, :, 0:CB],
                                          inv[u][:, :].unsqueeze(2).broadcast_to([P, before.heads, CB]),
                                          ALU.mult).then_inc(scaled, 1)
                    for u, t in heads:
                        dve.wait_ge(scaled, t + 1)
                        dve.tensor_tensor(v[u][:, :], v[u][:, :], bias[:, :], ALU.add).then_inc(v_ready, 1)
                    for u, t in heads:
                        dve.wait_ge(v_ready, t + 1)
                        if not is_first(i + 1):
                            dve.wait_ge(ex_ready, t - 1)
                        dve.tensor_scalar(neg[u][:, :], v[u][:, :], 0.0, None, ALU.min).then_inc(neg_ready, 1)
                    for u, t in heads:
                        dve.wait_ge(neg_ready, t + 1)
                        dve.tensor_scalar(v[u][:, :], v[u][:, :], 0.0, None, ALU.max).then_inc(positive, 1)
                    for u, t in heads:
                        dve.wait_ge(ex_ready, t + 1)
                        dve.wait_ge(positive, t + 1)
                        if not is_first(i + 1):
                            dve.wait_ge(transposed, t - 1)
                        dve.scalar_tensor_tensor(h[u][:, :], ex[u][:, :], -1.0, v[u][:, :], ALU.add, ALU.add
                                                 ).then_inc(h_ready, 1)
                for u in two:
                    if is_pair(i):
                        t = i * 2 + u
                        dve.wait_ge(row_ready, t + 1)
                        dve.tensor_scalar(att.by_head(mem.acc[:, cols(t, ACCW, 0, att.width)])[:, :, 0:C],
                                          product_ps[u][:, 0:D].rearrange("p (h c) -> p h c", c=C), 0.0, None, ALU.add
                                          ).then_inc(kept, 1)
                        for a, of_nodes in enumerate((att.src, att.dst)):
                            dve.tensor_scalar(of_nodes[:, cols(t, H)], product_ps[u][:, D + a * H:D + (a + 1) * H],
                                              0.0, None, ALU.add).then_inc(kept, 1)
            over_pairs(dve, step)
            dve.wait_ge(kept, 3 * BUCKETS)
            acc = mem.acc[:, :].rearrange("p (t c) -> p t c", c=ACCW)
            for head in range(H):
                dve.memset(acc[:, :, head * (C + 1) + C], 1.0)
            dve.tensor_reduce(att.least[:, :], att.src[:, :].rearrange("p (t h) -> p h t", h=H), AX.X, ALU.min
                              ).then_inc(least_ready, 1)
            dve.wait_ge(least_turned, 1)
            dve.tensor_copy(least_t[:, :], least_ps[0:H, 0:P]).then_inc(own, 1)
            dve.wait_ge(own, 1)
            dve.tensor_reduce(least_h[:, :], least_t[:, :], AX.X, ALU.min).then_inc(own, 1)
            dve.wait_ge(own, 2)
            dve.tensor_scalar(diag[:, :], mem.ident[0:H, 0:H], least_h[:, :], None, ALU.mult).then_inc(diag_ready, 1)
            dve.wait_ge(wide_ready, 1)
            dve.tensor_copy(att.least[:, :], wide_ps[:, 0:H]).then_inc(own, 1)
            dve.wait_ge(own, 3)
            src, dst = (a[:, :].rearrange("p (t h) -> p t h", h=H) for a in (att.src, att.dst))
            least = att.least[:, :].unsqueeze(1).broadcast_to([P, BUCKETS, H])
            dve.tensor_tensor(src, src, least, ALU.subtract).then_inc(counted, 1)
            dve.tensor_tensor(dst, dst, least, ALU.add)
            dve.wait_ge(counted, 1)
            dve.tensor_copy(att.top[:, :], att.src[:, :])


def attention_maxima(nc, mem, att, alphas):
    H = att.heads
    per_bank = 4 // H
    banks = GROUP // per_bank

    def by_dve(g):
        return g % 2 if H > 1 else 0

    def until(i, g, dve=False):
        share = [by_dve(x) if dve else GROUP - by_dve(x) for x in range(GROUPS)]
        return i * sum(share) + sum(share[:g])
    with Phase(nc, f"maxima{att.n}") as ph:
        sb, sem = ph.sb, ph.sem
        which = sb("which", [P, RING], I32)
        alpha = sb("alpha", [P, RING, H])
        onehot = sb("onehot", [P, 2 * GROUP, P])
        spread = sb("spread", [P, 2 * GROUP, H * P])
        best = sb("best", [P, 2 * GROUP, H])
        score_ps = [ph.psum(f"score_ps{b}", [P, 512]) for b in range(2 * banks)]
        staged = [sem(f"staged{g}") for g in range(GROUPS)]
        landed = [sem(f"landed{g}") for g in range(GROUPS)]
        onehots, spreads, dve_spreads, copies, spread_done, best_ready, raised = (
            sem(x) for x in ("onehots", "spreads", "dve_spreads", "copies", "spread_done", "best_ready", "raised"))
        block = ph.block()

        @block.sync
        def _(sp):
            def stage(i):
                for g in range(GROUPS):
                    if not is_first(i):
                        sp.wait_ge(landed[g], i * (16 * GROUP))
                        sp.sem_inc(ph.turn, 1)
                    sp.dma_start(which[:, cols(g, GROUP)], mem.slot_row[:, cols(i, RING, g * GROUP, GROUP)]
                                 ).then_inc(staged[g], 16)
            rounds(sp, NT // RING, stage)

        @block.gpsimd
        def _(pool):
            def gather(i):
                for g in range(GROUPS):
                    n = Group(i, g)
                    pool.wait_ge(staged[g], (i + 1) * 16)
                    if not is_first(i):
                        pool.wait_ge(copies, n.q - GROUPS + 1)
                        pool.wait_ge(spreads, until(i - 1, g + 1))
                        pool.sem_inc(ph.turn, 1)
                        if by_dve(g):
                            pool.wait_ge(dve_spreads, until(i - 1, g + 1, dve=True))
                            pool.sem_inc(ph.turn, 1)
                    for k in range(g * GROUP, (g + 1) * GROUP):
                        pool.indirect_dma_start(alpha[:, k, :], None, alphas,
                                                bass.IndirectOffsetOnAxis(which[:, k:k + 1], 0)
                                                ).then_inc(landed[g], 16)
            rounds(pool, NT // RING, gather)

        @block.scalar
        def _(act):
            def step(i, g):
                n = Group(i, g)
                act.wait_ge(landed[n.g], (n.i + 1) * (16 * GROUP))
                act.sem_inc(ph.turn, 1)
                act.copy(att.slot_src[:, cols(i, RING * H, g * GROUP * H, GROUP * H)],
                         alpha[:, cols(g, GROUP), :].rearrange("p k h -> p (k h)")).then_inc(copies, 1)
                for k in range(GROUP - by_dve(g)):
                    if n.after(2):
                        act.wait_ge(spread_done, n.t + k - 2 * GROUP + 1)
                    for head in range(H):
                        ins = act.activation(spread[:, g % 2 * GROUP + k, cols(head, P)], mem.ident[:, :], ACT.Copy,
                                             scale=alpha[:, g * GROUP + k, head:head + 1])
                    ins.then_inc(spreads, 1)
            over_groups(act, step, 0)

        @block.tensor
        def _(pe):
            def step(i, g):
                n = Group(i, g)
                for k in range(GROUP):
                    if k == 0:
                        pe.wait_ge(onehots, n.q + 1)
                    if k < GROUP - by_dve(g):
                        pe.wait_ge(spreads, until(i, g) + k + 1)
                    else:
                        pe.wait_ge(dve_spreads, until(i, g, dve=True) + k - (GROUP - by_dve(g)) + 1)
                    if n.after(2) and k % per_bank == 0:
                        pe.wait_ge(best_ready, (n.q - 2) * banks + k // per_bank + 1)
                    bank = score_ps[g % 2 * banks + k // per_bank]
                    pe.matmul(bank[:, cols(k % per_bank, H * P)], onehot[:, g % 2 * GROUP + k, :],
                              spread[:, g % 2 * GROUP + k, :], start=True, stop=True).then_inc(spread_done, 1)
            over_groups(pe, step, 0)

        @block.vector
        def _(dve):
            tiles = []

            def raise_top(n, k):
                top = att.top[:, cols(tiles[n.g * GROUP + k], H)]
                dve.wait_ge(best_ready, n.q * banks + k // per_bank + 1)
                if n.after(1) or k:
                    dve.wait_ge(raised, n.t + k)
                dve.tensor_tensor(top, top, best[:, n.g % 2 * GROUP + k, :], ALU.max).then_inc(raised, 1)

            def step(i, g):
                now, following = Group(i, g), Group(i, g + 1)
                if now.exists and g == 0:
                    tiles[:] = tiles_of(nc, dve, mem.tile_of, i, 0, RING)
                if now.exists and by_dve(g):
                    dve.wait_ge(landed[g], (now.i + 1) * (16 * GROUP))
                    for k in range(GROUP - by_dve(g), GROUP):
                        if now.after(2):
                            dve.wait_ge(spread_done, now.t + k - 2 * GROUP + 1)
                        dve.tensor_tensor(spread[:, g % 2 * GROUP + k, :].rearrange("p (h e) -> p h e", h=H),
                                          mem.ident[:, :].unsqueeze(1).broadcast_to([P, H, P]),
                                          alpha[:, g * GROUP + k, :].unsqueeze(2).broadcast_to([P, H, P]),
                                          ALU.mult).then_inc(dve_spreads, 1)
                for k in range(GROUP):
                    if now.exists and k % per_bank == 0:
                        b = k // per_bank
                        dve.wait_ge(spread_done, now.t + k + per_bank)
                        if now.after(2):
                            dve.wait_ge(raised, now.t - GROUP)
                        dve.tensor_reduce(best[:, g % 2 * GROUP + k:g % 2 * GROUP + k + per_bank, :]
                                          .rearrange("p k h -> p (k h)"),
                                          score_ps[g % 2 * banks + b][:, :].rearrange("p (h e) -> p h e", e=P),
                                          AX.X, ALU.max).then_inc(best_ready, 1)
                    if k == 0 and following.exists:
                        if following.after(2):
                            dve.wait_ge(spread_done, following.t - GROUP)
                        dve.tensor_tensor(onehot[:, cols(following.g % 2, GROUP), :],
                                          mem.iota[:, :].unsqueeze(1).broadcast_to([P, GROUP, P]),
                                          mem.slot_node[:, bass.ds(following.t, GROUP)].unsqueeze(2)
                                          .broadcast_to([P, GROUP, P]), ALU.is_equal).then_inc(onehots, 1)
                    if now.exists and k > 0:
                        raise_top(now, k - 1)
                if now.exists:
                    raise_top(now, GROUP - 1)
            over_groups(dve, step, 1)


def attention_start(nc, mem, att):
    H = att.heads
    with Phase(nc, f"start{att.n}") as ph:
        own, low, gap, weight = (ph.sb(x, [P, BUCKETS * H]) for x in ("own", "low", "gap", "weight"))
        chain, weights = ph.sem("chain"), ph.sem("weights")
        pair = [att.pair[:, :, a * H:(a + 1) * H] for a in range(2)]
        by_tile = [a[:, :].rearrange("p (t h) -> p t h", h=H) for a in (att.dst, att.top, low, gap)]
        dst, top, low_t, gap_t = by_tile
        block = ph.block()

        @block.scalar
        def _(act):
            act.wait_ge(chain, 5)
            act.activation(weight[:, :], gap[:, :], ACT.Exp).then_inc(weights, 1)

        @block.vector
        def _(dve):
            dve.tensor_tensor(own[:, :], att.src[:, :], att.dst[:, :], ALU.add).then_inc(chain, 1)
            dve.tensor_tensor(att.top[:, :], att.top[:, :], att.dst[:, :], ALU.add).then_inc(chain, 1)
            dve.tensor_copy(pair[0], dst)
            dve.wait_ge(chain, 2)
            dve.scalar_tensor_tensor(low[:, :], own[:, :], SLOPE, own[:, :], ALU.mult, ALU.max).then_inc(chain, 1)
            dve.scalar_tensor_tensor(pair[1], top, SLOPE, top, ALU.mult, ALU.max).then_inc(chain, 1)
            dve.wait_ge(chain, 4)
            dve.tensor_tensor(gap_t, low_t, pair[1], ALU.subtract).then_inc(chain, 1)
            dve.wait_ge(weights, 1)
            if att.width == ACCW:
                sums = mem.acc[:, :].rearrange("p (t c) -> p t c", c=att.part)
                dve.tensor_tensor(sums, sums, weight[:, :].unsqueeze(2).broadcast_to([P, BUCKETS * H, att.part]),
                                  ALU.mult)
            else:
                sums = mem.acc[:, :].rearrange("p (t c) -> p t c", c=ACCW)[:, :, 0:att.width]
                dve.tensor_tensor(sums, sums, weight[:, :].unsqueeze(2).broadcast_to([P, BUCKETS, att.width]),
                                  ALU.mult)


def attend(nc, mem, att, table):
    H, C, W = att.heads, D // att.heads, att.width
    by_row = H > 1
    with Phase(nc, f"attend{att.n}") as ph:
        sb, sem = ph.sb, ph.sem
        which = sb("which", [P, RING], I32)
        rows = sb("rows", [P, RING, D if by_row else W])
        onehot = sb("onehot", [P, RING, P])
        hot_t = sb("hot_t", [P, 2, GROUP * P])
        pair = sb("pair", [P, 2, GROUP, 2 * H])
        score, low, gap, cut = (sb(x, [P, GROUP * H]) for x in ("score", "low", "gap", "cut"))
        if by_row:
            weighed = sb("weighed", [P, 2 * GROUP, W])
        else:
            weighed = sb("weighed", [P, 2 * GROUP, P])
            weight = sb("weight", [P, 2 * GROUP])
        turn_ps = [ph.psum(f"turn_ps{b}", [P, 512]) for b in range(2)]
        look_ps = [ph.psum(f"look_ps{b}", [P, 512]) for b in range(2)]
        sums_ps = [ph.psum(f"sums_ps{k}", [P, 512]) for k in range(GROUP)]
        staged = [sem(f"staged{g}") for g in range(GROUPS)]
        landed = [sem(f"landed{g}") for g in range(GROUPS)]
        (onehots, turned, hot_t_ready, pairs, looked, score_ready, low_ready, gap_ready, cut_ready, weights,
         weighings, products, added, filled) = (
            sem(x) for x in ("onehots", "turned", "hot_t_ready", "pairs", "looked", "score_ready", "low_ready",
                             "gap_ready", "cut_ready", "weights", "weighings", "products", "added", "filled"))
        block = ph.block()

        @block.sync
        def _(sp):
            def stage(i):
                for g in range(GROUPS):
                    if not is_first(i):
                        sp.wait_ge(landed[g], i * (16 * GROUP))
                        sp.sem_inc(ph.turn, 1)
                    sp.dma_start(which[:, cols(g, GROUP)], mem.slot_row[:, cols(i, RING, g * GROUP, GROUP)]
                                 ).then_inc(staged[g], 16)
            rounds(sp, NT // RING, stage)

        @block.gpsimd
        def _(pool):
            used = weighings if by_row else products

            def gather(i):
                for g in range(GROUPS):
                    pool.wait_ge(staged[g], (i + 1) * 16)
                    if not is_first(i):
                        pool.wait_ge(used, (i - 1) * RING + (g + 1) * GROUP)
                        pool.sem_inc(ph.turn, 1)
                    for k in range(g * GROUP, (g + 1) * GROUP):
                        pool.indirect_dma_start(rows[:, k, 0:D], None, table,
                                                bass.IndirectOffsetOnAxis(which[:, k:k + 1], 0)
                                                ).then_inc(landed[g], 16)
            rounds(pool, NT // RING, gather)

        @block.scalar
        def _(act):
            def pairs_of(n):
                tiles = tiles_of(nc, act, mem.tile_of, n.i, n.g * GROUP, GROUP)
                if n.after(2):
                    act.wait_ge(looked, n.q - 1)
                    act.sem_inc(ph.turn, 1)
                for k in range(GROUP):
                    ins = act.copy(pair[:, n.g % 2, k, :], att.pair[:, bass.ds(tiles[k], 1), :]
                                   .rearrange("p t h -> p (t h)"))
                ins.then_inc(pairs, 1)

            def weights_of(n):
                act.wait_ge(cut_ready, n.q + 1)
                if n.after(2):
                    act.wait_ge(products, n.t - GROUP)
                if by_row:
                    into = weighed[:, cols(n.g % 2, GROUP), :].rearrange("p k (h c) -> p (k h) c", c=C + 1)[:, :, C]
                else:
                    into = weight[:, cols(n.g % 2, GROUP)]
                act.activation(into, cut[:, :], ACT.Exp).then_inc(weights, 1)

            def turned_of(n):
                act.wait_ge(turned, n.t + GROUP)
                if n.after(2):
                    act.wait_ge(looked, n.q - 1)
                act.copy(hot_t[:, n.g % 2, :], turn_ps[n.g % 2][:, :]).then_inc(hot_t_ready, 1)

            def step(i, g):
                if Group(i, g + 4).exists:
                    pairs_of(Group(i, g + 4))
                if Group(i, g + 2).exists:
                    weights_of(Group(i, g + 2))
                if Group(i, g + 4).exists:
                    turned_of(Group(i, g + 4))
            over_groups(act, step, 4)

        @block.tensor
        def _(pe):
            if not by_row:
                pe.wait_ge(filled, 1)

            def step(i, g):
                sums, looks, turns = Group(i, g + 1), Group(i, g + 3), Group(i, g + 4)
                if looks.exists:
                    pe.wait_ge(hot_t_ready, looks.q + 1)
                    pe.wait_ge(pairs, looks.q + 1)
                    if looks.after(2):
                        pe.wait_ge(gap_ready, looks.q - 1)
                    for k in range(GROUP):
                        ins = pe.matmul(look_ps[looks.g % 2][:, cols(k, 2 * H)], hot_t[:, looks.g % 2, cols(k, P)],
                                        pair[:, looks.g % 2, k, :], start=True, stop=True)
                    ins.then_inc(looked, 1)
                for k in range(GROUP):
                    if turns.exists:
                        pe.wait_ge(onehots, turns.t + k + 1)
                        if turns.after(2) and k == 0:
                            pe.wait_ge(hot_t_ready, turns.q - 1)
                        pe.transpose(turn_ps[turns.g % 2][:, cols(k, P)], onehot[:, turns.g * GROUP + k, :],
                                     mem.ident[:, :]).then_inc(turned, 1)
                    if sums.exists:
                        if not by_row and k == 0:
                            pe.wait_ge(landed[sums.g], (sums.i + 1) * (16 * GROUP))
                        pe.wait_ge(weighings, sums.t + k + 1)
                        if sums.after(1):
                            pe.wait_ge(added, sums.t + k - GROUP + 1)
                        row, hot = sums.g * GROUP + k, sums.g % 2 * GROUP + k
                        left, right = ((onehot[:, row, :], weighed[:, hot, :]) if by_row else
                                       (weighed[:, hot, :], rows[:, row, :]))
                        pe.matmul(sums_ps[k][:, 0:W], left, right, start=True, stop=True).then_inc(products, 1)
            over_groups(pe, step, 4)

        @block.vector
        def _(dve):
            tiles = []
            if not by_row:
                dve.memset(rows[:, :, D], 1.0).then_inc(filled, 1)

            def add(n, k):
                into = mem.acc[:, cols(tiles[n.g * GROUP + k], ACCW, 0, W)]
                dve.wait_ge(products, n.t + k + 1)
                if n.after(1) or k:
                    dve.wait_ge(added, n.t + k)
                dve.tensor_tensor(into, into, sums_ps[k][:, 0:W], ALU.add).then_inc(added, 1)

            def onehot_of(n, k):
                if n.after(4):
                    dve.wait_ge(products, n.t + k - RING + 1)
                dve.tensor_scalar(onehot[:, n.g * GROUP + k, :], mem.iota[:, :], mem.slot_node[:, bass.ds(n.t + k, 1)],
                                  None, ALU.is_equal).then_inc(onehots, 1)

            def weigh(n, k):
                dve.wait_ge(weights, n.q + 1)
                if by_row:
                    if k == 0:
                        dve.wait_ge(landed[n.g], (n.i + 1) * (16 * GROUP))
                    into = att.by_head(weighed[:, n.g % 2 * GROUP + k, :])
                    dve.tensor_tensor(into[:, :, 0:C],
                                      rows[:, n.g * GROUP + k, :].rearrange("p (h c) -> p h c", c=C),
                                      into[:, :, C:C + 1].broadcast_to([P, H, C]), ALU.mult).then_inc(weighings, 1)
                else:
                    if n.after(2):
                        dve.wait_ge(products, n.t + k - 2 * GROUP + 1)
                    dve.tensor_scalar(weighed[:, n.g % 2 * GROUP + k, :], mem.iota[:, :],
                                      mem.slot_node[:, bass.ds(n.t + k, 1)],
                                      weight[:, n.g % 2 * GROUP + k:n.g % 2 * GROUP + k + 1],
                                      ALU.is_equal, ALU.mult).then_inc(weighings, 1)

            def gaps_of(n, k):
                look = look_ps[n.g % 2][:, 0:GROUP * 2 * H].rearrange("p (k c) -> p k c", k=GROUP)
                by_tile = [a[:, :].rearrange("p (k h) -> p k h", h=H) for a in (score, low, gap)]
                if k == 0:
                    dve.wait_ge(looked, n.q + 1)
                    if n.after(1):
                        dve.wait_ge(low_ready, n.q)
                    slots = att.slot_src[:, cols(n.i, RING * H, n.g * GROUP * H, GROUP * H)]
                    dve.tensor_tensor(by_tile[0], slots.rearrange("p (k h) -> p k h", h=H), look[:, :, 0:H], ALU.add
                                      ).then_inc(score_ready, 1)
                if k == 1:
                    dve.wait_ge(score_ready, n.q + 1)
                    if n.after(1):
                        dve.wait_ge(gap_ready, n.q)
                    dve.scalar_tensor_tensor(low[:, :], score[:, :], SLOPE, score[:, :], ALU.mult, ALU.max
                                             ).then_inc(low_ready, 1)
                if k == 2:
                    dve.wait_ge(low_ready, n.q + 1)
                    if n.after(1):
                        dve.wait_ge(cut_ready, n.q)
                    dve.tensor_tensor(by_tile[2], by_tile[1], look[:, :, H:2 * H], ALU.subtract).then_inc(gap_ready, 1)

            def cut_of(n):
                dve.wait_ge(gap_ready, n.q + 1)
                if n.after(1):
                    dve.wait_ge(weights, n.q)
                dve.tensor_scalar(cut[:, :], gap[:, :], 0.0, None, ALU.min).then_inc(cut_ready, 1)

            def step(i, g):
                now = Group(i, g)
                if now.exists and g == 0:
                    tiles[:] = tiles_of(nc, dve, mem.tile_of, i, 0, RING)
                for k in range(GROUP):
                    if Group(i, g + 2).exists:
                        gaps_of(Group(i, g + 2), k)
                    if now.exists:
                        add(now, k)
                    if Group(i, g + 4).exists:
                        onehot_of(Group(i, g + 4), k)
                    if k == 2 and Group(i, g + 2).exists:
                        cut_of(Group(i, g + 2))
                    if Group(i, g + 1).exists:
                        weigh(Group(i, g + 1), k)
            over_groups(dve, step, 4)


LEAD, TAIL = 4, 2


def attend_at_once(nc, mem, att, table):
    BODY = 2 * GROUPS
    n_rounds = NT // GROUP // BODY
    slots = BODY * GROUP
    W = D + 1
    by_act = GROUP // 2
    with Phase(nc, f"attend{att.n}") as ph:
        sb, sem = ph.sb, ph.sem
        which = sb("which", [P, slots], I32)
        rows = sb("rows", [P, slots, W])
        onehot = sb("onehot", [P, slots, P])
        alpha = sb("alpha", [P, BODY, GROUP])
        spread = sb("spread", [P, 2 * GROUP, P])
        hot_t = sb("hot_t", [P, 4, GROUP * P])
        weighed = sb("weighed", [P, 2 * GROUP, P])
        best = sb("best", [P, GROUP])
        tops = sb("tops", [P, 2, 2, GROUP])
        scores = sb("scores", [P, 4, 3, GROUP])
        cand = sb("cand", [P, 2, GROUP])
        drop = sb("drop", [P, GROUP])
        factor, weight = sb("factor", [P, BODY, GROUP]), sb("weight", [P, 2, GROUP])
        score, low, gap, cut = (sb(x, [P, GROUP]) for x in ("score", "low", "gap", "cut"))
        less_least = sb("less_least", [P, 1])
        tile_flat = sb("tile_flat", [1, 2 * RING + NT + 2 * RING], I32)
        score_ps, turn_ps, look_ps = (ph.psum(x, [P, 512]) for x in ("score_ps", "turn_ps", "look_ps"))
        sums_ps = [ph.psum(f"sums_ps{k}", [P, 512]) for k in range(GROUP)]
        staged = [sem(f"staged{g}") for g in range(BODY)]
        landed = [sem(f"landed{g}") for g in range(BODY)]
        (prepared, onehots, alphas, spreads, spread_done, turned, hot_t_ready, best_ready, olds, news, raised, dsts,
         cands, score_pairs, dropped, factors, looked, score_ready, low_ready, gap_ready, cut_ready, weights,
         act_weighed, dve_weighed, products, added) = (
            sem(x) for x in ("prepared", "onehots", "alphas", "spreads", "spread_done", "turned", "hot_t_ready",
                             "best_ready", "olds", "news", "raised", "dsts", "cands", "score_pairs", "dropped",
                             "factors", "looked", "score_ready", "low_ready", "gap_ready", "cut_ready", "weights",
                             "act_weighed", "dve_weighed", "products", "added"))
        block = ph.block()

        def at(i, g):
            return Group(i, g, BODY)

        def steps(engine, step):
            def one_round(i, groups):
                for g in groups:
                    step(i, g)
            one_round(-1, range(BODY - LEAD, BODY))
            one_round(0, range(BODY))
            with engine.Fori(1, n_rounds - 1) as i:
                one_round(i, range(BODY))
            one_round(n_rounds - 1, range(BODY))
            one_round(n_rounds, range(TAIL))

        def tiles_from(engine, i, g, ahead):
            _, values = nc.values_load_multi_w_load_instructions(
                tile_flat[0:1, bass.ds(i * slots + (g + ahead) * GROUP + 2 * RING, 2 * GROUP)], engines=(engine.engine,),
                min_val=0, max_val=BUCKETS - 1,
                skip_runtime_bounds_check_because="a slot tile's node tile is a sum of REAL = BUCKETS - 1 zeros and ones")
            return values

        @block.sync
        def _(sp):
            def stage(i):
                for g in range(BODY):
                    if not is_first(i):
                        sp.wait_ge(landed[g], i * (16 * GROUP))
                        sp.sem_inc(ph.turn, 1)
                    sp.dma_start(which[:, cols(g, GROUP)], mem.slot_row[:, cols(i, slots, g * GROUP, GROUP)]
                                 ).then_inc(staged[g], 16)
            rounds(sp, n_rounds, stage)

        @block.gpsimd
        def _(pool):
            def gather(i):
                for g in range(BODY):
                    pool.wait_ge(staged[g], (i + 1) * 16)
                    if not is_first(i):
                        pool.wait_ge(products, (i - 1) * slots + (g + 1) * GROUP)
                        pool.sem_inc(ph.turn, 1)
                    for k in range(g * GROUP, (g + 1) * GROUP):
                        pool.indirect_dma_start(rows[:, k, :], None, table,
                                                bass.IndirectOffsetOnAxis(which[:, k:k + 1], 0)
                                                ).then_inc(landed[g], 16)
            rounds(pool, n_rounds, gather)

        @block.scalar
        def _(act):
            tiles = []
            act.wait_ge(prepared, 2)

            def alphas_of(n):
                act.wait_ge(landed[n.g], (n.i + 1) * (16 * GROUP))
                act.sem_inc(ph.turn, 1)
                column = rows[:, cols(n.g, GROUP), D]
                act.activation(alpha[:, n.g, :], column, ACT.Identity, bias=less_least[:, :]).then_inc(alphas, 1)
                act.wait_ge(alphas, n.q * 2 + 1)
                if n.after(2):
                    act.wait_ge(spread_done, n.t - GROUP)
                for k in range(GROUP):
                    act.activation(spread[:, n.g % 2 * GROUP + k, :], mem.ident[:, :], ACT.Copy,
                                   scale=alpha[:, n.g, k:k + 1]).then_inc(spreads, 1)
                act.copy(column, mem.ones[:, 0:GROUP]).then_inc(alphas, 1)

            def dst_of(n):
                if n.after(4):
                    act.wait_ge(looked, n.q - 3)
                act.sem_inc(ph.turn, 1)
                for k in range(GROUP):
                    ins = act.copy(scores[:, n.g % 4, 2, k:k + 1], att.dst[:, bass.ds(tiles[n.g % 2 * GROUP + k], 1)])
                ins.then_inc(dsts, 1)

            def factors_of(n):
                act.wait_ge(dropped, n.q + 1)
                if n.after(BODY):
                    act.wait_ge(added, n.t - slots + GROUP)
                act.activation(factor[:, n.g, :], drop[:, :], ACT.Exp).then_inc(factors, 1)

            def weights_of(n):
                act.wait_ge(cut_ready, n.q + 1)
                if n.after(2):
                    act.wait_ge(products, n.t - GROUP)
                act.activation(weight[:, n.g % 2, :], cut[:, :], ACT.Exp).then_inc(weights, 1)

            def weigh(n):
                act.wait_ge(weights, n.q + 1)
                for k in range(by_act):
                    if n.after(2):
                        act.wait_ge(products, n.t + k - 2 * GROUP + 1)
                    act.activation(weighed[:, n.g % 2 * GROUP + k, :], onehot[:, n.g * GROUP + k, :], ACT.Copy,
                                   scale=weight[:, n.g % 2, k:k + 1]).then_inc(act_weighed, 1)

            def turned_of(n):
                act.wait_ge(turned, n.t + GROUP)
                if n.after(4):
                    act.wait_ge(looked, n.q - 3)
                act.copy(hot_t[:, n.g % 4, :], turn_ps[:, :]).then_inc(hot_t_ready, 1)

            def step(i, g):
                if g % 2 == 0 and at(i, g + 3).exists:
                    tiles[:] = tiles_from(act, i, g, 2)
                for work, ahead in ((weigh, -1), (alphas_of, 3), (dst_of, 2), (factors_of, 1), (weights_of, 0),
                                    (turned_of, 3)):
                    if at(i, g + ahead).exists:
                        work(at(i, g + ahead))
            steps(act, step)

        @block.tensor
        def _(pe):
            def maxima_of(n, k):
                if k == 0:
                    pe.wait_ge(onehots, n.q + 1)
                    if n.after(1):
                        pe.wait_ge(best_ready, n.q)
                        pe.wait_ge(hot_t_ready, n.q)
                pe.wait_ge(spreads, n.t + k + 1)
                pe.matmul(score_ps[:, cols(k, P)], onehot[:, n.g * GROUP + k, :], spread[:, n.g % 2 * GROUP + k, :],
                          start=True, stop=True).then_inc(spread_done, 1)
                pe.transpose(turn_ps[:, cols(k, P)], onehot[:, n.g * GROUP + k, :], mem.ident[:, :]).then_inc(turned, 1)

            def look_up(n):
                pe.wait_ge(hot_t_ready, n.q + 1)
                pe.wait_ge(score_pairs, n.q + 1)
                if n.after(1):
                    pe.wait_ge(gap_ready, n.q)
                for k in range(GROUP):
                    ins = pe.matmul(look_ps[:, cols(k, 2)], hot_t[:, n.g % 4, cols(k, P)], scores[:, n.g % 4, 1:3, k],
                                    start=True, stop=True)
                ins.then_inc(looked, 1)

            def sum_of(n, k):
                if k == 0:
                    pe.wait_ge(alphas, (n.q + 1) * 2)
                if k < by_act:
                    pe.wait_ge(act_weighed, n.q * by_act + k + 1)
                else:
                    pe.wait_ge(dve_weighed, n.q * (GROUP - by_act) + k - by_act + 1)
                if n.after(1):
                    pe.wait_ge(added, n.t + k - GROUP + 1)
                pe.matmul(sums_ps[k][:, 0:W], weighed[:, n.g % 2 * GROUP + k, :], rows[:, n.g * GROUP + k, :],
                          start=True, stop=True).then_inc(products, 1)

            def step(i, g):
                summed, maxima, looked_up = at(i, g - 1), at(i, g + 3), at(i, g + 1)
                if maxima.exists:
                    for k in range(GROUP):
                        maxima_of(maxima, k)
                for k in range(GROUP):
                    if summed.exists:
                        sum_of(summed, k)
                    if k == by_act and looked_up.exists:
                        look_up(looked_up)
            steps(pe, step)

        @block.vector
        def _(dve):
            top_tiles, sum_tiles = [], []
            dve.memset(tile_flat[:, :], 0).then_inc(prepared, 1)
            dve.wait_ge(prepared, 1)
            dve.tensor_scalar(less_least[:, :], att.least[:, :], -1.0, None, ALU.mult)
            dve.tensor_copy(tile_flat[:, 2 * RING:2 * RING + NT].rearrange("p (i k) -> p i k", k=RING),
                            mem.tile_of[:, :, 0:RING]).then_inc(prepared, 1)
            dve.wait_ge(prepared, 2)

            def onehot_of(n):
                if n.after(BODY):
                    dve.wait_ge(products, n.t - slots + GROUP)
                dve.tensor_tensor(onehot[:, cols(n.g, GROUP), :],
                                  mem.iota[:, :].unsqueeze(1).broadcast_to([P, GROUP, P]),
                                  mem.slot_node[:, bass.ds(n.t, GROUP)].unsqueeze(2).broadcast_to([P, GROUP, P]),
                                  ALU.is_equal).then_inc(onehots, 1)

            def best_of(n):
                dve.wait_ge(spread_done, n.t + GROUP)
                if n.after(1):
                    dve.wait_ge(news, n.t)
                dve.tensor_reduce(best[:, :], score_ps[:, :].rearrange("p (k e) -> p k e", e=P), AX.X, ALU.max
                                  ).then_inc(best_ready, 1)

            def top_of(n, k, part):
                top = att.top[:, bass.ds(top_tiles[n.g % 2 * GROUP + k], 1)]
                old, new = (tops[:, n.g % 2, x, k:k + 1] for x in range(2))
                if part == 0:
                    if n.after(1) or k:
                        dve.wait_ge(raised, n.t + k)
                    if n.after(2) and k == 0:
                        dve.wait_ge(cands, n.q - 1)
                    dve.tensor_scalar(old, top, 0.0, None, ALU.add).then_inc(olds, 1)
                if part == 1:
                    dve.wait_ge(olds, n.t + k + 1)
                    if k == 0:
                        dve.wait_ge(best_ready, n.q + 1)
                    dve.tensor_tensor(new, old, best[:, k:k + 1], ALU.max).then_inc(news, 1)
                if part == 2:
                    dve.wait_ge(news, n.t + k + 1)
                    dve.tensor_scalar(top, new, 0.0, None, ALU.add).then_inc(raised, 1)

            def scores_of(n, k):
                pairs = scores[:, n.g % 4, 0:2, :]
                if k == 0:
                    dve.wait_ge(dsts, n.q + 1)
                    dve.wait_ge(news, n.t + GROUP)
                    if n.after(1):
                        dve.wait_ge(score_pairs, n.q)
                    dve.tensor_tensor(cand[:, :, :], tops[:, n.g % 2, :, :],
                                      scores[:, n.g % 4, 2:3, :].broadcast_to([P, 2, GROUP]), ALU.add).then_inc(cands, 1)
                if k == 1:
                    dve.wait_ge(cands, n.q + 1)
                    dve.scalar_tensor_tensor(pairs, cand[:, :, :], SLOPE, cand[:, :, :], ALU.mult, ALU.max
                                             ).then_inc(score_pairs, 1)
                if k == 2:
                    dve.wait_ge(score_pairs, n.q + 1)
                    if n.after(1):
                        dve.wait_ge(factors, n.q)
                    dve.tensor_tensor(drop[:, :], scores[:, n.g % 4, 0, :], scores[:, n.g % 4, 1, :], ALU.subtract
                                      ).then_inc(dropped, 1)

            def gaps_of(n, k):
                look = look_ps[:, 0:2 * GROUP].rearrange("p (k c) -> p k c", c=2)
                if k == 0:
                    dve.wait_ge(looked, n.q + 1)
                    if n.after(1):
                        dve.wait_ge(low_ready, n.q)
                    dve.tensor_tensor(score[:, :], alpha[:, n.g, :], look[:, :, 1], ALU.add).then_inc(score_ready, 1)
                if k == 1:
                    dve.wait_ge(score_ready, n.q + 1)
                    if n.after(1):
                        dve.wait_ge(gap_ready, n.q)
                    dve.scalar_tensor_tensor(low[:, :], score[:, :], SLOPE, score[:, :], ALU.mult, ALU.max
                                             ).then_inc(low_ready, 1)
                if k == 2:
                    dve.wait_ge(low_ready, n.q + 1)
                    if n.after(1):
                        dve.wait_ge(cut_ready, n.q)
                    dve.tensor_tensor(gap[:, :], low[:, :], look[:, :, 0], ALU.subtract).then_inc(gap_ready, 1)

            def cut_of(n):
                dve.wait_ge(gap_ready, n.q + 1)
                if n.after(1):
                    dve.wait_ge(weights, n.q)
                dve.tensor_scalar(cut[:, :], gap[:, :], 0.0, None, ALU.min).then_inc(cut_ready, 1)

            def weigh(n, k):
                dve.wait_ge(weights, n.q + 1)
                if n.after(2):
                    dve.wait_ge(products, n.t + k - 2 * GROUP + 1)
                dve.tensor_scalar(weighed[:, n.g % 2 * GROUP + k, :], mem.iota[:, :],
                                  mem.slot_node[:, bass.ds(n.t + k, 1)], weight[:, n.g % 2, k:k + 1],
                                  ALU.is_equal, ALU.mult).then_inc(dve_weighed, 1)

            def add(n, k):
                into = mem.acc[:, cols(sum_tiles[n.g % 2 * GROUP + k], ACCW, 0, W)]
                dve.wait_ge(factors, n.q + 1)
                dve.wait_ge(products, n.t + k + 1)
                if n.after(1) or k:
                    dve.wait_ge(added, n.t + k)
                dve.scalar_tensor_tensor(into, into, factor[:, n.g, k:k + 1], sums_ps[k][:, 0:W], ALU.mult, ALU.add
                                         ).then_inc(added, 1)

            def step(i, g):
                if g % 2 == 0:
                    if at(i, g + 3).exists:
                        top_tiles[:] = tiles_from(dve, i, g, 2)
                    if at(i, g - 2).exists:
                        sum_tiles[:] = tiles_from(dve, i, g, -2)
                hot, best_n, scored, gapped, summed, into_acc = (at(i, g + x) for x in (4, 2, 1, 0, -1, -2))
                if best_n.exists:
                    best_of(best_n)
                for k in range(GROUP):
                    if gapped.exists:
                        gaps_of(gapped, k)
                    if best_n.exists:
                        top_of(best_n, k, 0)
                    if k >= by_act and summed.exists:
                        weigh(summed, k)
                    if k == 0 and hot.exists:
                        onehot_of(hot)
                    if scored.exists:
                        scores_of(scored, k)
                    if best_n.exists:
                        top_of(best_n, k, 1)
                    if into_acc.exists:
                        add(into_acc, k)
                    if k == 2 and gapped.exists:
                        cut_of(gapped)
                    if best_n.exists:
                        top_of(best_n, k, 2)
            steps(dve, step)


def finish(nc, mem, e, att, out):
    with Phase(nc, "finish") as ph:
        bias, inv = ph.sb("bias", [P, D]), ph.sb("inv", [P, BUCKETS])
        v = [ph.sb(f"v{u}", [P, D]) for u in range(AWAY)]
        loaded, inv_ready, scaled, biased, ready = (ph.sem(x) for x in ("loaded", "inv_ready", "scaled", "biased", "ready"))
        stored = [ph.sem(f"stored{u}") for u in range(AWAY)]
        block = ph.block()

        @block.sync
        def _(sp):
            sp.dma_start(bias[:, :], e["att_b"][att.n].partition_broadcast(P)).then_inc(loaded, 16)
            with sp.Fori(0, BUCKETS // AWAY) as i:
                for u in range(AWAY):
                    t = i * AWAY + u
                    sp.wait_ge(ready, t + 1)
                    sp.sem_inc(ph.turn, 1)
                    sp.dma_start(out[bass.ds(t * P, P), :], v[u][:, :]).then_inc(stored[u], 16)
            for u in range(AWAY):
                sp.wait_ge(stored[u], 16 * BUCKETS // AWAY)

        @block.vector
        def _(dve):
            dve.wait_ge(loaded, 16)
            dve.reciprocal(inv[:, :], mem.acc[:, :].rearrange("p (t c) -> p t c", c=ACCW)[:, :, D]).then_inc(inv_ready, 1)
            dve.wait_ge(inv_ready, 1)

            def tiles(i):
                for u in range(AWAY):
                    t = i * AWAY + u
                    if not is_first(i):
                        dve.wait_ge(stored[u], i * 16)
                    dve.tensor_scalar(v[u][:, :], mem.acc[:, cols(t, ACCW, 0, D)], inv[:, bass.ds(t, 1)], None,
                                      ALU.mult).then_inc(scaled, 1)
                for u in range(AWAY):
                    t = i * AWAY + u
                    dve.wait_ge(scaled, t + 1)
                    dve.tensor_tensor(v[u][:, :], v[u][:, :], bias[:, :], ALU.add).then_inc(biased, 1)
                for u in range(AWAY):
                    t = i * AWAY + u
                    dve.wait_ge(biased, t + 1)
                    dve.tensor_tensor(v[u][:, :], v[u][:, :], mem.x[:, cols(t, D)], ALU.add).then_inc(ready, 1)
            rounds(dve, BUCKETS // AWAY, tiles)


def build(nc, e, out):
    def dram(name, shape, dt=F32):
        return nc.dram_tensor(name, shape, dt).ap()

    slots, edge_rows = dram("slots", (SLOTS, 3), I32), dram("edge_rows", (SLOTS, 1 + ECOLS))
    rel_table, table = dram("rel_table", (NPAD * REL, D)), dram("table", (NPAD, D))
    n_rounds = COLS // RING
    with ExitStack() as ctx:
        mem = Mem(nc, ctx)
        constants(nc, mem)
        load_nodes(nc, mem, e)
        with ExitStack() as inner:
            halves = inner.enter_context(nc.sbuf_tensor("halves", [P, BUCKETS * 6], F32))
            mem.edge_acc = inner.enter_context(nc.sbuf_tensor("edge_acc", [P, BUCKETS * ECOLS], F32))
            first_stats(nc, mem, halves)
            finish_stats(nc, mem, "stats0", halves)
            with nc.sbuf_tensor("info", [P, COLS, 3], I32) as info, ExitStack() as sorting:
                by_target = TileSort(nc, sorting, "dst", e["dst"], mem.tile_of[:, :, 0:RING],
                                     info[:, :, 2].bitcast(F32))
                count_edges(nc, mem, by_target)
                rank_edges(nc, by_target)
                end_sort(nc, by_target)
                pack_info(nc, e, info, slots)
                relational_tables(nc, mem, e, 0, rel_table, dict(
                    table=slots, addr=by_target.addr, first=0, n_rounds=n_rounds, info=info))
            unpack_slots(nc, mem, slots)
            with ExitStack() as sorting:
                by_source = TileSort(nc, sorting, "src", e["src"], mem.tile_of[:, :, RING:2 * RING])
                count_edges(nc, mem, by_source, edge_rows)
                aggregate(nc, mem, "rel_sum0", rel_table, mem.slot_row, degree=True, ranked=by_source)
                end_sort(nc, by_source)
                to_slots = dict(table=edge_rows, addr=by_source.addr, attr=e["attr"], node=by_source.node)
                relational_tables(nc, mem, e, 1, rel_table, dict(to_slots, first=0, n_rounds=PAIRS))
                aggregate(nc, mem, "rel_sum1", rel_table, mem.slot_row)
                relational_tables(nc, mem, e, 2, rel_table, dict(to_slots, first=PAIRS, n_rounds=n_rounds - PAIRS))
            aggregate(nc, mem, "rel_sum2", rel_table, mem.slot_row, edge_rows=edge_rows)
            slot_sources(nc, mem)
            relational_end(nc, mem, halves)
            finish_stats(nc, mem, "stats1", halves)
            node_table(nc, mem, table)
            aggregate(nc, mem, "mean_sum", table, mem.slot_row, weighted=True)
            conv_layers(nc, mem, e, table)
            mlp_layer(nc, mem, e, 0, halves)
            mlp_layer(nc, mem, e, 1, halves)
            finish_stats(nc, mem, "stats2", halves)
            edge_layer(nc, mem, e, halves)
            finish_stats(nc, mem, "stats3", halves)
        with ExitStack() as first:
            att = Attention(nc, first, 0, HEADS)
            alphas = dram("alphas", (NPAD, HEADS))
            attention_tables(nc, mem, e, att, table, alphas)
            attention_maxima(nc, mem, att, alphas)
            attention_start(nc, mem, att)
            attend(nc, mem, att, table)
        last = Attention(nc, ctx, 1, 1)
        rows = dram("rows", (NPAD, D + 1))
        attention_tables(nc, mem, e, last, rows, None, before=att)
        attend_at_once(nc, mem, last, rows)
        finish(nc, mem, e, last, out)


def lay_out(inputs):
    def f32(name):
        return np.ascontiguousarray(inputs[name])

    def edges(name, fill):
        a = np.asarray(inputs[name])
        out = np.full((EPAD,) + a.shape[1:], fill, a.dtype)
        out[:N_EDGES] = a
        return out.reshape((P, COLS) + a.shape[1:])

    def split_rows(w):
        w = np.asarray(w)
        w = w.reshape(w.shape[:-2] + (w.shape[-2] // P, P, w.shape[-1]))
        return np.ascontiguousarray(np.moveaxis(w, -2, 0))

    x = np.zeros((NPAD, D), np.float32)
    x[:N_NODES] = inputs["x"]
    rel = np.concatenate([np.moveaxis(np.asarray(inputs["L0_gnn_weights"]), 1, 2).reshape(3, D, REL * D),
                          np.asarray(inputs["L0_gnn_roots"])], axis=2)
    conv = np.stack([np.moveaxis(np.asarray(inputs[n]), (0, 1, 2), (1, 2, 0)).reshape(D, 4 * D)
                     for n in ("L1_gnn_W_rel", "L1_gnn_W_root")])
    w = {
        "x": x,
        "src": edges("src", REAL * P), "dst": edges("dst", REAL * P), "rel": edges("edge_type_8", 0),
        "weight": edges("edge_weight", 0), "attr": edges("edge_attr_64", 0),
        "rel_w": split_rows(rel),
        "rel_b": f32("L0_gnn_biases"),
        "conv_w": split_rows(conv),
        "conv_b": f32("L1_gnn_b_rel").reshape(1, -1), "conv_g": f32("L1_gnn_ln_g").reshape(1, -1),
        "conv_n": f32("L1_gnn_ln_b").reshape(1, -1),
        "mlp_w": split_rows(np.stack([np.asarray(inputs["L1_gnn_W1"]).T, np.asarray(inputs["L1_gnn_W2"]).T])),
        "mlp_v": np.stack([np.asarray(inputs["L1_gnn_" + n]) for n in ("b1", "mg1", "mb1", "b2", "mg2", "mb2")]),
        "edge_w": split_rows(np.asarray(inputs["L2_gnn_W1"])[:D]),
        "edge_we": np.ascontiguousarray(np.asarray(inputs["L2_gnn_W1"])[D:D + EDGE_D]),
        "edge_wu": np.ascontiguousarray(np.asarray(inputs["L2_gnn_W1"])[D + EDGE_D:]),
        "edge_u": np.ascontiguousarray(np.asarray(inputs["L2_gnn_u"])[0:1].T),
        "edge_b1": f32("L2_gnn_b1").reshape(1, -1),
        "edge_w2": split_rows(inputs["L2_gnn_W2"]), "edge_b2": f32("L2_gnn_b2").reshape(1, -1),
        "att_w": split_rows(np.stack([np.asarray(inputs["L3_gnn_W1"]), np.asarray(inputs["L3_gnn_W2"])])),
        "att_src": np.stack([np.asarray(inputs[f"L3_gnn_a_src{n}"]).reshape(-1) for n in (1, 2)]),
        "att_dst": np.stack([np.asarray(inputs[f"L3_gnn_a_dst{n}"]).reshape(-1) for n in (1, 2)]),
        "att_b": np.stack([np.asarray(inputs[f"L3_gnn_b{n}"]) for n in (1, 2)]),
    }
    return w


def kernel(**inputs):
    import concourse.bacc as bacc
    from concourse.bass_utils import run_bass_kernel_spmd

    nc = bacc.Bacc("TRN2", target_bir_lowering=False, num_devices=1)
    arrays = lay_out(inputs)
    args = {n: nc.dram_tensor(f"in_{n}", a.shape, mybir.dt.from_np(a.dtype), kind="ExternalInput").ap()
            for n, a in arrays.items()}
    out = nc.dram_tensor("out", (NPAD, D), F32, kind="ExternalOutput").ap()
    build(nc, args, out)
    result = run_bass_kernel_spmd(nc, [{f"in_{n}": a for n, a in arrays.items()}], core_ids=[0])
    return result.results[0]["out"][:N_NODES]
```
